# Optimizing a Trainium2 kernel written in Bass

```python
import numpy as np
import jax
import jax.numpy as jnp

def _softmax(x, axis=-1):
    return jax.nn.softmax(x, axis=axis)

def _gelu(x):
    return jax.nn.gelu(x, approximate=True)

def _silu(x):
    return jax.nn.silu(x)

def _sigmoid(x):
    return jax.nn.sigmoid(x)

def _layernorm(x, axis=-1, eps=1e-05):
    m = jnp.mean(x, axis=axis, keepdims=True)
    v = jnp.var(x, axis=axis, keepdims=True)
    return (x - m) / jnp.sqrt(v + eps)

def _scatter_add(tgt, idx, src, axis=0):
    return tgt.at[idx].add(src)

def _segment_sum(src, seg, n):
    return jax.ops.segment_sum(src, seg, n)
kernel_name = 'mk_pixart_seq_d2_seqx_r8_5bef21'

def setup_inputs(seed: int=0):
    np.random.seed(seed)
    _w = jnp.asarray

    def _rec_inputs():
        import jax
        import jax.numpy as jnp
        _rk = jax.random.key(seed)
        x = -0.0005207 + 1.001 * jax.random.normal(jax.random.fold_in(_rk, 1), (4, 512, 128), jnp.float32)
        _lenS = 512 - jax.random.randint(jax.random.fold_in(_rk, 7), (4,), 0, max(1, 512 // 4) + 1, jnp.int32)
        _lenS2 = 32 - jax.random.randint(jax.random.fold_in(_rk, 8), (4,), 0, max(1, 32 // 4) + 1, jnp.int32)
        cond_1024 = 0.000887014 + 1.03683 * jax.random.normal(jax.random.fold_in(_rk, 11), (4, 128), jnp.float32)
        _ctx_768P = jax.random.normal(jax.random.fold_in(_rk, 12), (4, 16, 96), jnp.float32)
        _ctx_768c = jax.random.dirichlet(jax.random.fold_in(_rk, 512), 0.3 * jnp.ones((16,), jnp.float32), (4, 32))
        _ctx_768t = jnp.einsum('bsk,bkd->bsd', _ctx_768c, _ctx_768P)
        _ctx_768t = _ctx_768t * jax.lax.rsqrt(jnp.mean(jnp.square(_ctx_768t)) + 1e-12) * 0.953939
        ctx_768 = 0.000599585 + 1.00006 * (_ctx_768t + 0.3 * jax.random.normal(jax.random.fold_in(_rk, 612), (4, 32, 96), jnp.float32))
        return (x, cond_1024, ctx_768)
    x, cond_1024, ctx_768 = _rec_inputs()

    def _L0_xcond_setup():
        import jax, jax.numpy as jnp
        import numpy as np
        B, N, M = (2, 128, 64)
        D, H, DH = (128, 16, 64)
        MID = H * DH
        DC = 96
        MULT = 4
        EPS = 1e-05

        def _ln(x, w, b):
            mu = jnp.mean(x, -1, keepdims=True)
            var = jnp.mean((x - mu) ** 2, -1, keepdims=True)
            return (x - mu) * jax.lax.rsqrt(var + EPS) * w + b

        def _sincos(n, d):
            inv = 1.0 / 10000.0 ** (jnp.arange(0, d, 2, dtype=jnp.float32) / d)
            ang = jnp.arange(n, dtype=jnp.float32)[:, None] * inv[None, :]
            return (jnp.sin(ang), jnp.cos(ang))

        def _rope(x, sin, cos):
            s = sin[None, None]
            c = cos[None, None]
            xe = x[..., ::2]
            xo = x[..., 1::2]
            re = xe * c - xo * s
            ro = xe * s + xo * c
            return jnp.stack((re, ro), axis=-1).reshape(x.shape)

        def _heads(t):
            b, n, _ = t.shape
            return t.reshape(b, n, H, DH).transpose(0, 2, 1, 3)

        def _attn(xq, ctx, wq, wkv, wo, bo):
            q = _heads(xq @ wq)
            k, v = jnp.split(ctx @ wkv, 2, axis=-1)
            k = _heads(k)
            v = _heads(v)
            sq, cq = _sincos(q.shape[2], DH)
            sk, ck = _sincos(k.shape[2], DH)
            q = _rope(q, sq, cq)
            k = _rope(k, sk, ck)
            sim = jnp.einsum('bhnd,bhmd->bhnm', q, k) * DH ** (-0.5)
            a = jax.nn.softmax(sim, axis=-1)
            o = jnp.einsum('bhnm,bhmd->bhnd', a, v)
            o = o.transpose(0, 2, 1, 3).reshape(xq.shape[0], xq.shape[1], MID)
            return o @ wo + bo

        def _adaln(x, c, lw, lb, gw, gb, bw, bb):
            g = (c @ gw + gb)[:, None, :]
            bt = (c @ bw + bb)[:, None, :]
            return _ln(x, lw, lb) * (1.0 + g) + bt
        ks = jax.random.split(jax.random.key(seed), 24)
        s = 0.02
        inp = {'x': jax.random.normal(ks[0], (B, N, D), jnp.float32), 'cond': jax.random.normal(ks[1], (B, D), jnp.float32), 'context': jax.random.normal(ks[2], (B, M, DC), jnp.float32), 'ln1_w': jnp.ones((D,), jnp.float32), 'ln1_b': jnp.zeros((D,), jnp.float32), 'g1_w': jax.random.normal(ks[3], (D, D), jnp.float32) * s, 'g1_b': jnp.zeros((D,), jnp.float32), 'b1_w': jax.random.normal(ks[4], (D, D), jnp.float32) * s, 'b1_b': jnp.zeros((D,), jnp.float32), 'ln2_w': jnp.ones((D,), jnp.float32), 'ln2_b': jnp.zeros((D,), jnp.float32), 'g2_w': jax.random.normal(ks[5], (D, D), jnp.float32) * s, 'g2_b': jnp.zeros((D,), jnp.float32), 'b2_w': jax.random.normal(ks[6], (D, D), jnp.float32) * s, 'b2_b': jnp.zeros((D,), jnp.float32), 'sa_wq': jax.random.normal(ks[7], (D, MID), jnp.float32) * s, 'sa_wkv': jax.random.normal(ks[8], (D, 2 * MID), jnp.float32) * s, 'sa_wo': jax.random.normal(ks[9], (MID, D), jnp.float32) * s, 'sa_bo': jnp.zeros((D,), jnp.float32), 'ca_lnc_w': jnp.ones((DC,), jnp.float32), 'ca_lnc_b': jnp.zeros((DC,), jnp.float32), 'ca_wq': jax.random.normal(ks[10], (D, MID), jnp.float32) * s, 'ca_wkv': jax.random.normal(ks[11], (DC, 2 * MID), jnp.float32) * s, 'ca_wo': jax.random.normal(ks[12], (MID, D), jnp.float32) * s, 'ca_bo': jnp.zeros((D,), jnp.float32), 'ff_w1': jax.random.normal(ks[13], (D, MULT * D), jnp.float32) * s, 'ff_b1': jnp.zeros((MULT * D,), jnp.float32), 'ff_w2': jax.random.normal(ks[14], (MULT * D, D), jnp.float32) * s, 'ff_b2': jnp.zeros((D,), jnp.float32)}
        return inp
    _L0_xcond_all = _L0_xcond_setup()
    _L0_xcond_in = {k: v for k, v in _L0_xcond_all.items() if k in ('ln1_w', 'ln1_b', 'g1_w', 'g1_b', 'b1_w', 'b1_b', 'ln2_w', 'ln2_b', 'g2_w', 'g2_b', 'b2_w', 'b2_b', 'sa_wq', 'sa_wkv', 'sa_wo', 'sa_bo', 'ca_lnc_w', 'ca_lnc_b', 'ca_wq', 'ca_wkv', 'ca_wo', 'ca_bo', 'ff_w1', 'ff_b1', 'ff_w2', 'ff_b2')}
    del _L0_xcond_all

    def _L1_xcond_setup():
        import jax, jax.numpy as jnp
        import numpy as np
        EPS = 1e-05

        def _ada_ln(x, t, W, b):
            emb = t @ W + b
            scale, shift = jnp.split(emb, 2, axis=-1)
            mu = x.mean(-1, keepdims=True)
            var = ((x - mu) ** 2).mean(-1, keepdims=True)
            xn = (x - mu) * jax.lax.rsqrt(var + EPS)
            return xn * (1.0 + scale) + shift

        def _attn(x, ctx, Wq, Wk, Wv, Wo, bo, heads):
            b, n, _ = x.shape
            j = ctx.shape[1]
            q = (x @ Wq).reshape(b, n, heads, -1)
            k = (ctx @ Wk).reshape(b, j, heads, -1)
            v = (ctx @ Wv).reshape(b, j, heads, -1)
            scale = q.shape[-1] ** (-0.5)
            sim = jnp.einsum('bihd,bjhd->bhij', q, k) * scale
            attn = jax.nn.softmax(sim, axis=-1)
            out = jnp.einsum('bhij,bjhd->bihd', attn, v).reshape(b, n, -1)
            return out @ Wo + bo

        def _ff(x, W1, b1, W2, b2):
            p = x @ W1 + b1
            a, gate = jnp.split(p, 2, axis=-1)
            return a * jax.nn.gelu(gate, approximate=False) @ W2 + b2
        key = jax.random.key(seed)
        ks = jax.random.split(key, 32)
        B, N, D = (4, 256, 128)
        J, CD = (32, 96)
        H, DH = (16, 64)
        INNER = H * DH
        FF = 4 * D
        w = lambda k, shp: jax.random.normal(k, shp, jnp.float32) * 0.02
        inp = {'x': jax.random.normal(ks[0], (B, N, D), jnp.float32), 't': jax.random.normal(ks[1], (B, 1, D), jnp.float32), 'context': jax.random.normal(ks[2], (B, J, CD), jnp.float32), 'n1_w': w(ks[3], (D, 2 * D)), 'n1_b': jnp.zeros((2 * D,), jnp.float32), 'n2_w': w(ks[4], (D, 2 * D)), 'n2_b': jnp.zeros((2 * D,), jnp.float32), 'n3_w': w(ks[5], (D, 2 * D)), 'n3_b': jnp.zeros((2 * D,), jnp.float32), 'q1': w(ks[6], (D, INNER)), 'k1': w(ks[7], (D, INNER)), 'v1': w(ks[8], (D, INNER)), 'o1_w': w(ks[9], (INNER, D)), 'o1_b': jnp.zeros((D,), jnp.float32), 'q2': w(ks[10], (D, INNER)), 'k2': w(ks[11], (CD, INNER)), 'v2': w(ks[12], (CD, INNER)), 'o2_w': w(ks[13], (INNER, D)), 'o2_b': jnp.zeros((D,), jnp.float32), 'ff_w1': w(ks[14], (D, 2 * FF)), 'ff_b1': jnp.zeros((2 * FF,), jnp.float32), 'ff_w2': w(ks[15], (FF, D)), 'ff_b2': jnp.zeros((D,), jnp.float32)}
        return inp
    _L1_xcond_all = _L1_xcond_setup()
    _L1_xcond_in = {k: v for k, v in _L1_xcond_all.items() if k in ('n1_w', 'n1_b', 'n2_w', 'n2_b', 'n3_w', 'n3_b', 'q1', 'k1', 'v1', 'o1_w', 'o1_b', 'q2', 'k2', 'v2', 'o2_w', 'o2_b', 'ff_w1', 'ff_b1', 'ff_w2', 'ff_b2')}
    del _L1_xcond_all
    return {'x': x, 'cond_1024': cond_1024, 'ctx_768': ctx_768, 'L0_xcond_ln1_w': _L0_xcond_in['ln1_w'], 'L0_xcond_ln1_b': _L0_xcond_in['ln1_b'], 'L0_xcond_g1_w': _L0_xcond_in['g1_w'], 'L0_xcond_g1_b': _L0_xcond_in['g1_b'], 'L0_xcond_b1_w': _L0_xcond_in['b1_w'], 'L0_xcond_b1_b': _L0_xcond_in['b1_b'], 'L0_xcond_ln2_w': _L0_xcond_in['ln2_w'], 'L0_xcond_ln2_b': _L0_xcond_in['ln2_b'], 'L0_xcond_g2_w': _L0_xcond_in['g2_w'], 'L0_xcond_g2_b': _L0_xcond_in['g2_b'], 'L0_xcond_b2_w': _L0_xcond_in['b2_w'], 'L0_xcond_b2_b': _L0_xcond_in['b2_b'], 'L0_xcond_sa_wq': _L0_xcond_in['sa_wq'], 'L0_xcond_sa_wkv': _L0_xcond_in['sa_wkv'], 'L0_xcond_sa_wo': _L0_xcond_in['sa_wo'], 'L0_xcond_sa_bo': _L0_xcond_in['sa_bo'], 'L0_xcond_ca_lnc_w': _L0_xcond_in['ca_lnc_w'], 'L0_xcond_ca_lnc_b': _L0_xcond_in['ca_lnc_b'], 'L0_xcond_ca_wq': _L0_xcond_in['ca_wq'], 'L0_xcond_ca_wkv': _L0_xcond_in['ca_wkv'], 'L0_xcond_ca_wo': _L0_xcond_in['ca_wo'], 'L0_xcond_ca_bo': _L0_xcond_in['ca_bo'], 'L0_xcond_ff_w1': _L0_xcond_in['ff_w1'], 'L0_xcond_ff_b1': _L0_xcond_in['ff_b1'], 'L0_xcond_ff_w2': _L0_xcond_in['ff_w2'], 'L0_xcond_ff_b2': _L0_xcond_in['ff_b2'], 'L1_xcond_n1_w': _L1_xcond_in['n1_w'], 'L1_xcond_n1_b': _L1_xcond_in['n1_b'], 'L1_xcond_n2_w': _L1_xcond_in['n2_w'], 'L1_xcond_n2_b': _L1_xcond_in['n2_b'], 'L1_xcond_n3_w': _L1_xcond_in['n3_w'], 'L1_xcond_n3_b': _L1_xcond_in['n3_b'], 'L1_xcond_q1': _L1_xcond_in['q1'], 'L1_xcond_k1': _L1_xcond_in['k1'], 'L1_xcond_v1': _L1_xcond_in['v1'], 'L1_xcond_o1_w': _L1_xcond_in['o1_w'], 'L1_xcond_o1_b': _L1_xcond_in['o1_b'], 'L1_xcond_q2': _L1_xcond_in['q2'], 'L1_xcond_k2': _L1_xcond_in['k2'], 'L1_xcond_v2': _L1_xcond_in['v2'], 'L1_xcond_o2_w': _L1_xcond_in['o2_w'], 'L1_xcond_o2_b': _L1_xcond_in['o2_b'], 'L1_xcond_ff_w1': _L1_xcond_in['ff_w1'], 'L1_xcond_ff_b1': _L1_xcond_in['ff_b1'], 'L1_xcond_ff_w2': _L1_xcond_in['ff_w2'], 'L1_xcond_ff_b2': _L1_xcond_in['ff_b2']}

def reference(x, cond_1024, ctx_768, L0_xcond_ln1_w, L0_xcond_ln1_b, L0_xcond_g1_w, L0_xcond_g1_b, L0_xcond_b1_w, L0_xcond_b1_b, L0_xcond_ln2_w, L0_xcond_ln2_b, L0_xcond_g2_w, L0_xcond_g2_b, L0_xcond_b2_w, L0_xcond_b2_b, L0_xcond_sa_wq, L0_xcond_sa_wkv, L0_xcond_sa_wo, L0_xcond_sa_bo, L0_xcond_ca_lnc_w, L0_xcond_ca_lnc_b, L0_xcond_ca_wq, L0_xcond_ca_wkv, L0_xcond_ca_wo, L0_xcond_ca_bo, L0_xcond_ff_w1, L0_xcond_ff_b1, L0_xcond_ff_w2, L0_xcond_ff_b2, L1_xcond_n1_w, L1_xcond_n1_b, L1_xcond_n2_w, L1_xcond_n2_b, L1_xcond_n3_w, L1_xcond_n3_b, L1_xcond_q1, L1_xcond_k1, L1_xcond_v1, L1_xcond_o1_w, L1_xcond_o1_b, L1_xcond_q2, L1_xcond_k2, L1_xcond_v2, L1_xcond_o2_w, L1_xcond_o2_b, L1_xcond_ff_w1, L1_xcond_ff_b1, L1_xcond_ff_w2, L1_xcond_ff_b2):
    import jax
    import jax.numpy as jnp

    def _L0_xcond_ref(x, cond, context, ln1_w, ln1_b, g1_w, g1_b, b1_w, b1_b, ln2_w, ln2_b, g2_w, g2_b, b2_w, b2_b, sa_wq, sa_wkv, sa_wo, sa_bo, ca_lnc_w, ca_lnc_b, ca_wq, ca_wkv, ca_wo, ca_bo, ff_w1, ff_b1, ff_w2, ff_b2):
        import jax, jax.numpy as jnp
        import numpy as np
        B, N, M = (2, 128, 64)
        D, H, DH = (128, 16, 64)
        MID = H * DH
        DC = 96
        MULT = 4
        EPS = 1e-05

        def _ln(x, w, b):
            mu = jnp.mean(x, -1, keepdims=True)
            var = jnp.mean((x - mu) ** 2, -1, keepdims=True)
            return (x - mu) * jax.lax.rsqrt(var + EPS) * w + b

        def _sincos(n, d):
            inv = 1.0 / 10000.0 ** (jnp.arange(0, d, 2, dtype=jnp.float32) / d)
            ang = jnp.arange(n, dtype=jnp.float32)[:, None] * inv[None, :]
            return (jnp.sin(ang), jnp.cos(ang))

        def _rope(x, sin, cos):
            s = sin[None, None]
            c = cos[None, None]
            xe = x[..., ::2]
            xo = x[..., 1::2]
            re = xe * c - xo * s
            ro = xe * s + xo * c
            return jnp.stack((re, ro), axis=-1).reshape(x.shape)

        def _heads(t):
            b, n, _ = t.shape
            return t.reshape(b, n, H, DH).transpose(0, 2, 1, 3)

        def _attn(xq, ctx, wq, wkv, wo, bo):
            q = _heads(xq @ wq)
            k, v = jnp.split(ctx @ wkv, 2, axis=-1)
            k = _heads(k)
            v = _heads(v)
            sq, cq = _sincos(q.shape[2], DH)
            sk, ck = _sincos(k.shape[2], DH)
            q = _rope(q, sq, cq)
            k = _rope(k, sk, ck)
            sim = jnp.einsum('bhnd,bhmd->bhnm', q, k) * DH ** (-0.5)
            a = jax.nn.softmax(sim, axis=-1)
            o = jnp.einsum('bhnm,bhmd->bhnd', a, v)
            o = o.transpose(0, 2, 1, 3).reshape(xq.shape[0], xq.shape[1], MID)
            return o @ wo + bo

        def _adaln(x, c, lw, lb, gw, gb, bw, bb):
            g = (c @ gw + gb)[:, None, :]
            bt = (c @ bw + bb)[:, None, :]
            return _ln(x, lw, lb) * (1.0 + g) + bt
        attn_in = _adaln(x, cond, ln1_w, ln1_b, g1_w, g1_b, b1_w, b1_b)
        x = _attn(attn_in, attn_in, sa_wq, sa_wkv, sa_wo, sa_bo) + x
        cross_in = _adaln(x, cond, ln1_w, ln1_b, g1_w, g1_b, b1_w, b1_b)
        ctx_n = _ln(context, ca_lnc_w, ca_lnc_b)
        x = _attn(cross_in, ctx_n, ca_wq, ca_wkv, ca_wo, ca_bo) + x
        ffn_in = _adaln(x, cond, ln2_w, ln2_b, g2_w, g2_b, b2_w, b2_b)
        h = jax.nn.gelu(ffn_in @ ff_w1 + ff_b1, approximate=False)
        x = h @ ff_w2 + ff_b2 + x
        return x

    def _L1_xcond_ref(x, t, context, n1_w, n1_b, n2_w, n2_b, n3_w, n3_b, q1, k1, v1, o1_w, o1_b, q2, k2, v2, o2_w, o2_b, ff_w1, ff_b1, ff_w2, ff_b2):
        import jax, jax.numpy as jnp
        import numpy as np
        EPS = 1e-05

        def _ada_ln(x, t, W, b):
            emb = t @ W + b
            scale, shift = jnp.split(emb, 2, axis=-1)
            mu = x.mean(-1, keepdims=True)
            var = ((x - mu) ** 2).mean(-1, keepdims=True)
            xn = (x - mu) * jax.lax.rsqrt(var + EPS)
            return xn * (1.0 + scale) + shift

        def _attn(x, ctx, Wq, Wk, Wv, Wo, bo, heads):
            b, n, _ = x.shape
            j = ctx.shape[1]
            q = (x @ Wq).reshape(b, n, heads, -1)
            k = (ctx @ Wk).reshape(b, j, heads, -1)
            v = (ctx @ Wv).reshape(b, j, heads, -1)
            scale = q.shape[-1] ** (-0.5)
            sim = jnp.einsum('bihd,bjhd->bhij', q, k) * scale
            attn = jax.nn.softmax(sim, axis=-1)
            out = jnp.einsum('bhij,bjhd->bihd', attn, v).reshape(b, n, -1)
            return out @ Wo + bo

        def _ff(x, W1, b1, W2, b2):
            p = x @ W1 + b1
            a, gate = jnp.split(p, 2, axis=-1)
            return a * jax.nn.gelu(gate, approximate=False) @ W2 + b2
        H = 16
        h = _ada_ln(x, t, n1_w, n1_b)
        x = _attn(h, h, q1, k1, v1, o1_w, o1_b, H) + x
        h = _ada_ln(x, t, n2_w, n2_b)
        x = _attn(h, context, q2, k2, v2, o2_w, o2_b, H) + x
        h = _ada_ln(x, t, n3_w, n3_b)
        x = _ff(h, ff_w1, ff_b1, ff_w2, ff_b2) + x
        return x
    x = _L0_xcond_ref(x, cond_1024, ctx_768, L0_xcond_ln1_w, L0_xcond_ln1_b, L0_xcond_g1_w, L0_xcond_g1_b, L0_xcond_b1_w, L0_xcond_b1_b, L0_xcond_ln2_w, L0_xcond_ln2_b, L0_xcond_g2_w, L0_xcond_g2_b, L0_xcond_b2_w, L0_xcond_b2_b, L0_xcond_sa_wq, L0_xcond_sa_wkv, L0_xcond_sa_wo, L0_xcond_sa_bo, L0_xcond_ca_lnc_w, L0_xcond_ca_lnc_b, L0_xcond_ca_wq, L0_xcond_ca_wkv, L0_xcond_ca_wo, L0_xcond_ca_bo, L0_xcond_ff_w1, L0_xcond_ff_b1, L0_xcond_ff_w2, L0_xcond_ff_b2)
    x = _L1_xcond_ref(x, cond_1024[:, None, :], ctx_768, L1_xcond_n1_w, L1_xcond_n1_b, L1_xcond_n2_w, L1_xcond_n2_b, L1_xcond_n3_w, L1_xcond_n3_b, L1_xcond_q1, L1_xcond_k1, L1_xcond_v1, L1_xcond_o1_w, L1_xcond_o1_b, L1_xcond_q2, L1_xcond_k2, L1_xcond_v2, L1_xcond_o2_w, L1_xcond_o2_b, L1_xcond_ff_w1, L1_xcond_ff_b1, L1_xcond_ff_w2, L1_xcond_ff_b2)
    return x

_drawn_inputs = setup_inputs


def setup_inputs(seed=0):
    import zlib

    import numpy as np

    out = dict(_drawn_inputs(seed))
    spreads = {'L0_xcond_ln1_w': (1.0, 0.6),
     'L0_xcond_ln1_b': (0.0, 0.584),
     'L0_xcond_g1_b': (0.0, 0.8),
     'L0_xcond_b1_b': (0.0, 0.52),
     'L0_xcond_ln2_w': (1.0, 0.6),
     'L0_xcond_ln2_b': (0.0, 0.8),
     'L0_xcond_g2_b': (0.0, 0.8),
     'L0_xcond_b2_b': (0.0, 0.8),
     'L0_xcond_sa_bo': (0.0, 0.1),
     'L0_xcond_ca_lnc_w': (1.0, 0.6),
     'L0_xcond_ca_lnc_b': (0.0, 0.635),
     'L0_xcond_ca_bo': (0.0, 0.1),
     'L0_xcond_ff_b1': (0.0, 0.354),
     'L0_xcond_ff_b2': (0.0, 0.1),
     'L1_xcond_n1_b': (0.0, 0.557),
     'L1_xcond_n2_b': (0.0, 0.8),
     'L1_xcond_n3_b': (0.0, 0.8),
     'L1_xcond_o1_b': (0.0, 0.1),
     'L1_xcond_o2_b': (0.0, 0.1),
     'L1_xcond_ff_b1': (0.0, 0.8),
     'L1_xcond_ff_b2': (0.0, 0.715)}
    factors = {'L0_xcond_g1_w': 8.0,
     'L0_xcond_g2_w': 4.304,
     'L0_xcond_b2_w': 4.662,
     'L0_xcond_sa_wq': 8.0,
     'L0_xcond_ca_wq': 8.0,
     'L1_xcond_n2_w': 8.0,
     'L1_xcond_n3_w': 8.0,
     'L1_xcond_q1': 8.0,
     'L1_xcond_k1': 8.0,
     'L1_xcond_q2': 8.0,
     'L1_xcond_k2': 8.0,
     'L1_xcond_ff_w1': 3.745,
     'L1_xcond_ff_w2': 3.64}
    for name, (base, spread) in spreads.items():
        noise = np.random.default_rng([zlib.crc32(name.encode()), seed]).standard_normal(out[name].shape)
        drawn = base * np.exp(spread * noise) if base else spread * noise
        out[name] = jnp.asarray(drawn.astype(out[name].dtype))
    for name, factor in factors.items():
        out[name] = (out[name] * factor).astype(out[name].dtype)
    return out
```

```python
from contextlib import ExitStack

import numpy as np

import concourse.bass as bass
from concourse import mybir

F32 = mybir.dt.float32
F32R = mybir.dt.float32r
ALU = mybir.AluOpType
ACT = mybir.ActivationFunctionType
AX_X = mybir.AxisListType.X

B, N, D = 4, 512, 128
H, DH = 16, 64
J, CD = 32, 96
P = 128
QT = N // P
KT = N // P
MID = H * DH
PAIRS = H // 2
FC = 4
TILES = 2 * QT
CG = H * J // P
SCALE = float(DH) ** -0.5
EPS = 1e-5

S_BANKS = 3
P_SLOTS = 12
NM = 16

SPLIT = ([("q", MID), ("k", MID), ("v", MID), ("cq", MID), ("f", FC * P)],
         [("q", MID), ("k", MID), ("v", MID), ("f", 2 * FC * P)])
SETUP = ([("ada", 4 * D), ("co", PAIRS * D)],
         [("ada", 6 * D), ("co", PAIRS * D), ("cq", MID)])
KEEP = [("wo", PAIRS * D), ("f2", FC * D)]
CTXW = [("ck", MID), ("cv", MID)]
N_COLS = (8 + FC, 6 + 2 * FC)
N_ROWS = (3 * D + 2 * CD, 3 * D)


def spans(parts):
    out, at = {}, 0
    for name, n in parts:
        out[name] = (at, n)
        at += n
    return out, at


class Layer:

    def __init__(self, rope):
        self.rope = rope
        order = [("h", 0)] + [("v", j) for j in range(2 * KT)]
        order += [(x, 0) for x in self.qk_kinds()]
        for c in range(PAIRS + 2):
            for s in range(TILES):
                order += self.projected(c, s)
        order += [("out", 0), ("h", 1)]
        if rope:
            for c in range(PAIRS):
                order += [("cq", c), ("cqs", c)]
        order += [("out", 1), ("h", 2)]
        for i in range(FC):
            order += [("gate", i)] if rope else [("gate", i), ("up", i)]
        order += [("out", 2)]
        self.order = order
        self.index = {x: i for i, x in enumerate(order)}
        self.n_proj = len(order)
        self.n_mul = 4 * PAIRS + 2 * PAIRS if rope else 0
        self.n_add = 2 * PAIRS + PAIRS if rope else 0

    def qk_kinds(self):
        return ["q", "qs", "k", "ks"] if self.rope else ["q", "k"]

    def projected(self, c, s):
        out = []
        if c + 1 < PAIRS:
            at = {1: "q", 2: "qs", 3: "k", 4: "ks"} if self.rope else {1: "q", 3: "k"}
            if s in at:
                out.append((at[s], c + 1))
        if 1 <= c <= PAIRS and s == 5:
            out.append(("r", c - 1))
        return out


N_S = PAIRS * TILES + QT
N_T = PAIRS * TILES + CG
N_QK = 3 * PAIRS
N_AV = PAIRS * KT
LN_STEPS = 5


def build(nc, x_in, x_mid, x_out, ctx_in, cond_in, tables, w128, w96, colp, rowp):
    with ExitStack() as top:
        def sb(name, shape, dt=F32, stack=top):
            return stack.enter_context(nc.sbuf_tensor(name, shape, dt))

        ident = sb("ident", [P, P])
        arena = sb("arena", [P, 20, N])
        probs = arena[:, 0:P_SLOTS, :]
        probsT = arena[:, P_SLOTS:P_SLOTS + 8, :]
        raw = arena[:, :, :].rearrange("p a n -> p (a n)")
        v_sb = sb("v_sb", [P, KT, MID])
        oT = sb("oT", [P, PAIRS, N])
        h_f = sb("h_f", [P, N])
        xn = h_f[:, :].rearrange("p (t d) -> p t d", t=QT)
        h_hi = sb("h_hi", [P, N], F32R)
        h_lo = sb("h_lo", [P, N], F32R)
        q_hi = sb("q_hi", [P, 2, N], F32R)
        q_lo = sb("q_lo", [P, 2, N], F32R)
        k_hi = sb("k_hi", [P, 2, 2, N], F32R)
        k_lo = sb("k_lo", [P, 2, 2, N], F32R)
        x_sb = sb("x_sb", [P, QT, D])
        x_new = sb("x_new", [P, QT, D])
        r_in = sb("r_in", [P, QT, 2, DH])
        r_sb = sb("r_sb", [P, N])
        condT = sb("condT", [P, B])
        stats = sb("stats", [P, QT, 6])
        mv = sb("mv", [P, QT, 2])
        rstd = sb("rstd", [P, QT])
        log_var = sb("log_var", [P, QT])
        root = sb("root", [P, QT])
        sq = sb("sq", [P, QT])
        negmax = sb("negmax", [P, NM])
        sums = sb("sums", [P, 2, TILES])
        recips = sb("recips", [P, TILES])
        c_negmax = sb("c_negmax", [P, QT, H])
        c_sum = sb("c_sum", [P, QT, H])
        c_recip = sb("c_recip", [P, QT, H])
        vec_b = sb("vec_b", [P, 6])
        ones = sb("ones", [P, 1])

        def bank(name):
            return top.enter_context(nc.psum_tensor(name, [P, N], F32))

        s_bank = [bank(f"s_bank{i}") for i in range(S_BANKS)]
        t_bank = [bank(f"t_bank{i}") for i in range(2)]
        pj_bank = [bank(f"pj_bank{i}") for i in range(2)]
        o_bank = bank("o_bank")

        for li in range(2):
            with ExitStack() as lay:
                L = Layer(rope=li == 0)

                def lsb(name, shape, dt=F32):
                    return sb(f"l{li}_{name}", shape, dt, lay)

                w_hi = {n: lsb(f"{n}_hi", [P, c], F32R) for n, c in SPLIT[li]}
                w_lo = {n: lsb(f"{n}_lo", [P, c], F32R) for n, c in SPLIT[li]}
                swapped = [("q", "qs"), ("k", "ks"), ("cq", "cqs")] if L.rope else []
                for _, n in swapped:
                    w_hi[n] = lsb(f"{n}_hi", [P, MID], F32R)
                    w_lo[n] = lsb(f"{n}_lo", [P, MID], F32R)
                wo = lsb("wo", [P, PAIRS, D])
                f2 = lsb("f2", [P, FC, D])
                cols = lsb("cols", [P, N_COLS[li]])
                bias_rows = lsb("bias_rows", [P, 3, D])
                vecs = lsb("vecs", [P, B, 6])
                vw = lsb("vw", [P, B, CG, D])
                env = dict(locals())
                env.pop("env", None)
                if L.rope:
                    env["rope_cs"] = lsb("rope_cs", [P, 2, N])
                    env["rot_a"] = lsb("rot_a", [P, 2, N])
                    env["rot_b"] = lsb("rot_b", [P, 2, N])
                    env["kc"] = lsb("kc", [P, PAIRS, B * J])
                    env["k_diag"] = lsb("k_diag", [P, PAIRS, P])
                else:
                    env["kw_hi"] = lsb("kw_hi", [P, B, H * J], F32R)
                    env["kw_lo"] = lsb("kw_lo", [P, B, H * J], F32R)
                src = (x_in, x_mid)[li]
                dst = (x_mid, x_out)[li]
                setup(nc, li, L, env, ctx_in, cond_in, tables, w128[li], w96[li], colp[li], rowp[li])
                batch_loop(nc, li, L, env, src, dst)


def setup(nc, li, L, e, ctx_in, cond_in, tables, w128, w96, colp, rowp):
    raw, ident, v_sb, oT, condT = e["raw"], e["ident"], e["v_sb"], e["oT"], e["condT"]
    w_hi, w_lo, wo, f2, cols, bias_rows = e["w_hi"], e["w_lo"], e["wo"], e["f2"], e["cols"], e["bias_rows"]
    vecs, vw, swapped = e["vecs"], e["vw"], e["swapped"]
    s_bank, t_bank, pj_bank, o_bank = e["s_bank"], e["t_bank"], e["pj_bank"], e["o_bank"]
    split_at, n_split = spans(SPLIT[li])
    setup_at, n_setup = spans(SETUP[li])
    keep_at, n_keep = spans(KEEP)
    ctx_at, n_ctx = spans(CTXW)

    def part(name):
        if name in split_at:
            a, n = split_at[name]
        elif name in setup_at:
            a, n = setup_at[name]
            a += n_split
        else:
            a, n = ctx_at[name]
            a += n_split + n_setup
        return raw[:, a:a + n]

    ctx_sb = v_sb[:, 0, 0:CD]
    ctx_n = v_sb[:, 0, P:P + CD]
    ctxT = v_sb[:, 0, 2 * P:3 * P]
    lnc = v_sb[:, 0, 3 * P:3 * P + 2 * CD]
    vcT = v_sb[:, 1, :].rearrange("p (c n) -> p c n", c=PAIRS)
    wqT = v_sb[:, 2, :].rearrange("p (c n) -> p c n", c=PAIRS)
    kT = e["kc"] if L.rope else v_sb[:, 3, :].rearrange("p (c n) -> p c n", c=PAIRS)
    kT2 = v_sb[:, 2, :].rearrange("p (c n) -> p c n", c=PAIRS)
    vw_rows = oT[:, 0:4, :].rearrange("p c (h d) -> p (c h) d", d=D)
    cks = oT[:, 4:6, :].rearrange("p a n -> p (a n)")
    co = part("co").rearrange("p (c d) -> p c d", c=PAIRS)

    with ExitStack() as st:
        def sem(name):
            return st.enter_context(nc.semaphore(f"l{li}_{name}"))

        small_in, ctx_in_s, kv_in, setup_in, keep_in = (
            sem("small_in"), sem("ctx_in"), sem("kv_in"), sem("setup_in"), sem("keep_in"))
        w_in = {n: sem(f"w_in_{n}") for n, _ in SPLIT[li]}
        id_made = sem("id_made")
        hi_made, lo_made, swap_made = sem("hi_made"), sem("lo_made"), sem("swap_made")
        ctx_step, ctx_ready = sem("ctx_step"), sem("ctx_ready")
        log_made, root_made = sem("log_made"), sem("root_made")
        ctxT_full, ctxT_made = sem("ctxT_full"), sem("ctxT_made")
        ada_full, ada_step = sem("ada_full"), sem("ada_step")
        kT_full, vT_full, wqT_full = sem("kT_full"), sem("vT_full"), sem("wqT_full")
        kT_step, vT_made, wqT_made = sem("kT_step"), sem("vT_made"), sem("wqT_made")
        cks_made = sem("cks_made")
        vw_full, vw_made, vw_moved = sem("vw_full"), sem("vw_made"), sem("vw_moved")
        kw_full, kw_hi_made, kw_lo_made = sem("kw_full"), sem("kw_hi_made"), sem("kw_lo_made")

        block = st.enter_context(nc.Block())

        @block.sync
        def _(sp):
            sp.dma_start(ctx_sb, ctx_in).then_inc(ctx_in_s, 16)
            a = n_split + n_setup
            if L.rope:
                sp.dma_start(lnc, rowp[0:1, 3 * D:3 * D + 2 * CD].broadcast_to([P, 2 * CD])).then_inc(small_in, 16)
                sp.dma_start(e["rope_cs"][:, :, :], tables.rearrange("p (a n) -> p a n", a=2)).then_inc(small_in, 16)
            sp.dma_start(condT[:, :], cond_in).then_inc(small_in, 16)
            sp.dma_start(cols[:, :], colp).then_inc(small_in, 16)
            sp.dma_start(bias_rows[:, :, :].rearrange("p a d -> p (a d)"),
                         rowp[0:1, 0:3 * D].broadcast_to([P, 3 * D])).then_inc(small_in, 16)
            sp.dma_start(raw[0:CD, a:a + n_ctx], w96).then_inc(kv_in, 16)
            sp.dma_start(raw[:, n_split:a], w128[:, n_split:a]).then_inc(setup_in, 16)
            sp.dma_start(wo[:, :, :].rearrange("p c d -> p (c d)"), w128[:, a:a + PAIRS * D]).then_inc(keep_in, 16)
            sp.dma_start(f2[:, :, :].rearrange("p c d -> p (c d)"),
                         w128[:, a + PAIRS * D:a + n_keep]).then_inc(keep_in, 16)
            sp.wait_ge(vw_made, 4)
            for b in range(B):
                for r in range(P // J):
                    sp.dma_start(vw[r * J:(r + 1) * J, b, :, :],
                                 vw_rows[b * J:(b + 1) * J, :, :].rearrange(
                                     "p (g r) d -> p g r d", r=P // J)[:, :, r, :]).then_inc(vw_moved, 16)
            sp.wait_ge(vw_moved, 16 * B * (P // J))
            sp.wait_ge(keep_in, 32)
            sp.wait_ge(small_in, 16 * (5 if L.rope else 3))

        @block.gpsimd
        def _(pool):
            if li == 0:
                pool.memset(ident[:, :], 0.0).then_inc(id_made, 1)
                pool.wait_ge(id_made, 1)
                pool.affine_select(out=ident[:, :], in_=ident[:, :], compare_op=ALU.not_equal, fill=1.0,
                                   base=0, pattern=[[-1, P]], channel_multiplier=1).then_inc(id_made, 1)
            if L.rope:
                pool.wait_ge(kv_in, 16)
                pair = "p (i t) -> p i t"
                for t in range(2):
                    pool.tensor_copy(cks[0:CD, :].rearrange(pair, t=2)[:, :, t],
                                     part("ck")[0:CD, :].rearrange(pair, t=2)[:, :, 1 - t]).then_inc(cks_made, 1)

        @block.scalar
        def _(act):
            for n, _ in SPLIT[li]:
                a, c = split_at[n]
                act.dma_start(raw[:, a:a + c], w128[:, a:a + c]).then_inc(w_in[n], 16)
            if L.rope:
                act.wait_ge(ctx_step, 2)
                act.activation(e["log_var"][:, 0:1], e["mv"][:, 0, 1:2], ACT.Ln, bias=EPS).then_inc(log_made, 1)
                act.wait_ge(log_made, 1)
                act.activation(e["root"][:, 0:1], e["log_var"][:, 0:1], ACT.Exp, scale=-0.5).then_inc(root_made, 1)
            act.wait_ge(ctxT_full, 1)
            act.copy(ctxT[0:CD, :], o_bank[0:CD, 0:P]).then_inc(ctxT_made, 1)
            act.wait_ge(vT_full, 1)
            for i in range(2):
                act.copy(vcT[:, 4 * i:4 * i + 4, :].rearrange("p c n -> p (c n)"), s_bank[i][:, :]).then_inc(vT_made, 1)
            if not L.rope:
                act.wait_ge(kT_full, 1)
                for i in range(2):
                    act.copy(kT[:, 4 * i:4 * i + 4, :].rearrange("p c n -> p (c n)"),
                             pj_bank[i][:, :]).then_inc(kT_step, 1)
                act.wait_ge(wqT_full, 1)
                for i in range(2):
                    act.mul(wqT[:, 4 * i:4 * i + 4, :].rearrange("p c n -> p (c n)"),
                            t_bank[i][:, :], SCALE).then_inc(wqT_made, 1)
            for n, _ in SPLIT[li]:
                act.wait_ge(w_in[n], 16)
                act.copy(w_hi[n][:, :], part(n)).then_inc(hi_made, 1)
            act.wait_ge(vw_full, 1)
            for i, bk in enumerate((pj_bank[0], pj_bank[1], t_bank[0], t_bank[1])):
                odd, half = i // 2, i % 2
                act.copy(vw_rows[:, 8 * half:8 * half + 8, :].rearrange("p (j o) d -> p j o d", o=2)[:, :, odd, :],
                         bk[:, :].rearrange("p (j d) -> p j d", d=D)).then_inc(vw_made, 1)
            if not L.rope:
                act.wait_ge(kw_full, 1)
                for i, bk in enumerate((s_bank[0], s_bank[1], s_bank[2], o_bank)):
                    odd, half = i // 2, i % 2
                    for j in range(4):
                        h = 8 * half + 2 * j + odd
                        ins = act.copy(e["kw_hi"][:, :, h * J:(h + 1) * J],
                                       bk[:, j * P:(j + 1) * P].rearrange("p (b k) -> p b k", b=B))
                    ins.then_inc(kw_hi_made, 1)

        @block.vector
        def _(dve):
            if li == 0:
                for t in (e["k_hi"], e["k_lo"]):
                    for half in range(2):
                        dve.memset(t[DH * half:DH * half + DH, :, 1 - half, :].bitcast(F32), 0.0)
                dve.memset(e["ones"][:, :], 1.0)
                dve.memset(e["k_diag"][:, :, :], 0.0)
            if L.rope:
                dve.wait_ge(ctx_in_s, 16)
                dve.bn_stats(e["stats"][:, 0, :], ctx_sb).then_inc(ctx_step, 1)
                dve.wait_ge(ctx_step, 1)
                dve.bn_aggr(e["mv"][:, 0, :], e["stats"][:, 0, :]).then_inc(ctx_step, 1)
                dve.wait_ge(ctx_step, 2)
                root, sq, rstd, var = e["root"][:, 0:1], e["sq"][:, 0:1], e["rstd"][:, 0:1], e["mv"][:, 0, 1:2]
                dve.wait_ge(root_made, 1)
                dve.tensor_tensor(sq, root, root, ALU.mult).then_inc(ctx_step, 1)
                dve.wait_ge(ctx_step, 3)
                dve.scalar_tensor_tensor(out=sq, in0=var, scalar=EPS, in1=sq, op0=ALU.add, op1=ALU.mult).then_inc(ctx_step, 1)
                dve.wait_ge(ctx_step, 4)
                dve.tensor_scalar(sq, sq, -0.5, 1.5, ALU.mult, ALU.add).then_inc(ctx_step, 1)
                dve.wait_ge(ctx_step, 5)
                dve.tensor_tensor(rstd, root, sq, ALU.mult).then_inc(ctx_step, 1)
                dve.wait_ge(ctx_step, 6)
                dve.tensor_scalar(ctx_n, ctx_sb, e["mv"][:, 0, 0:1], e["rstd"][:, 0:1],
                                  ALU.subtract, ALU.mult).then_inc(ctx_step, 1)
                dve.wait_ge(ctx_step, 7)
                dve.wait_ge(small_in, 16 * 5)
                dve.tensor_tensor(ctx_n, ctx_n, lnc[:, 0:CD], ALU.mult).then_inc(ctx_step, 1)
                dve.wait_ge(ctx_step, 8)
                dve.tensor_tensor(ctx_n, ctx_n, lnc[:, CD:2 * CD], ALU.add).then_inc(ctx_ready, 1)
            dve.wait_ge(small_in, 16 * (5 if L.rope else 3))
            dve.wait_ge(ada_full, 1)
            A = s_bank[2]
            if L.rope:
                for m in range(2):
                    n = (0, 2)[m]
                    g, bt = A[:, 8 * m:8 * m + B], A[:, 8 * m + 4:8 * m + 4 + B]
                    lw, lb, gb, bb = (cols[:, 4 * m + i:4 * m + i + 1] for i in range(4))
                    sc, sh = vecs[:, :, 2 * n], vecs[:, :, 2 * n + 1]
                    dve.tensor_scalar(sc, g, gb, 1.0, ALU.add, ALU.add).then_inc(ada_step, 1)
                    dve.wait_ge(ada_step, 4 * m + 1)
                    dve.tensor_scalar(sh, sc, lb, bb, ALU.mult, ALU.add).then_inc(ada_step, 1)
                    dve.wait_ge(ada_step, 4 * m + 2)
                    dve.tensor_tensor(sh, sh, bt, ALU.add).then_inc(ada_step, 1)
                    dve.tensor_scalar(sc, sc, lw, None, ALU.mult).then_inc(ada_step, 1)
                    dve.wait_ge(ada_step, 4 * m + 4)
                dve.tensor_copy(vecs[:, :, 2:4], vecs[:, :, 0:2]).then_inc(ada_step, 1)
            else:
                for n in range(3):
                    dve.tensor_scalar(vecs[:, :, 2 * n], A[:, 8 * n:8 * n + B], cols[:, 2 * n:2 * n + 1], 1.0,
                                      ALU.add, ALU.add).then_inc(ada_step, 1)
                    dve.tensor_scalar(vecs[:, :, 2 * n + 1], A[:, 8 * n + 4:8 * n + 4 + B],
                                      cols[:, 2 * n + 1:2 * n + 2], None, ALU.add).then_inc(ada_step, 1)
            if L.rope:
                dve.wait_ge(kT_full, 1)
                for src, dst, cs in ((pj_bank, kT, 0), (t_bank, kT2, 1)):
                    for i in range(2):
                        dve.tensor_tensor(
                            dst[:, 4 * i:4 * i + 4, :].rearrange("p c (b k) -> p (c b) k", k=J),
                            src[i][:, :].rearrange("p (m k) -> p m k", k=J),
                            e["rope_cs"][:, cs, 0:J].unsqueeze(1).broadcast_to([P, 4 * B, J]),
                            ALU.mult).then_inc(kT_step, 1)
                dve.wait_ge(kT_step, 4)
                dve.tensor_tensor(kT[:, :, :], kT[:, :, :], kT2[:, :, :], ALU.add).then_inc(kT_step, 1)
            for i, (n, _) in enumerate(SPLIT[li]):
                dve.wait_ge(hi_made, i + 1)
                dve.tensor_tensor(w_lo[n][:, :], part(n), w_hi[n][:, :].bitcast(F32), ALU.subtract).then_inc(lo_made, 1)
            for n, ns in swapped:
                i = [m for m, _ in SPLIT[li]].index(n)
                dve.wait_ge(lo_made, i + 1)
                for w in (w_hi, w_lo):
                    s = w[n][:, :].bitcast(F32).rearrange("p (i t) -> p i t", t=2)
                    d = w[ns][:, :].rearrange("p (i t) -> p i t", t=2)
                    for t in range(2):
                        dve.tensor_copy(d[:, :, t], s[:, :, 1 - t]).then_inc(swap_made, 1)
            if not L.rope:
                for i, bk in enumerate((s_bank[0], s_bank[1], s_bank[2], o_bank)):
                    odd, half = i // 2, i % 2
                    dve.wait_ge(kw_hi_made, i + 1)
                    for j in range(4):
                        h = 8 * half + 2 * j + odd
                        ins = dve.tensor_tensor(e["kw_lo"][:, :, h * J:(h + 1) * J],
                                                bk[:, j * P:(j + 1) * P].rearrange("p (b k) -> p b k", b=B),
                                                e["kw_hi"][:, :, h * J:(h + 1) * J].bitcast(F32), ALU.subtract)
                    ins.then_inc(kw_lo_made, 1)

        @block.tensor
        def _(pe):
            if li == 0:
                pe.wait_ge(id_made, 2)
            if L.rope:
                pe.wait_ge(ctx_ready, 1)
            else:
                pe.wait_ge(ctx_in_s, 16)
            pe.transpose(o_bank[0:CD, 0:P], ctx_n if L.rope else ctx_sb, ident[:, :]).then_inc(ctxT_full, 1)
            pe.wait_ge(setup_in, 16)
            pe.wait_ge(small_in, 16 * (5 if L.rope else 3))
            ada = part("ada")
            for m in range(SETUP[li][0][1] // D):
                ins = pe.matmul(s_bank[2][:, 4 * m:4 * m + B], ada[:, m * D:(m + 1) * D], condT[:, :],
                                start=True, stop=True)
            ins.then_inc(ada_full, 1)
            pe.wait_ge(ctxT_made, 1)
            pe.wait_ge(kv_in, 16)
            ck, cv = part("ck"), part("cv")
            for c in range(PAIRS):
                ins = pe.matmul(s_bank[c // 4][:, (c % 4) * P:(c % 4 + 1) * P], cv[0:CD, c * P:(c + 1) * P],
                                ctxT[0:CD, :], start=True, stop=True)
            ins.then_inc(vT_full, 1)
            for c in range(PAIRS):
                ins = pe.matmul(pj_bank[c // 4][:, (c % 4) * P:(c % 4 + 1) * P], ck[0:CD, c * P:(c + 1) * P],
                                ctxT[0:CD, :], start=True, stop=True)
            if L.rope:
                pe.wait_ge(cks_made, 2)
                for c in range(PAIRS):
                    ins = pe.matmul(t_bank[c // 4][:, (c % 4) * P:(c % 4 + 1) * P], cks[0:CD, c * P:(c + 1) * P],
                                    ctxT[0:CD, :], start=True, stop=True)
            ins.then_inc(kT_full, 1)
            if not L.rope:
                cq = part("cq")
                for c in range(PAIRS):
                    ins = pe.transpose(t_bank[c // 4][:, (c % 4) * P:(c % 4 + 1) * P], cq[:, c * P:(c + 1) * P],
                                       ident[:, :])
                ins.then_inc(wqT_full, 1)
            pe.wait_ge(vT_made, 2)
            if L.rope:
                pe.wait_ge(kT_step, 4)
            else:
                pe.wait_ge(kT_step, 2)
                pe.wait_ge(wqT_made, 2)
            for odd in range(2):
                r = slice(DH * odd, DH * odd + DH)
                for c in range(PAIRS):
                    bk = (t_bank if odd else pj_bank)[c // 4]
                    ins = pe.matmul(bk[:, (c % 4) * P:(c % 4 + 1) * P], vcT[r, c, :], co[r, c, :],
                                    start=True, stop=True)
            ins.then_inc(vw_full, 1)
            if not L.rope:
                pe.wait_ge(ada_step, 6)
                for odd in range(2):
                    r = slice(DH * odd, DH * odd + DH)
                    for c in range(PAIRS):
                        bk = (s_bank[0], s_bank[1], s_bank[2], o_bank)[2 * odd + c // 4]
                        ins = pe.matmul(bk[:, (c % 4) * P:(c % 4 + 1) * P], wqT[r, c, :], kT[r, c, :],
                                        start=True, stop=True)
                ins.then_inc(kw_full, 1)


def batch_loop(nc, li, L, e, src, dst):
    ident, v_sb, oT, probs, probsT = e["ident"], e["v_sb"], e["oT"], e["probs"], e["probsT"]
    h_f, xn, h_hi, h_lo = e["h_f"], e["xn"], e["h_hi"], e["h_lo"]
    q_hi, q_lo, k_hi, k_lo = e["q_hi"], e["q_lo"], e["k_hi"], e["k_lo"]
    x_sb, x_new, r_in, r_sb = e["x_sb"], e["x_new"], e["r_in"], e["r_sb"]
    stats, mv, rstd, negmax = e["stats"], e["mv"], e["rstd"], e["negmax"]
    log_var, root, sq = e["log_var"], e["root"], e["sq"]
    sums, recips, c_negmax, c_sum, c_recip = e["sums"], e["recips"], e["c_negmax"], e["c_sum"], e["c_recip"]
    vec_b, vecs, vw, cols, bias_rows = e["vec_b"], e["vecs"], e["vw"], e["cols"], e["bias_rows"]
    w_hi, w_lo, wo, f2 = e["w_hi"], e["w_lo"], e["wo"], e["f2"]
    s_bank, t_bank, pj_bank, o_bank = e["s_bank"], e["t_bank"], e["pj_bank"], e["o_bank"]
    STEPS = range(PAIRS + 2)

    with ExitStack() as st:
        def sem(name):
            return st.enter_context(nc.semaphore(f"l{li}_{name}"))

        x_loaded, x_new_free = sem("x_loaded"), sem("x_new_free")
        biased = sem("biased")
        log_made, root_made = sem("log_made"), sem("root_made")
        ln_step, xn_made, h_full, h_hi_made, h_lo_made = (
            sem("ln_step"), sem("xn_made"), sem("h_full"), sem("h_hi_made"), sem("h_lo_made"))
        pj_full = sem("pj_full")
        v_act, v_dve = sem("v_act"), sem("v_dve")
        rope_mul, rope_add = sem("rope_mul"), sem("rope_add")
        qk_hi, qk_lo = sem("qk_hi"), sem("qk_lo")
        s_full, max_made, exp_made = sem("s_full"), sem("max_made"), sem("exp_made")
        t_full, pt_act, pt_dve = sem("t_full"), sem("pt_act"), sem("pt_dve")
        recip_made, r_in_made, r_made = sem("recip_made"), sem("r_in_made"), sem("r_made")
        av_done, o_made, added = sem("av_done"), sem("o_made"), sem("added")
        diag_made, c_max, c_sub, c_summed, c_inv, c_norm = (
            sem("diag_made"), sem("c_max"), sem("c_sub"), sem("c_summed"), sem("c_inv"), sem("c_norm"))
        gelu_made, hid_made = sem("gelu_made"), sem("hid_made")

        def pj(name):
            return pj_bank[L.index[name] % 2]

        def filled(name, b):
            return b * L.n_proj + L.index[name] + 1

        def freed(name):
            kind, i = name
            if kind == "h":
                return h_full, 3, i + 1
            if kind == "v":
                return (v_dve if i % 2 else v_act), KT, i // 2 + 1
            if kind == "r":
                return r_made, PAIRS, i + 1
            if kind == "out":
                return added, 3, i + 1
            if kind == "gate":
                return gelu_made, FC, i + 1
            if kind == "up":
                return hid_made, FC, i + 1
            if L.rope:
                if kind in ("cq", "cqs"):
                    return rope_mul, L.n_mul, 4 * PAIRS + 2 * i + ("cq", "cqs").index(kind) + 1
                return rope_mul, L.n_mul, 4 * i + L.qk_kinds().index(kind) + 1
            return qk_lo, N_QK, 3 * i + (1 if kind == "q" else 3)

        block = st.enter_context(nc.Block())

        @block.sync
        def _(sp):
            rows = "b (t p) d -> b p t d"
            sp.sem_inc(x_new_free, 16)
            sp.dma_start(x_sb[:, :, :], src.rearrange(rows, p=P)[0]).then_inc(x_loaded, 16)
            with sp.Fori(0, B - 1) as b:
                sp.wait_ge(added, b * 3 + 1)
                sp.dma_start(x_sb[:, :, :], src.rearrange(rows, p=P)[bass.ds(b + 1, 1)].rearrange(
                    "b p t d -> (b p) t d")).then_inc(x_loaded, 16)
                sp.wait_ge(added, b * 3 + 3)
                sp.dma_start(dst.rearrange(rows, p=P)[bass.ds(b, 1)].rearrange("b p t d -> (b p) t d"),
                             x_new[:, :, :]).then_inc(x_new_free, 16)
            sp.wait_ge(added, 3 * B)
            sp.dma_start(dst.rearrange(rows, p=P)[B - 1], x_new[:, :, :]).then_inc(x_new_free, 16)
            sp.wait_ge(x_new_free, 16 * (B + 1))

        @block.gpsimd
        def _(pool):
            def add_bias(b, n):
                x = x_sb if n == 0 else x_new
                pool.wait_ge(xn_made, b * 3 + n + 1)
                pool.tensor_tensor(x[:, :, :], x[:, :, :],
                                   bias_rows[:, n, :].unsqueeze(1).broadcast_to([P, QT, D]),
                                   ALU.add).then_inc(biased, 1)

            def rope_sum(b, j, out):
                pool.wait_ge(rope_mul, b * L.n_mul + 2 * j + 2)
                pool.tensor_tensor(out, e["rot_a"][:, j % 2, :], e["rot_b"][:, j % 2, :], ALU.add).then_inc(rope_add, 1)

            with pool.Fori(0, B) as b:
                add_bias(b, 0)
                if L.rope:
                    for j in range(2):
                        rope_sum(b, j, e["rot_a"][:, j, :])
                for c in STEPS:
                    if 1 <= c <= PAIRS:
                        pool.wait_ge(recip_made, b * PAIRS + c)
                        if c >= 2:
                            pool.wait_ge(pj_full, filled(("r", c - 2), b))
                        pool.tensor_tensor(r_in[:, :, :, :].rearrange("p t h d -> p h t d"),
                                           recips[:, :].rearrange("p (h t) -> p h t", h=2).unsqueeze(3)
                                           .broadcast_to([P, 2, QT, DH]),
                                           e["ones"][:, 0:1].unsqueeze(2).unsqueeze(3).broadcast_to([P, 2, QT, DH]),
                                           ALU.mult).then_inc(r_in_made, 1)
                    if L.rope and c + 1 < PAIRS:
                        for j in range(2 * c + 2, 2 * c + 4):
                            rope_sum(b, j, e["rot_a"][:, j % 2, :])
                add_bias(b, 1)
                if L.rope:
                    for c in range(PAIRS):
                        rope_sum(b, 2 * PAIRS + c, oT[:, c, :])
                for t in range(QT):
                    pool.wait_ge(c_inv, b * QT + t + 1)
                    p4 = probs[:, t, :].rearrange("p (h k) -> p h k", k=J)
                    pool.tensor_tensor(p4, p4, c_recip[:, t, :].unsqueeze(2).broadcast_to([P, H, J]),
                                       ALU.mult).then_inc(c_norm, 1)
                add_bias(b, 2)

        @block.tensor
        def _(pe):
            def claim(name, b):
                i = L.index[name]
                if i >= 2:
                    s, per, n = freed(L.order[i - 2])
                    pe.wait_ge(s, b * per + n)

            def three(out, a_hi, a_lo, b_hi, b_lo):
                pe.matmul(out, a_hi, b_hi, start=True, stop=False)
                pe.matmul(out, a_lo, b_hi, start=False, stop=False)
                return pe.matmul(out, a_hi, b_lo, start=False, stop=True)

            def turn_norm(b, n):
                pe.wait_ge(xn_made, b * 3 + n + 1)
                claim(("h", n), b)
                for t in range(QT):
                    ins = pe.transpose(pj(("h", n))[:, t * P:(t + 1) * P], xn[:, t, :], ident[:, :])
                ins.then_inc(pj_full, 1)

            def project(name, w, chunk, b):
                claim(name, b)
                cs = slice(chunk * P, chunk * P + P)
                three(pj(name)[:, :], w_hi[w][:, cs], w_lo[w][:, cs], h_hi[:, :], h_lo[:, :]).then_inc(pj_full, 1)

            def values(j, b):
                kt, half = j // 2, j % 2
                claim(("v", j), b)
                ts, cs = slice(kt * P, kt * P + P), slice(half * N, half * N + N)
                three(pj(("v", j))[:, :], h_hi[:, ts], h_lo[:, ts], w_hi["v"][:, cs], w_lo["v"][:, cs]).then_inc(pj_full, 1)

            def recip_rows(p, b):
                pe.wait_ge(r_in_made, b * PAIRS + p + 1)
                claim(("r", p), b)
                for t in range(QT):
                    ins = pe.transpose(pj(("r", p))[:, t * P:(t + 1) * P],
                                       r_in[:, t, :, :].rearrange("p h d -> p (h d)"), ident[:, :])
                ins.then_inc(pj_full, 1)

            def scores(c, s, b):
                n = c * TILES + s
                head, qt = s // QT, s % QT
                if s == 0:
                    pe.wait_ge(qk_lo, b * N_QK + 3 * c + 3)
                if n >= S_BANKS:
                    pe.wait_ge(exp_made, b * N_S + n - S_BANKS + 1)
                ts = slice(qt * P, qt * P + P)
                three(s_bank[n % S_BANKS][:, :], q_hi[:, c % 2, ts], q_lo[:, c % 2, ts],
                      k_hi[:, c % 2, head, :], k_lo[:, c % 2, head, :]).then_inc(s_full, 1)

            def turn_probs(p, i, b):
                head, kt = i // KT, i % KT
                if kt == 0:
                    pe.wait_ge(exp_made, b * N_S + p * TILES + head * QT + QT)
                if 4 * p + i // 2:
                    pe.wait_ge((pt_act, pt_dve)[i % 2], b * (N_T // 2) + 4 * p + i // 2)
                for t in range(QT):
                    slot = (p * TILES + head * QT + t) % P_SLOTS
                    ins = pe.transpose(t_bank[i % 2][:, t * P:(t + 1) * P], probs[:, slot, kt * P:(kt + 1) * P],
                                       ident[:, :])
                ins.then_inc(t_full, 1)

            def weigh(p, k, b):
                if k == 0 and p == 0:
                    pe.wait_ge(v_act, b * KT + KT)
                    pe.wait_ge(v_dve, b * KT + KT)
                elif k == 0:
                    pe.wait_ge(o_made, b * PAIRS + p)
                pe.wait_ge((pt_act, pt_dve)[k % 2], b * (N_T // 2) + 4 * p + (KT + k) // 2 + 1)
                for head in range(2):
                    h = 2 * p + head
                    ins = pe.matmul(o_bank[DH * head:DH * head + DH, :], v_sb[:, k, h * DH:(h + 1) * DH],
                                    probsT[:, KT * head + k, :], start=(k == 0), stop=(k == KT - 1))
                ins.then_inc(av_done, 1)

            def output(n, b, lhs, rhs, steps):
                claim(("out", n), b)
                for t in range(QT):
                    for g in range(steps):
                        ins = pe.matmul(pj(("out", n))[:, t * P:(t + 1) * P], lhs(g, slice(t * P, t * P + P)), rhs(g),
                                        start=(g == 0), stop=(g == steps - 1))
                ins.then_inc(pj_full, 1)

            with pe.Fori(0, B) as b:
                turn_norm(b, 0)
                pe.wait_ge(h_lo_made, b * 3 + 1)
                for j in range(2 * KT):
                    values(j, b)
                for kind in L.qk_kinds():
                    project((kind, 0), kind, 0, b)
                for c in STEPS:
                    for s in range(TILES):
                        if c < PAIRS:
                            scores(c, s, b)
                        if 1 <= c <= PAIRS:
                            turn_probs(c - 1, s, b)
                            if s >= 5:
                                weigh(c - 1, s - 5, b)
                        if c >= 2 and s == 1:
                            weigh(c - 2, KT - 1, b)
                        for name in L.projected(c, s):
                            if name[0] == "r":
                                recip_rows(name[1], b)
                            else:
                                project(name, name[0], name[1], b)
                pe.wait_ge(o_made, b * PAIRS + PAIRS)
                output(0, b, lambda g, ts: oT[:, g, ts], lambda g: wo[:, g, :], PAIRS)
                turn_norm(b, 1)
                pe.wait_ge(h_lo_made, b * 3 + 2)
                if L.rope:
                    for c in range(PAIRS):
                        project(("cq", c), "cq", c, b)
                        project(("cqs", c), "cqs", c, b)
                    pe.wait_ge(rope_add, b * L.n_add + L.n_add)
                    pe.wait_ge(diag_made, b * 4 + 4)
                for t in range(QT):
                    n = PAIRS * TILES + t
                    ts = slice(t * P, t * P + P)
                    pe.wait_ge(exp_made, b * N_S + n - S_BANKS + 1)
                    if L.rope:
                        for c in range(PAIRS):
                            g = c // 2
                            ins = pe.matmul(s_bank[n % S_BANKS][:, g * P:(g + 1) * P], oT[:, c, ts],
                                            e["k_diag"][:, c, :], start=(c % 2 == 0), stop=(c % 2 == 1))
                        ins.then_inc(s_full, 1)
                    else:
                        kwh = e["kw_hi"][:, bass.ds(b, 1), :].rearrange("p b n -> p (b n)")
                        kwl = e["kw_lo"][:, bass.ds(b, 1), :].rearrange("p b n -> p (b n)")
                        three(s_bank[n % S_BANKS][:, :], h_hi[:, ts], h_lo[:, ts], kwh, kwl).then_inc(s_full, 1)
                pe.wait_ge(c_norm, b * QT + QT)
                for g in range(CG):
                    pe.wait_ge((pt_act, pt_dve)[g % 2], b * (N_T // 2) + 4 * PAIRS + g // 2)
                    for t in range(QT):
                        ins = pe.transpose(t_bank[g % 2][:, t * P:(t + 1) * P], probs[:, t, g * P:(g + 1) * P],
                                           ident[:, :])
                    ins.then_inc(t_full, 1)
                pe.wait_ge(pt_act, b * (N_T // 2) + N_T // 2)
                pe.wait_ge(pt_dve, b * (N_T // 2) + N_T // 2)
                output(1, b, lambda g, ts: probsT[:, g, ts],
                       lambda g: vw[:, bass.ds(b, 1), g, :].rearrange("p b d -> p (b d)"), CG)
                turn_norm(b, 2)
                pe.wait_ge(h_lo_made, b * 3 + 3)
                for i in range(FC):
                    project(("gate", i), "f", i if L.rope else FC + i, b)
                    if not L.rope:
                        project(("up", i), "f", i, b)
                if L.rope:
                    pe.wait_ge(gelu_made, b * FC + FC)
                else:
                    pe.wait_ge(hid_made, b * FC + FC)
                output(2, b, lambda g, ts: oT[:, g, ts], lambda g: f2[:, g, :], FC)

        @block.scalar
        def _(act):
            def norm_root(b, n):
                act.wait_ge(ln_step, (b * 3 + n) * LN_STEPS + 1)
                act.activation(log_var[:, :], mv[:, :, 1], ACT.Ln, bias=EPS).then_inc(log_made, 1)
                act.wait_ge(log_made, b * 3 + n + 1)
                act.activation(root[:, :], log_var[:, :], ACT.Exp, scale=-0.5).then_inc(root_made, 1)

            def norm_hi(b, n):
                norm_root(b, n)
                act.wait_ge(h_full, b * 3 + n + 1)
                act.copy(h_hi[:, :], h_f[:, :]).then_inc(h_hi_made, 1)

            def qk_highs(c, part, b):
                if part == 0 and c >= 2:
                    act.wait_ge(s_full, b * N_S + (c - 1) * TILES)
                if L.rope:
                    act.wait_ge(rope_add, b * L.n_add + 2 * c + part + 1)
                    src_t = e["rot_a"][:, part, :]
                else:
                    act.wait_ge(pj_full, filled((("q", "k")[part], c), b))
                    src_t = pj((("q", "k")[part], c))[:, :]
                if part == 0:
                    if L.rope:
                        act.copy(q_hi[:, c % 2, :], src_t).then_inc(qk_hi, 1)
                    else:
                        act.mul(q_hi[:, c % 2, :], src_t, SCALE).then_inc(qk_hi, 1)
                else:
                    for head in range(2):
                        r = slice(DH * head, DH * head + DH)
                        act.copy(k_hi[r, c % 2, head, :], src_t[r, :]).then_inc(qk_hi, 1)

            def exps(n, b, c):
                if n >= P_SLOTS:
                    old = n - P_SLOTS
                    act.wait_ge(t_full, b * N_T + old // TILES * TILES + old % TILES // QT * KT + KT)
                if n % TILES == 0 and c >= 2:
                    act.wait_ge(recip_made, b * PAIRS + c - 1)
                act.wait_ge(max_made, b * PAIRS * TILES + n + 1)
                act.activation(probs[:, n % P_SLOTS, :], s_bank[n % S_BANKS][:, :], ACT.Exp,
                               bias=negmax[:, n % NM:n % NM + 1],
                               accum_out=sums[:, c % 2, n % TILES:n % TILES + 1]).then_inc(exp_made, 1)

            with act.Fori(0, B) as b:
                norm_hi(b, 0)
                for j in range(0, 2 * KT, 2):
                    act.wait_ge(pj_full, filled(("v", j), b))
                    act.copy(v_sb[:, j // 2, 0:N], pj(("v", j))[:, :]).then_inc(v_act, 1)
                qk_highs(0, 0, b)
                qk_highs(0, 1, b)
                for c in STEPS:
                    for s in range(TILES):
                        if c < PAIRS:
                            exps(c * TILES + s, b, c)
                        if 1 <= c <= PAIRS and s % 2 == 0:
                            p = c - 1
                            act.wait_ge(t_full, b * N_T + p * TILES + s + 1)
                            if p:
                                act.wait_ge(av_done, b * N_AV + KT * (p - 1) + s % KT + 1)
                            act.copy(probsT[:, s, :], t_bank[0][:, :]).then_inc(pt_act, 1)
                        if c + 1 < PAIRS:
                            if s == (5 if L.rope else 2):
                                qk_highs(c + 1, 0, b)
                            if s == (7 if L.rope else 4):
                                qk_highs(c + 1, 1, b)
                        if 1 <= c <= PAIRS and s == 6:
                            act.wait_ge(pj_full, filled(("r", c - 1), b))
                            if c > 1:
                                act.wait_ge(o_made, b * PAIRS + c - 1)
                            act.copy(r_sb[:, :], pj(("r", c - 1))[:, :]).then_inc(r_made, 1)
                norm_hi(b, 1)
                for t in range(QT):
                    act.wait_ge(c_sub, b * QT + t + 1)
                    act.activation(probs[:, t, :], probs[:, t, :], ACT.Exp).then_inc(exp_made, 1)
                for g in range(0, CG, 2):
                    act.wait_ge(t_full, b * N_T + PAIRS * TILES + g + 1)
                    if g == 0:
                        act.wait_ge(av_done, b * N_AV + N_AV)
                    act.copy(probsT[:, g, :], t_bank[0][:, :]).then_inc(pt_act, 1)
                norm_hi(b, 2)
                for i in range(FC):
                    act.wait_ge(pj_full, filled(("gate", i), b))
                    out = oT[:, i, :] if L.rope else oT[:, FC + i, :]
                    col = 8 + i if L.rope else 6 + FC + i
                    act.activation(out, pj(("gate", i))[:, :], ACT.Gelu, bias=cols[:, col:col + 1]).then_inc(gelu_made, 1)

        @block.vector
        def _(dve):
            def norm(b, n):
                x = x_sb if n == 0 else x_new
                if n == 0:
                    dve.wait_ge(x_loaded, b * 16 + 16)
                else:
                    dve.wait_ge(added, b * 3 + n)
                for t in range(QT):
                    ins = dve.bn_stats(stats[:, t, :], x[:, t, :])
                at = (b * 3 + n) * LN_STEPS
                dve.drain()
                for t in range(QT):
                    ins = dve.bn_aggr(mv[:, t, :], stats[:, t, :])
                ins.then_inc(ln_step, 1)
                dve.wait_ge(root_made, b * 3 + n + 1)
                dve.tensor_tensor(sq[:, :], root[:, :], root[:, :], ALU.mult).then_inc(ln_step, 1)
                dve.wait_ge(ln_step, at + 2)
                dve.scalar_tensor_tensor(out=sq[:, :], in0=mv[:, :, 1], scalar=EPS, in1=sq[:, :],
                                         op0=ALU.add, op1=ALU.mult).then_inc(ln_step, 1)
                dve.wait_ge(ln_step, at + 3)
                dve.tensor_scalar(sq[:, :], sq[:, :], -0.5, 1.5, ALU.mult, ALU.add).then_inc(ln_step, 1)
                dve.wait_ge(ln_step, at + 4)
                dve.tensor_tensor(rstd[:, :], root[:, :], sq[:, :], ALU.mult).then_inc(ln_step, 1)
                dve.wait_ge(ln_step, at + 5)
                for t in range(QT):
                    ins = dve.tensor_scalar(xn[:, t, :], x[:, t, :], mv[:, t, 0:1], rstd[:, t:t + 1],
                                            ALU.subtract, ALU.mult)
                ins.then_inc(xn_made, 1)
                dve.wait_ge(pj_full, filled(("h", n), b))
                dve.tensor_scalar(h_f[:, :], pj(("h", n))[:, :], vec_b[:, 2 * n:2 * n + 1], vec_b[:, 2 * n + 1:2 * n + 2],
                                  ALU.mult, ALU.add).then_inc(h_full, 1)
                dve.wait_ge(h_hi_made, b * 3 + n + 1)
                dve.wait_ge(h_full, b * 3 + n + 1)
                dve.tensor_tensor(h_lo[:, :], h_f[:, :], h_hi[:, :].bitcast(F32), ALU.subtract).then_inc(h_lo_made, 1)

            def rotate(j, kind, c, b):
                swapped = kind.endswith("s")
                dve.wait_ge(pj_full, filled((kind, c), b))
                if j >= 2 * PAIRS:
                    dve.wait_ge(rope_add, b * L.n_add + j - 1)
                out = e["rot_b" if swapped else "rot_a"][:, j % 2, :]
                cs = e["rope_cs"][:, int(swapped), :]
                dve.scalar_tensor_tensor(out=out, in0=pj((kind, c))[:, :], scalar=1.0 if kind[0] == "k" else SCALE,
                                         in1=cs, op0=ALU.mult, op1=ALU.mult).then_inc(rope_mul, 1)

            def q_low(c, b):
                dve.wait_ge(qk_hi, b * N_QK + 3 * c + 1)
                hi = q_hi[:, c % 2, :].bitcast(F32)
                if L.rope:
                    dve.tensor_tensor(q_lo[:, c % 2, :], e["rot_a"][:, 0, :], hi, ALU.subtract).then_inc(qk_lo, 1)
                else:
                    dve.scalar_tensor_tensor(out=q_lo[:, c % 2, :], in0=pj(("q", c))[:, :], scalar=SCALE, in1=hi,
                                             op0=ALU.mult, op1=ALU.subtract).then_inc(qk_lo, 1)

            def k_low(c, b):
                dve.wait_ge(qk_hi, b * N_QK + 3 * c + 3)
                full = e["rot_a"][:, 1, :] if L.rope else pj(("k", c))[:, :]
                for head in range(2):
                    r = slice(DH * head, DH * head + DH)
                    dve.tensor_tensor(k_lo[r, c % 2, head, :], full[r, :], k_hi[r, c % 2, head, :].bitcast(F32),
                                      ALU.subtract).then_inc(qk_lo, 1)

            def add_residual(n, b):
                x = x_sb if n == 0 else x_new
                dve.wait_ge(pj_full, filled(("out", n), b))
                dve.wait_ge(biased, b * 3 + n + 1)
                if n == 0:
                    dve.wait_ge(x_new_free, b * 16 + 16)
                dve.tensor_tensor(x_new[:, :, :], pj(("out", n))[:, :].rearrange("p (t d) -> p t d", d=D), x[:, :, :],
                                  ALU.add).then_inc(added, 1)

            with dve.Fori(0, B) as b:
                dve.tensor_copy(vec_b[:, :], vecs[:, bass.ds(b, 1), :].rearrange("p b n -> p (b n)"))
                norm(b, 0)
                for j in range(1, 2 * KT, 2):
                    dve.wait_ge(pj_full, filled(("v", j), b))
                    dve.tensor_copy(v_sb[:, j // 2, N:2 * N], pj(("v", j))[:, :]).then_inc(v_dve, 1)
                if L.rope:
                    for i, kind in enumerate(L.qk_kinds()):
                        rotate(i // 2, kind, 0, b)
                q_low(0, b)
                k_low(0, b)
                if L.rope:
                    kd = e["k_diag"][:, :, :].rearrange("p (g o) n -> p g o n", o=2)
                    kc = e["kc"][:, :, bass.ds(b * J, J)].rearrange("p (g o) n -> p g o n", o=2)
                    for half in range(2):
                        r = slice(DH * half, DH * half + DH)
                        for o in range(2):
                            at = 2 * J * o + J * half
                            dve.tensor_copy(kd[r, :, o, at:at + J], kc[r, :, o, :]).then_inc(diag_made, 1)
                for c in STEPS:
                    for s in range(TILES):
                        if c < PAIRS:
                            n = c * TILES + s
                            dve.wait_ge(s_full, b * N_S + n + 1)
                            dve.tensor_reduce(negmax[:, n % NM:n % NM + 1], s_bank[n % S_BANKS][:, :], AX_X, ALU.max,
                                              negate=True).then_inc(max_made, 1)
                        if 1 <= c <= PAIRS and s == 1:
                            dve.wait_ge(exp_made, b * N_S + c * TILES)
                            if c > 1:
                                dve.wait_ge(r_in_made, b * PAIRS + c - 1)
                            dve.reciprocal(recips[:, :], sums[:, (c - 1) % 2, :]).then_inc(recip_made, 1)
                        if 1 <= c <= PAIRS and s % 2 == 1:
                            p = c - 1
                            dve.wait_ge(t_full, b * N_T + p * TILES + s + 1)
                            if p:
                                dve.wait_ge(av_done, b * N_AV + KT * (p - 1) + s % KT + 1)
                            dve.tensor_copy(probsT[:, s, :], t_bank[1][:, :]).then_inc(pt_dve, 1)
                        if c + 1 < PAIRS:
                            if L.rope:
                                if 2 <= s <= 5:
                                    i = s - 2
                                    rotate(2 * c + 2 + i // 2, L.qk_kinds()[i], c + 1, b)
                                if s == 6:
                                    q_low(c + 1, b)
                                if s == 7:
                                    k_low(c + 1, b)
                            else:
                                if s == 2:
                                    q_low(c + 1, b)
                                if s == 4:
                                    k_low(c + 1, b)
                        if c >= 2 and s == 2:
                            p = c - 2
                            dve.wait_ge(av_done, b * N_AV + KT * p + KT)
                            dve.wait_ge(r_made, b * PAIRS + p + 1)
                            dve.tensor_tensor(oT[:, p, :], o_bank[:, :], r_sb[:, :], ALU.mult).then_inc(o_made, 1)
                add_residual(0, b)
                norm(b, 1)
                if L.rope:
                    for c in range(PAIRS):
                        rotate(2 * PAIRS + c, "cq", c, b)
                        rotate(2 * PAIRS + c, "cqs", c, b)
                for t in range(QT):
                    n = PAIRS * TILES + t
                    sv = s_bank[n % S_BANKS][:, :].rearrange("p (h k) -> p h k", k=J)
                    dve.wait_ge(s_full, b * N_S + n + 1)
                    dve.tensor_reduce(c_negmax[:, t, :], sv, AX_X, ALU.max, negate=True).then_inc(c_max, 1)
                    dve.wait_ge(c_max, b * QT + t + 1)
                    dve.tensor_tensor(probs[:, t, :].rearrange("p (h k) -> p h k", k=J), sv,
                                      c_negmax[:, t, :].unsqueeze(2).broadcast_to([P, H, J]),
                                      ALU.add).then_inc(c_sub, 1)
                for t in range(QT):
                    dve.wait_ge(exp_made, b * N_S + PAIRS * TILES + t + 1)
                    dve.tensor_reduce(c_sum[:, t, :], probs[:, t, :].rearrange("p (h k) -> p h k", k=J), AX_X,
                                      ALU.add).then_inc(c_summed, 1)
                    dve.wait_ge(c_summed, b * QT + t + 1)
                    dve.reciprocal(c_recip[:, t, :], c_sum[:, t, :]).then_inc(c_inv, 1)
                for g in range(1, CG, 2):
                    dve.wait_ge(t_full, b * N_T + PAIRS * TILES + g + 1)
                    dve.tensor_copy(probsT[:, g, :], t_bank[1][:, :]).then_inc(pt_dve, 1)
                add_residual(1, b)
                norm(b, 2)
                if not L.rope:
                    for i in range(FC):
                        dve.wait_ge(pj_full, filled(("up", i), b))
                        dve.wait_ge(gelu_made, b * FC + i + 1)
                        dve.scalar_tensor_tensor(out=oT[:, i, :], in0=pj(("up", i))[:, :], scalar=cols[:, 6 + i:7 + i],
                                                 in1=oT[:, FC + i, :], op0=ALU.add, op1=ALU.mult).then_inc(hid_made, 1)
                add_residual(2, b)


def rope_tables():
    inv = (1.0 / np.float32(10000.0) ** (np.arange(0, DH, 2, dtype=np.float32) / np.float32(DH))).astype(np.float32)
    ang = np.arange(N, dtype=np.float32)[None, :] * inv[:, None]
    cos, sin = (np.repeat(f(ang).astype(np.float32), 2, axis=0) for f in (np.cos, np.sin))
    sin[0::2] *= -1
    return np.ascontiguousarray(np.concatenate([np.tile(cos, (2, 1)), np.tile(sin, (2, 1))], axis=1))


def kernel(**inputs):
    import numpy as _np
    import concourse.bacc as _bacc
    from concourse.bass_utils import run_bass_kernel_spmd as _run

    w = {k: _np.asarray(v) for k, v in inputs.items()}

    def l0(n):
        return w[f"L0_xcond_{n}"]

    def l1(n):
        return w[f"L1_xcond_{n}"]

    def stack(m):
        return m.reshape(-1, P, m.shape[1]).transpose(1, 0, 2).reshape(P, -1)

    def columns(*vs):
        return _np.concatenate([v.reshape(-1, P).T for v in vs], axis=1)

    arrays = {
        "x": w["x"],
        "ctx": w["ctx_768"].reshape(B * J, CD),
        "cond": w["cond_1024"].T,
        "tables": rope_tables(),
        "w128_0": _np.concatenate([
            l0("sa_wq"), l0("sa_wkv"), l0("ca_wq"), l0("ff_w1"),
            l0("g1_w"), l0("b1_w"), l0("g2_w"), l0("b2_w"), stack(l0("ca_wo")),
            stack(l0("sa_wo")), stack(l0("ff_w2"))], axis=1),
        "w128_1": _np.concatenate([
            l1("q1"), l1("k1"), l1("v1"), l1("ff_w1"),
            l1("n1_w"), l1("n2_w"), l1("n3_w"), stack(l1("o2_w")), l1("q2"),
            stack(l1("o1_w")), stack(l1("ff_w2"))], axis=1),
        "w96_0": l0("ca_wkv"),
        "w96_1": _np.concatenate([l1("k2"), l1("v2")], axis=1),
        "cols_0": columns(l0("ln1_w"), l0("ln1_b"), l0("g1_b"), l0("b1_b"),
                          l0("ln2_w"), l0("ln2_b"), l0("g2_b"), l0("b2_b"), l0("ff_b1")),
        "cols_1": columns(l1("n1_b"), l1("n2_b"), l1("n3_b"), l1("ff_b1")),
        "rows_0": _np.concatenate([l0("sa_bo"), l0("ca_bo"), l0("ff_b2"), l0("ca_lnc_w"), l0("ca_lnc_b")])[None],
        "rows_1": _np.concatenate([l1("o1_b"), l1("o2_b"), l1("ff_b2")])[None],
    }
    arrays = {k: _np.ascontiguousarray(v) for k, v in arrays.items()}
    nc = _bacc.Bacc("TRN2", target_bir_lowering=False, num_devices=1)
    ap = {k: nc.dram_tensor(k, v.shape, F32, kind="ExternalInput").ap() for k, v in arrays.items()}
    mid = nc.dram_tensor("x_mid", (B, N, D), F32, kind="Internal").ap()
    out = nc.dram_tensor("out", (B, N, D), F32, kind="ExternalOutput").ap()
    build(nc, ap["x"], mid, out, ap["ctx"], ap["cond"], ap["tables"], (ap["w128_0"], ap["w128_1"]),
          (ap["w96_0"], ap["w96_1"]), (ap["cols_0"], ap["cols_1"]), (ap["rows_0"], ap["rows_1"]))
    r = _run(nc, [arrays], core_ids=[0])
    return r.results[0]["out"]
```

```python
from contextlib import ExitStack

import numpy as np

import concourse.bass as bass
from concourse import mybir

F32 = mybir.dt.float32
F32R = mybir.dt.float32r
ALU = mybir.AluOpType
ACT = mybir.ActivationFunctionType
AX_X = mybir.AxisListType.X

B, N, D = 4, 512, 128
H, DH = 16, 64
J, CD = 32, 96
P = 128
QT = N // P
KT = N // P
MID = H * DH
PAIRS = H // 2
FC = 4
TILES = 2 * QT
CG = H * J // P
SCALE = float(DH) ** -0.5
EPS = 1e-5

S_BANKS = 2
P_SLOTS = 12
NM = 16

SPLIT = ([("q", MID), ("k", MID), ("v", MID), ("cq", MID), ("f", FC * P)],
         [("q", MID), ("k", MID), ("v", MID), ("f", 2 * FC * P)])
SETUP = ([("ada", 4 * D), ("co", PAIRS * D)],
         [("ada", 6 * D), ("co", PAIRS * D), ("cq", MID)])
KEEP = [("wo", PAIRS * D), ("f2", FC * D)]
CTXW = [("ck", MID), ("cv", MID)]
N_COLS = (8 + FC, 6 + 2 * FC)
N_ROWS = (3 * D + 2 * CD, 3 * D)


def spans(parts):
    out, at = {}, 0
    for name, n in parts:
        out[name] = (at, n)
        at += n
    return out, at


START = -8
PAIR_STEPS = TILES
TIMES = {
    True: (
        {
            "s": (0.05, 1.05, 2.2, 3.05, 4.05, 5.05, 6.05, 6.25),
            "max": (0.05, 1.1, 2.05, 3.05, 4.05, 5.05, 6.05, 7.05),
            "exp": (0.6, 2.8, 2.9, 3.6, 4.9, 5.6, 6.3, 7.6),
            "t": (5.05, 6.05, 7.05, 8.05, 9.05, 10.05, 11.05, 12.05),
            "t_copy": (5.15, 6.2, 7.2, 8.2, 9.2, 10.2, 11.2, 12.2),
            "av": (10.85, 12.35, 12.55, 13.55),
            "recip": (9.8,),
            "r": (12.2,),
            "o": (14,),
            "q": (-7.5,),
            "rot_q": (-7.55,),
            "k": (-5.85,),
            "rot_k": (-5.5,),
            "hi_q": (-3.8,),
            "lo_q": (-2.6,),
            "hi_k": (-3.4, -2.4),
            "lo_k": (-1.9, -0.6),
        },
        {
            "q": (-4.85,),
            "rot_q": (-4.35,),
            "k": (-3.65,),
            "rot_k": (-3.15,),
            "hi_q": (-3.8,),
            "lo_q": (-1.9,),
            "hi_k": (-1.9, -0.6),
            "lo_k": (-1, -0.4),
        },
        {
            "norm": (-7.14,),
            "turn": (-5.15,),
            "v": (-0.4, 2.6, 3.1, 9.1, 11.55, 12.6, 13.6, 19.6),
            "bias": (13.2,),
        },
        {
            "load": (-5.1,),
            "out": (6.45, 7.65, 8.65, 9.35),
            "res": (10.45, 36.5, 53),
            "norm": (None, 11.05, 36.9),
            "turn": (None, 14.95, 41.4),
            "bias": (None, 14.55, 41.4),
            "cq": (15.65, 17.4, 19.65, 20.8, 23.65, 23.7, 26.85, 27.8),
            "rot_cq": (16.2, 17.05, 20.05, 21, 23.25, 24.3, 27.25, 28.25),
            "cs": (19.9, 23.9, 27.15, 31.1),
            "cmax": (20.21, 24.06, 27.41, 31.41),
            "cexp": (21.2, 24.9, 28.9, 32.9),
            "csum": (22.25, 25.4, 29.55, 33.4),
            "ct": (24.7, 27.4, 31.9, 34.2),
            "ct_copy": (23.85, 27.8, 33, 34.6),
            "cout": (25.25, 29.35, 33.25, 36.05),
            "gate": (43.7, 44.17, 44.19, 44.71),
            "fout": (45.5, 46.5, 48.05, 48.55),
        },
    ),
    False: (
        {
            "s": (0.3, 1, 2, 3.15, 4, 5, 6, 7),
            "max": (0.05, 1.05, 2.05, 3.05, 4.05, 5.05, 6.05, 7.05),
            "exp": (0.55, 2, 2.85, 3.7, 4.85, 5.8, 6.8, 7.85),
            "t": (5.15, 6, 7.15, 8.15, 9.15, 9.65, 11.15, 12.1),
            "t_copy": (5.3, 6.3, 7.3, 8.3, 9.3, 10.15, 11.3, 12),
            "av": (10.6, 11.3, 12.6, 13.45),
            "recip": (9.35,),
            "r": (11.25,),
            "o": (13.85,),
            "q": (-7.55,),
            "hi_q": (-6.8,),
            "lo_q": (-6.3,),
            "k": (-5.15,),
            "hi_k": (-5.25, -5.1),
            "lo_k": (-4.75, -4.15),
        },
        {
            "q": (-4.05,),
            "hi_q": (-4.25,),
            "lo_q": (-3.7,),
            "k": (-3.85,),
            "hi_k": (-4.2, -3.65),
            "lo_k": (-2.2, -1.45),
        },
        {
            "norm": (-7.99,),
            "turn": (-6.25,),
            "v": (2.25, 5.3, 6.3, 8.3, 14.3, 15.3, 16.2, 22.3),
            "bias": (20.3,),
        },
        {
            "out": (7.85, 8.2, 9.35, 9.85),
            "res": (10.75, 31.15, 47.2),
            "norm": (None, 10.9, 32.15),
            "turn": (None, 14.75, 36.1),
            "bias": (None, 12.6, 34.4),
            "cs": (15.55, 17.3, 21.65, 24.65),
            "cmax": (15.51, 18.51, 21.66, 24.66),
            "cexp": (16.5, 19.7, 23.45, 25.6),
            "csum": (17.1, 20.7, 23.7, 26.6),
            "ct": (19.65, 22.65, 25.6, 28.6),
            "ct_copy": (19.7, 22.7, 25.6, 28.65),
            "cout": (21.65, 24.65, 28.4, 30.6),
            "gate": (39.15, 39.17, 39.19, 41.71),
            "up": (39.61, 39.63, 39.65, 42.32),
            "fout": (41.7, 42.4, 44.7, 46.7),
        },
    ),
}
EVACUATE = "aaaaaaaa"
SLOT_GROUP = [g % 3 for g in range(H - 1)] + [1]
CHAIN = 12


def shape(variant):
    return variant != "last", variant != "first"


def make_plan(rope, variant):
    own, prev = shape(variant)
    steps = []

    def add(t, *step):
        steps.append((t, len(steps), step))

    pair, first_pair, entry, rest = TIMES[rope]
    for p in range(-3, PAIRS):
        for name, times in pair.items():
            if p == 0:
                times = first_pair.get(name, times)
            for i, t in enumerate(times):
                t += PAIR_STEPS * p
                if START <= t < START + PAIR_STEPS * PAIRS and (own if p >= 0 else prev):
                    add(t, name, p, *([i] if len(times) > 1 else []))
    for there, steps_of in ((own, entry), (prev, rest)):
        for name, times in steps_of.items():
            for i, t in enumerate(times):
                if there and t is not None:
                    add(t, name, i)
    return [step for _, _, step in sorted(steps)]


def evacuator(step):
    if step[0].startswith("t"):
        return EVACUATE[step[2]]
    return "av"[step[1] % 2]


SIGNALS = {
    "pj_full": lambda s: s[0] in ("turn", "v", "q", "k", "r", "cq", "gate", "up"),
    "acc_full": lambda s: (s[0] == "out" and s[1] == QT - 1) or (s[0] == "cout" and s[1] == QT - 1)
    or (s[0] == "fout" and s[1] == FC - 1),
    "chain": lambda s: CHAIN * (s[0] == "norm"),
    "xn_made": lambda s: s[0] == "norm",
    "h_full": lambda s: s[0] == "turn",
    "h_hi_made": lambda s: s[0] == "turn",
    "h_lo_made": lambda s: s[0] == "turn",
    "v_act": lambda s: s[0] == "v" and s[1] % 2 == 0,
    "v_dve": lambda s: s[0] == "v" and s[1] % 2 == 1,
    "shuffled": lambda s: s[0] == "rot_cq",
    "sin_mul": lambda s: s[0] in ("rot_q", "rot_k"),
    "rope_mul": lambda s: s[0].startswith("rot"),
    "rope_add": lambda s: s[0].startswith("rot"),
    "qk_hi": lambda s: s[0] in ("hi_q", "hi_k"),
    "qk_lo": lambda s: s[0] in ("lo_q", "lo_k"),
    "s_full": lambda s: s[0] in ("s", "cs"),
    "max_made": lambda s: s[0] == "max",
    "exp_made": lambda s: s[0] == "exp",
    "t_full": lambda s: s[0] in ("t", "ct"),
    "pt_act": lambda s: s[0] in ("t_copy", "ct_copy") and evacuator(s) == "a",
    "pt_dve": lambda s: s[0] in ("t_copy", "ct_copy") and evacuator(s) == "v",
    "recip_made": lambda s: s[0] == "recip",
    "r_in_made": lambda s: s[0] == "recip",
    "r_made": lambda s: s[0] == "r",
    "av_done": lambda s: s[0] == "av",
    "o_made": lambda s: s[0] == "o",
    "added": lambda s: s[0] == "res",
    "bias0_made": lambda s: s == ("bias", 0),
    "biased": lambda s: s[0] == "bias" and s[1] > 0,
    "diag_made": lambda s: 4 * (s[0] == "load"),
    "c_max": lambda s: s[0] == "cmax",
    "c_sub": lambda s: s[0] == "cmax",
    "c_exp": lambda s: s[0] == "cexp",
    "c_summed": lambda s: s[0] == "csum",
    "c_inv": lambda s: s[0] == "csum",
    "c_norm": lambda s: s[0] == "csum",
    "c_done": lambda s: s[0] == "cout" and s[1] < QT - 1,
    "gelu_made": lambda s: s[0] == "gate",
    "hid_made": lambda s: s[0] == "up",
}


class Pass:

    def __init__(self, plans, variant, b):
        self.plan, self.b, self.variant, self.plans = plans[variant], b, variant, plans
        self.own, self.prev = shape(variant)
        self.per_pass = {}
        for name, count in SIGNALS.items():
            first, full = (sum(int(count(s)) for s in plans[v]) for v in ("first", "full"))
            self.per_pass[name] = (first, full)

    def before(self, name):
        first, full = self.per_pass[name]
        if self.variant == "first":
            return 0
        return (self.b - 1) * full + first

    def at(self, name, *step):
        if step not in self.plan:
            assert self.has(*step) and self.per_pass[name][0] > 0, step
            return self.before(name)
        n = sum(int(SIGNALS[name](s)) for s in self.plan[:self.plan.index(step) + 1])
        return self.before(name) + n

    def has(self, *step):
        return step in self.plan or (self.prev and step[1] < 0)

    def ring(self, kinds, step):
        these, first, full = ([s for s in plan if s[0] in kinds]
                              for plan in (self.plan, self.plans["first"], self.plans["full"]))
        shift = (len(full) - len(first)) % 2 if self.variant == "first" else 0
        i = these.index(step)
        buffer = (i + shift) % 2
        if i >= 2:
            return buffer, these[i - 2]
        if not self.prev:
            return buffer, None
        assert first[-2:] == full[-2:]
        old = full[-1] if (len(full) - 1) % 2 == buffer else full[-2]
        return buffer, (old[0], old[1] - PAIRS) + old[2:]


PJ_KINDS = ("turn", "v", "q", "k", "r", "cq", "gate", "up")
ROTATIONS = ("rot_q", "rot_k", "rot_cq")


def build(nc, x_in, x_mid, x_out, ctx_in, cond_in, tables, w128, w96, colp, rowp):
    with ExitStack() as top:
        def sb(name, shape, dt=F32, stack=top):
            return stack.enter_context(nc.sbuf_tensor(name, shape, dt))

        ident = sb("ident", [P, P])
        arena = sb("arena", [P, 20, N])
        probs = arena[:, 0:P_SLOTS, :]
        probsT = arena[:, P_SLOTS:P_SLOTS + 8, :]
        raw = arena[:, :, :].rearrange("p a n -> p (a n)")
        v_sb = sb("v_sb", [P, KT, MID])
        oT = sb("oT", [P, PAIRS, N])
        h_f = sb("h_f", [P, N])
        xn = h_f[:, :].rearrange("p (t d) -> p t d", t=QT)
        h_hi = sb("h_hi", [P, N], F32R)
        h_lo = sb("h_lo", [P, N], F32R)
        q_hi = sb("q_hi", [P, 2, N], F32R)
        q_lo = sb("q_lo", [P, 2, N], F32R)
        k_hi = sb("k_hi", [P, 2, 2, N], F32R)
        k_lo = sb("k_lo", [P, 2, 2, N], F32R)
        x_sb = sb("x_sb", [P, QT, D])
        x_new = sb("x_new", [P, QT, D])
        x_res = sb("x_res", [P, QT, D])
        h2_f = sb("h2_f", [P, N])
        xn2 = h2_f[:, :].rearrange("p (t d) -> p t d", t=QT)
        h2_hi = sb("h2_hi", [P, N], F32R)
        h2_lo = sb("h2_lo", [P, N], F32R)
        c_probs = sb("c_probs", [P, 2, N])
        c_probsT = sb("c_probsT", [P, 2, N])
        r_in = sb("r_in", [P, QT, 2, DH])
        r_sb = sb("r_sb", [P, N])
        condT = sb("condT", [P, B])
        stats = sb("stats", [P, QT, 6])
        mv = sb("mv", [P, QT, 2])
        rstd = sb("rstd", [P, QT])
        var_eps = sb("var_eps", [P, QT])
        half_var = sb("half_var", [P, QT])
        sq = sb("sq", [P, QT])
        negmax = sb("negmax", [P, NM])
        sums = sb("sums", [P, 2, TILES])
        recips = sb("recips", [P, TILES])
        c_negmax = sb("c_negmax", [P, QT, H])
        c_sum = sb("c_sum", [P, QT, H])
        c_recip = sb("c_recip", [P, QT, H])
        vec_own = sb("vec_own", [P, 2])
        vec_prev = sb("vec_prev", [P, 4])
        ones = sb("ones", [P, 1])

        def bank(name):
            return top.enter_context(nc.psum_tensor(name, [P, N], F32))

        s_bank = [bank(f"s_bank{i}") for i in range(S_BANKS)]
        acc_bank = bank("acc_bank")
        t_bank = [bank(f"t_bank{i}") for i in range(2)]
        pj_bank = [bank(f"pj_bank{i}") for i in range(2)]
        o_bank = bank("o_bank")

        for li in range(2):
            with ExitStack() as lay:
                rope = li == 0

                def lsb(name, shape, dt=F32):
                    return sb(f"l{li}_{name}", shape, dt, lay)

                w_hi = {n: lsb(f"{n}_hi", [P, c], F32R) for n, c in SPLIT[li]}
                w_lo = {n: lsb(f"{n}_lo", [P, c], F32R) for n, c in SPLIT[li]}
                wo = lsb("wo", [P, PAIRS, D])
                f2 = lsb("f2", [P, FC, D])
                cols = lsb("cols", [P, N_COLS[li]])
                bias_rows = lsb("bias_rows", [P, 3, D])
                vecs = lsb("vecs", [P, B, 6])
                vw = lsb("vw", [P, B, CG, D])
                env = dict(locals())
                env.pop("env", None)
                if rope:
                    env["rope_cs"] = lsb("rope_cs", [P, 2, N])
                    env["rot_a"] = lsb("rot_a", [P, 2, N])
                    env["rot_b"] = lsb("rot_b", [P, 2, N])
                    env["cqT"] = lsb("cqT", [P, 2, N])
                    env["kc"] = lsb("kc", [P, PAIRS, B * J])
                    env["k_diag"] = lsb("k_diag", [P, PAIRS, P])
                else:
                    env["cqT"] = lsb("cqT", [P, 4, N])
                    env["kw_hi"] = lsb("kw_hi", [P, B, H * J], F32R)
                    env["kw_lo"] = lsb("kw_lo", [P, B, H * J], F32R)
                src = (x_in, x_mid)[li]
                dst = (x_mid, x_out)[li]
                setup(nc, li, rope, env, ctx_in, cond_in, tables, w128[li], w96[li], colp[li], rowp[li])
                batch_loop(nc, li, rope, env, src, dst)


SWAP = [i ^ 1 for i in range(32)]


def inverse_root(dve, var, var_eps, half_var, sq, y, step, n):
    dve.wait_ge(step, n)
    dve.tensor_scalar(var_eps, var, EPS, None, ALU.add).then_inc(step, 1)
    dve.wait_ge(step, n + 1)
    dve.tensor_scalar(y.bitcast(mybir.dt.int32), var_eps.bitcast(mybir.dt.int32), -0.5, float(0x5F3759DF),
                      ALU.mult, ALU.add)
    dve.tensor_scalar(half_var, var_eps, -0.5, None, ALU.mult).then_inc(step, 1)
    for k in range(3):
        dve.wait_ge(step, n + 3 * k + 2)
        dve.tensor_tensor(sq, y, y, ALU.mult).then_inc(step, 1)
        dve.wait_ge(step, n + 3 * k + 3)
        dve.tensor_tensor(sq, sq, half_var, ALU.mult).then_inc(step, 1)
        dve.wait_ge(step, n + 3 * k + 4)
        dve.scalar_tensor_tensor(out=y, in0=sq, scalar=1.5, in1=y, op0=ALU.add, op1=ALU.mult).then_inc(step, 1)
    dve.wait_ge(step, n + CHAIN - 1)


def setup(nc, li, rope, e, ctx_in, cond_in, tables, w128, w96, colp, rowp):
    raw, ident, v_sb, oT, condT = e["raw"], e["ident"], e["v_sb"], e["oT"], e["condT"]
    w_hi, w_lo, wo, f2, cols, bias_rows = e["w_hi"], e["w_lo"], e["wo"], e["f2"], e["cols"], e["bias_rows"]
    vecs, vw = e["vecs"], e["vw"]
    s_bank, t_bank, pj_bank, o_bank = e["s_bank"], e["t_bank"], e["pj_bank"], e["o_bank"]
    acc_bank = e["acc_bank"]
    split_at, n_split = spans(SPLIT[li])
    setup_at, n_setup = spans(SETUP[li])
    keep_at, n_keep = spans(KEEP)
    ctx_at, n_ctx = spans(CTXW)

    def part(name):
        if name in split_at:
            a, n = split_at[name]
        elif name in setup_at:
            a, n = setup_at[name]
            a += n_split
        else:
            a, n = ctx_at[name]
            a += n_split + n_setup
        return raw[:, a:a + n]

    ctx_sb = v_sb[:, 0, 0:CD]
    ctx_n = v_sb[:, 0, P:P + CD]
    ctxT = v_sb[:, 0, 2 * P:3 * P]
    lnc = v_sb[:, 0, 3 * P:3 * P + 2 * CD]
    vcT = v_sb[:, 1, :].rearrange("p (c n) -> p c n", c=PAIRS)
    wqT = v_sb[:, 2, :].rearrange("p (c n) -> p c n", c=PAIRS)
    kT = e["kc"] if rope else v_sb[:, 3, :].rearrange("p (c n) -> p c n", c=PAIRS)
    kT2 = v_sb[:, 2, :].rearrange("p (c n) -> p c n", c=PAIRS)
    vw_rows = oT[:, 0:4, :].rearrange("p c (h d) -> p (c h) d", d=D)
    co = part("co").rearrange("p (c d) -> p c d", c=PAIRS)

    with ExitStack() as st:
        def sem(name):
            return st.enter_context(nc.semaphore(f"l{li}_{name}"))

        small_in, ctx_in_s, kv_in, setup_in, keep_in = (
            sem("small_in"), sem("ctx_in"), sem("kv_in"), sem("setup_in"), sem("keep_in"))
        w_in = {n: sem(f"w_in_{n}") for n, _ in SPLIT[li]}
        id_made = sem("id_made")
        hi_made, lo_made, swap_made = sem("hi_made"), sem("lo_made"), sem("swap_made")
        ctx_step, ctx_ready = sem("ctx_step"), sem("ctx_ready")
        ctxT_full, ctxT_made = sem("ctxT_full"), sem("ctxT_made")
        ada_full, ada_step = sem("ada_full"), sem("ada_step")
        kT_full, vT_full, wqT_full = sem("kT_full"), sem("vT_full"), sem("wqT_full")
        kT_step, vT_made, wqT_made = sem("kT_step"), sem("vT_made"), sem("wqT_made")
        vw_full, vw_made, vw_moved = sem("vw_full"), sem("vw_made"), sem("vw_moved")
        kw_full, kw_hi_made, kw_lo_made = sem("kw_full"), sem("kw_hi_made"), sem("kw_lo_made")

        block = st.enter_context(nc.Block())

        @block.sync
        def _(sp):
            sp.dma_start(ctx_sb, ctx_in).then_inc(ctx_in_s, 16)
            a = n_split + n_setup
            if rope:
                sp.dma_start(lnc, rowp[0:1, 3 * D:3 * D + 2 * CD].broadcast_to([P, 2 * CD])).then_inc(small_in, 16)
                sp.dma_start(e["rope_cs"][:, :, :], tables.rearrange("p (a n) -> p a n", a=2)).then_inc(small_in, 16)
            sp.dma_start(condT[:, :], cond_in).then_inc(small_in, 16)
            sp.dma_start(cols[:, :], colp).then_inc(small_in, 16)
            sp.dma_start(bias_rows[:, :, :].rearrange("p a d -> p (a d)"),
                         rowp[0:1, 0:3 * D].broadcast_to([P, 3 * D])).then_inc(small_in, 16)
            sp.dma_start(raw[0:CD, a:a + n_ctx], w96).then_inc(kv_in, 16)
            sp.dma_start(raw[:, n_split:a], w128[:, n_split:a]).then_inc(setup_in, 16)
            sp.dma_start(wo[:, :, :].rearrange("p c d -> p (c d)"), w128[:, a:a + PAIRS * D]).then_inc(keep_in, 16)
            sp.dma_start(f2[:, :, :].rearrange("p c d -> p (c d)"),
                         w128[:, a + PAIRS * D:a + n_keep]).then_inc(keep_in, 16)
            sp.wait_ge(vw_made, 4)
            for b in range(B):
                for r in range(P // J):
                    sp.dma_start(vw[r * J:(r + 1) * J, b, :, :],
                                 vw_rows[b * J:(b + 1) * J, :, :].rearrange(
                                     "p (g r) d -> p g r d", r=P // J)[:, :, r, :]).then_inc(vw_moved, 16)
            sp.wait_ge(vw_moved, 16 * B * (P // J))
            sp.wait_ge(keep_in, 32)
            sp.wait_ge(small_in, 16 * (5 if rope else 3))

        @block.gpsimd
        def _(pool):
            if li == 0:
                pool.memset(ident[:, :], 0.0).then_inc(id_made, 1)
                pool.wait_ge(id_made, 1)
                pool.affine_select(out=ident[:, :], in_=ident[:, :], compare_op=ALU.not_equal, fill=1.0,
                                   base=0, pattern=[[-1, P]], channel_multiplier=1).then_inc(id_made, 1)

        @block.scalar
        def _(act):
            for n, _ in SPLIT[li]:
                a, c = split_at[n]
                act.dma_start(raw[:, a:a + c], w128[:, a:a + c]).then_inc(w_in[n], 16)
            act.wait_ge(ctxT_full, 1)
            act.copy(ctxT[0:CD, :], o_bank[0:CD, 0:P]).then_inc(ctxT_made, 1)
            act.wait_ge(vT_full, 1)
            for i in range(2):
                act.copy(vcT[:, 4 * i:4 * i + 4, :].rearrange("p c n -> p (c n)"), s_bank[i][:, :]).then_inc(vT_made, 1)
            if not rope:
                act.wait_ge(kT_full, 1)
                for i in range(2):
                    act.copy(kT[:, 4 * i:4 * i + 4, :].rearrange("p c n -> p (c n)"),
                             pj_bank[i][:, :]).then_inc(kT_step, 1)
                act.wait_ge(wqT_full, 1)
                for i in range(2):
                    act.mul(wqT[:, 4 * i:4 * i + 4, :].rearrange("p c n -> p (c n)"),
                            t_bank[i][:, :], SCALE).then_inc(wqT_made, 1)
            for n, _ in SPLIT[li]:
                act.wait_ge(w_in[n], 16)
                act.copy(w_hi[n][:, :], part(n)).then_inc(hi_made, 1)
            act.wait_ge(vw_full, 1)
            for i, bk in enumerate((pj_bank[0], pj_bank[1], t_bank[0], t_bank[1])):
                odd, half = i // 2, i % 2
                act.copy(vw_rows[:, 8 * half:8 * half + 8, :].rearrange("p (j o) d -> p j o d", o=2)[:, :, odd, :],
                         bk[:, :].rearrange("p (j d) -> p j d", d=D)).then_inc(vw_made, 1)
            if not rope:
                act.wait_ge(kw_full, 1)
                for i, bk in enumerate((s_bank[0], s_bank[1], acc_bank, o_bank)):
                    odd, half = i // 2, i % 2
                    for j in range(4):
                        h = 8 * half + 2 * j + odd
                        ins = act.copy(e["kw_hi"][:, :, h * J:(h + 1) * J],
                                       bk[:, j * P:(j + 1) * P].rearrange("p (b k) -> p b k", b=B))
                    ins.then_inc(kw_hi_made, 1)

        @block.vector
        def _(dve):
            if li == 0:
                for t in (e["k_hi"], e["k_lo"]):
                    for half in range(2):
                        dve.memset(t[DH * half:DH * half + DH, :, 1 - half, :].bitcast(F32), 0.0)
                dve.memset(e["ones"][:, :], 1.0)
                dve.memset(e["k_diag"][:, :, :], 0.0)
            if rope:
                dve.wait_ge(ctx_in_s, 16)
                dve.bn_stats(e["stats"][:, 0, :], ctx_sb).then_inc(ctx_step, 1)
                dve.wait_ge(ctx_step, 1)
                dve.bn_aggr(e["mv"][:, 0, :], e["stats"][:, 0, :]).then_inc(ctx_step, 1)
                inverse_root(dve, e["mv"][:, 0, 1:2], e["var_eps"][:, 0:1], e["half_var"][:, 0:1], e["sq"][:, 0:1],
                             e["rstd"][:, 0:1], ctx_step, 2)
                dve.tensor_scalar(ctx_n, ctx_sb, e["mv"][:, 0, 0:1], e["rstd"][:, 0:1],
                                  ALU.subtract, ALU.mult).then_inc(ctx_step, 1)
                dve.wait_ge(ctx_step, CHAIN + 2)
                dve.wait_ge(small_in, 16 * 5)
                dve.tensor_tensor(ctx_n, ctx_n, lnc[:, 0:CD], ALU.mult).then_inc(ctx_step, 1)
                dve.wait_ge(ctx_step, CHAIN + 3)
                dve.tensor_tensor(ctx_n, ctx_n, lnc[:, CD:2 * CD], ALU.add).then_inc(ctx_ready, 1)
            dve.wait_ge(small_in, 16 * (5 if rope else 3))
            dve.wait_ge(ada_full, 1)
            A = acc_bank
            if rope:
                for m in range(2):
                    n = (0, 2)[m]
                    g, bt = A[:, 8 * m:8 * m + B], A[:, 8 * m + 4:8 * m + 4 + B]
                    lw, lb, gb, bb = (cols[:, 4 * m + i:4 * m + i + 1] for i in range(4))
                    sc, sh = vecs[:, :, 2 * n], vecs[:, :, 2 * n + 1]
                    dve.tensor_scalar(sc, g, gb, 1.0, ALU.add, ALU.add).then_inc(ada_step, 1)
                    dve.wait_ge(ada_step, 4 * m + 1)
                    dve.tensor_scalar(sh, sc, lb, bb, ALU.mult, ALU.add).then_inc(ada_step, 1)
                    dve.wait_ge(ada_step, 4 * m + 2)
                    dve.tensor_tensor(sh, sh, bt, ALU.add).then_inc(ada_step, 1)
                    dve.tensor_scalar(sc, sc, lw, None, ALU.mult).then_inc(ada_step, 1)
                    dve.wait_ge(ada_step, 4 * m + 4)
                dve.tensor_copy(vecs[:, :, 2:4], vecs[:, :, 0:2]).then_inc(ada_step, 1)
            else:
                for n in range(3):
                    dve.tensor_scalar(vecs[:, :, 2 * n], A[:, 8 * n:8 * n + B], cols[:, 2 * n:2 * n + 1], 1.0,
                                      ALU.add, ALU.add).then_inc(ada_step, 1)
                    dve.tensor_scalar(vecs[:, :, 2 * n + 1], A[:, 8 * n + 4:8 * n + 4 + B],
                                      cols[:, 2 * n + 1:2 * n + 2], None, ALU.add).then_inc(ada_step, 1)
            if rope:
                dve.wait_ge(kT_full, 1)
                cos, sin = (e["rope_cs"][:, i, 0:J].unsqueeze(1).broadcast_to([P, 4 * B, J]) for i in range(2))
                for i in range(2):
                    a = kT[:, 4 * i:4 * i + 4, :].rearrange("p c (b k) -> p (c b) k", k=J)
                    dve.tensor_tensor(a, pj_bank[i][:, :].rearrange("p (m k) -> p m k", k=J), cos,
                                      ALU.mult).then_inc(kT_step, 1)
                    dve.stream_shuffle(kT2[:, 4 * i:4 * i + 4, :].rearrange("p c n -> p (c n)"),
                                       pj_bank[i][:, :], SWAP).then_inc(kT_step, 1)
                for i in range(2):
                    b_ = kT2[:, 4 * i:4 * i + 4, :].rearrange("p c (b k) -> p (c b) k", k=J)
                    dve.wait_ge(kT_step, 4 + i)
                    dve.tensor_tensor(b_, b_, sin, ALU.mult).then_inc(kT_step, 1)
                dve.wait_ge(kT_step, 6)
                dve.tensor_tensor(kT[:, :, :], kT[:, :, :], kT2[:, :, :], ALU.add).then_inc(kT_step, 1)
                dve.wait_ge(kT_step, 7)
                dve.tensor_scalar(kT[:, :, :], kT[:, :, :], SCALE, None, ALU.mult).then_inc(kT_step, 1)
            for i, (n, _) in enumerate(SPLIT[li]):
                dve.wait_ge(hi_made, i + 1)
                dve.tensor_tensor(w_lo[n][:, :], part(n), w_hi[n][:, :].bitcast(F32), ALU.subtract).then_inc(lo_made, 1)
            if not rope:
                for i, bk in enumerate((s_bank[0], s_bank[1], acc_bank, o_bank)):
                    odd, half = i // 2, i % 2
                    dve.wait_ge(kw_hi_made, i + 1)
                    for j in range(4):
                        h = 8 * half + 2 * j + odd
                        ins = dve.tensor_tensor(e["kw_lo"][:, :, h * J:(h + 1) * J],
                                                bk[:, j * P:(j + 1) * P].rearrange("p (b k) -> p b k", b=B),
                                                e["kw_hi"][:, :, h * J:(h + 1) * J].bitcast(F32), ALU.subtract)
                    ins.then_inc(kw_lo_made, 1)

        @block.tensor
        def _(pe):
            if li == 0:
                pe.wait_ge(id_made, 2)
            if rope:
                pe.wait_ge(ctx_ready, 1)
            else:
                pe.wait_ge(ctx_in_s, 16)
            pe.transpose(o_bank[0:CD, 0:P], ctx_n if rope else ctx_sb, ident[:, :]).then_inc(ctxT_full, 1)
            pe.wait_ge(setup_in, 16)
            pe.wait_ge(small_in, 16 * (5 if rope else 3))
            ada = part("ada")
            for m in range(SETUP[li][0][1] // D):
                ins = pe.matmul(acc_bank[:, 4 * m:4 * m + B], ada[:, m * D:(m + 1) * D], condT[:, :],
                                start=True, stop=True)
            ins.then_inc(ada_full, 1)
            pe.wait_ge(ctxT_made, 1)
            pe.wait_ge(kv_in, 16)
            ck, cv = part("ck"), part("cv")
            for c in range(PAIRS):
                ins = pe.matmul(s_bank[c // 4][:, (c % 4) * P:(c % 4 + 1) * P], cv[0:CD, c * P:(c + 1) * P],
                                ctxT[0:CD, :], start=True, stop=True)
            ins.then_inc(vT_full, 1)
            for c in range(PAIRS):
                ins = pe.matmul(pj_bank[c // 4][:, (c % 4) * P:(c % 4 + 1) * P], ck[0:CD, c * P:(c + 1) * P],
                                ctxT[0:CD, :], start=True, stop=True)
            ins.then_inc(kT_full, 1)
            if not rope:
                cq = part("cq")
                for c in range(PAIRS):
                    ins = pe.transpose(t_bank[c // 4][:, (c % 4) * P:(c % 4 + 1) * P], cq[:, c * P:(c + 1) * P],
                                       ident[:, :])
                ins.then_inc(wqT_full, 1)
            pe.wait_ge(vT_made, 2)
            if rope:
                pe.wait_ge(kT_step, 4)
            else:
                pe.wait_ge(kT_step, 2)
                pe.wait_ge(wqT_made, 2)
            for odd in range(2):
                r = slice(DH * odd, DH * odd + DH)
                for c in range(PAIRS):
                    bk = (t_bank if odd else pj_bank)[c // 4]
                    ins = pe.matmul(bk[:, (c % 4) * P:(c % 4 + 1) * P], vcT[r, c, :], co[r, c, :],
                                    start=True, stop=True)
            ins.then_inc(vw_full, 1)
            if not rope:
                pe.wait_ge(ada_step, 6)
                for odd in range(2):
                    r = slice(DH * odd, DH * odd + DH)
                    for c in range(PAIRS):
                        bk = (s_bank[0], s_bank[1], acc_bank, o_bank)[2 * odd + c // 4]
                        ins = pe.matmul(bk[:, (c % 4) * P:(c % 4 + 1) * P], wqT[r, c, :], kT[r, c, :],
                                        start=True, stop=True)
                ins.then_inc(kw_full, 1)


def batch_loop(nc, li, rope, e, src, dst):
    ident, v_sb, oT, probs, probsT = e["ident"], e["v_sb"], e["oT"], e["probs"], e["probsT"]
    h_f, xn, h_hi, h_lo = e["h_f"], e["xn"], e["h_hi"], e["h_lo"]
    h2_f, xn2, h2_hi, h2_lo = e["h2_f"], e["xn2"], e["h2_hi"], e["h2_lo"]
    q_hi, q_lo, k_hi, k_lo = e["q_hi"], e["q_lo"], e["k_hi"], e["k_lo"]
    x_sb, x_new, x_res, r_in, r_sb = e["x_sb"], e["x_new"], e["x_res"], e["r_in"], e["r_sb"]
    stats, mv, rstd, negmax = e["stats"], e["mv"], e["rstd"], e["negmax"]
    var_eps, half_var, sq = e["var_eps"], e["half_var"], e["sq"]
    sums, recips, c_negmax, c_sum, c_recip = e["sums"], e["recips"], e["c_negmax"], e["c_sum"], e["c_recip"]
    vec_own, vec_prev, vecs, vw = e["vec_own"], e["vec_prev"], e["vecs"], e["vw"]
    cols, bias_rows, cqT, c_probs, c_probsT = e["cols"], e["bias_rows"], e["cqT"], e["c_probs"], e["c_probsT"]
    w_hi, w_lo, wo, f2 = e["w_hi"], e["w_lo"], e["wo"], e["f2"]
    s_bank, t_bank, pj_bank = e["s_bank"], e["t_bank"], e["pj_bank"]
    o_bank, acc_bank = e["o_bank"], e["acc_bank"]
    plans = {v: make_plan(rope, v) for v in ("first", "full", "last")}

    with ExitStack() as st:
        def sem(name):
            return st.enter_context(nc.semaphore(f"l{li}_{name}"))

        S = {name: sem(name) for name in SIGNALS}
        x_loaded, x_new_free = sem("x_loaded"), sem("x_new_free")

        def passes(eng, run):
            run(Pass(plans, "first", 0))
            with eng.Fori(1, B) as b:
                run(Pass(plans, "full", b))
            run(Pass(plans, "last", B))

        def pj(w, *step):
            return pj_bank[w.ring(PJ_KINDS, step)[0]]

        def t_of(w, *step):
            return t_bank[w.ring(("t", "ct"), step)[0]]

        def s_of(w, *step):
            return s_bank[w.ring(("s", "cs"), step)[0]]

        def tile(p, head, qt):
            return SLOT_GROUP[2 * (p % PAIRS) + head] * QT + qt

        def copied(step):
            return (step[0] + "_copy",) + step[1:]

        def rotated(step):
            kind, c = step
            return cqT[:, c % 2, :] if kind == "rot_cq" else e["rot_a"][:, kind == "rot_k", :]

        def hidden(i):
            return (cqT, c_probs)[i // 2][:, i % 2, :] if rope else cqT[:, i, :]

        def reader(w, step):
            kind, i = step
            if kind in ("q", "k"):
                if rope:
                    return "rope_mul", "rot_" + kind, i
                return ("qk_lo", "lo_q", i) if kind == "q" else ("qk_lo", "lo_k", i, 1)
            return {"turn": ("h_full", "turn", i), "v": ("v_dve" if i % 2 else "v_act", "v", i),
                    "r": ("r_made", "r", i), "cq": ("rope_mul", "rot_cq", i),
                    "gate": ("gelu_made", "gate", i), "up": ("hid_made", "up", i)}[kind]

        block = st.enter_context(nc.Block())

        @block.sync
        def _(sp):
            rows = "b (t p) d -> b p t d"
            flat = "b p t d -> (b p) t d"
            sp.sem_inc(x_new_free, 16)
            sp.dma_start(x_sb[:, :, :], src.rearrange(rows, p=P)[0]).then_inc(x_loaded, 16)
            sp.wait_ge(S["bias0_made"], 1)
            sp.dma_start(x_sb[:, :, :], src.rearrange(rows, p=P)[1]).then_inc(x_loaded, 16)
            with sp.Fori(1, B - 1) as b:
                sp.wait_ge(S["bias0_made"], b + 1)
                sp.dma_start(x_sb[:, :, :], src.rearrange(rows, p=P)[bass.ds(b + 1, 1)].rearrange(flat)
                             ).then_inc(x_loaded, 16)
                sp.wait_ge(S["added"], b * 3)
                sp.dma_start(dst.rearrange(rows, p=P)[bass.ds(b - 1, 1)].rearrange(flat),
                             x_new[:, :, :]).then_inc(x_new_free, 16)
            for b in (B - 2, B - 1):
                sp.wait_ge(S["added"], 3 * b + 3)
                sp.dma_start(dst.rearrange(rows, p=P)[b], x_new[:, :, :]).then_inc(x_new_free, 16)
            sp.wait_ge(x_new_free, 16 * (B + 1))

        @block.gpsimd
        def _(pool):
            def bias(w, n):
                pool.wait_ge(S["xn_made"], w.at("xn_made", "norm", n))
                if n == 0 and w.prev:
                    pool.wait_ge(S["added"], w.at("added", "res", 0))
                x, out, made = (x_sb, x_res, "bias0_made") if n == 0 else (x_new, x_new, "biased")
                pool.tensor_tensor(out[:, :, :], x[:, :, :], bias_rows[:, n, :].unsqueeze(1).broadcast_to([P, QT, D]),
                                   ALU.add).then_inc(S[made], 1)

            def rope_sum(w, step):
                pool.wait_ge(S["rope_mul"], w.at("rope_mul", *step))
                out, swapped = rotated(step), e["rot_b"][:, w.ring(ROTATIONS, step)[0], :]
                if step[0] != "rot_cq":
                    pool.tensor_tensor(swapped, swapped, e["rope_cs"][:, 1, :], ALU.mult).then_inc(S["sin_mul"], 1)
                    pool.wait_ge(S["sin_mul"], w.at("sin_mul", *step))
                pool.tensor_tensor(out, out, swapped, ALU.add).then_inc(S["rope_add"], 1)

            def spread(w, p):
                if w.has("r", p - 1):
                    pool.wait_ge(S["pj_full"], w.at("pj_full", "r", p - 1))
                pool.wait_ge(S["recip_made"], w.at("recip_made", "recip", p))
                shape4 = [P, 2, QT, DH]
                pool.tensor_tensor(r_in[:, :, :, :].rearrange("p t h d -> p h t d"),
                                   recips[:, :].rearrange("p (h t) -> p h t", h=2).unsqueeze(3).broadcast_to(shape4),
                                   e["ones"][:, 0:1].unsqueeze(2).unsqueeze(3).broadcast_to(shape4),
                                   ALU.mult).then_inc(S["r_in_made"], 1)

            def cross_norm(w, u):
                pool.wait_ge(S["c_inv"], w.at("c_inv", "csum", u))
                p4 = c_probs[:, u % 2, :].rearrange("p (h k) -> p h k", k=J)
                pool.tensor_tensor(p4, p4, c_recip[:, u, :].unsqueeze(2).broadcast_to([P, H, J]),
                                   ALU.mult).then_inc(S["c_norm"], 1)

            def run(w):
                for step in w.plan:
                    kind = step[0]
                    if kind == "bias":
                        bias(w, step[1])
                    elif kind.startswith("rot") and rope:
                        rope_sum(w, step)
                    elif kind == "recip":
                        spread(w, step[1])
                    elif kind == "csum":
                        cross_norm(w, step[1])

            passes(pool, run)

        @block.tensor
        def _(pe):
            def claim(w, *step):
                old = w.ring(PJ_KINDS, step)[1]
                if old:
                    name, *read = reader(w, old)
                    pe.wait_ge(S[name], w.at(name, *read))

            def three(out, a_hi, a_lo, b_hi, b_lo):
                pe.matmul(out, a_hi, b_hi, start=True, stop=False)
                pe.matmul(out, a_lo, b_hi, start=False, stop=False)
                return pe.matmul(out, a_hi, b_lo, start=False, stop=True)

            def turn_norm(w, n):
                pe.wait_ge(S["xn_made"], w.at("xn_made", "norm", n))
                claim(w, "turn", n)
                x = xn if n == 0 else xn2
                for t in range(QT):
                    ins = pe.transpose(pj(w, "turn", n)[:, t * P:(t + 1) * P], x[:, t, :], ident[:, :])
                ins.then_inc(S["pj_full"], 1)

            def project(w, step, weight, chunk):
                norm = {"q": 0, "k": 0, "cq": 1, "f": 2}[weight]
                pe.wait_ge(S["h_lo_made"], w.at("h_lo_made", "turn", norm))
                claim(w, *step)
                cs = slice(chunk * P, chunk * P + P)
                hh, hl = (h_hi, h_lo) if norm == 0 else (h2_hi, h2_lo)
                three(pj(w, *step)[:, :], w_hi[weight][:, cs], w_lo[weight][:, cs], hh[:, :], hl[:, :]
                      ).then_inc(S["pj_full"], 1)

            def values(w, j):
                half, kt = j // KT, j % KT
                pe.wait_ge(S["h_lo_made"], w.at("h_lo_made", "turn", 0))
                claim(w, "v", j)
                ts, cs = slice(kt * P, kt * P + P), slice(half * N, half * N + N)
                three(pj(w, "v", j)[:, :], h_hi[:, ts], h_lo[:, ts], w_hi["v"][:, cs], w_lo["v"][:, cs]
                      ).then_inc(S["pj_full"], 1)

            def recip_rows(w, p):
                pe.wait_ge(S["r_in_made"], w.at("r_in_made", "recip", p))
                claim(w, "r", p)
                for t in range(QT):
                    ins = pe.transpose(pj(w, "r", p)[:, t * P:(t + 1) * P],
                                       r_in[:, t, :, :].rearrange("p h d -> p (h d)"), ident[:, :])
                ins.then_inc(S["pj_full"], 1)

            def claim_s(w, *step):
                old = w.ring(("s", "cs"), step)[1]
                if old:
                    if old[0] == "s":
                        pe.wait_ge(S["exp_made"], w.at("exp_made", "exp", *old[1:]))
                    else:
                        pe.wait_ge(S["c_sub"], w.at("c_sub", "cmax", old[1]))

            def scores(w, c, s):
                head, qt = s // QT, s % QT
                if qt == 0:
                    pe.wait_ge(S["qk_lo"], w.at("qk_lo", "lo_k", c, head))
                claim_s(w, "s", c, s)
                ts = slice(qt * P, qt * P + P)
                three(s_of(w, "s", c, s)[:, :], q_hi[:, c % 2, ts], q_lo[:, c % 2, ts],
                      k_hi[:, c % 2, head, :], k_lo[:, c % 2, head, :]).then_inc(S["s_full"], 1)

            def claim_t(w, *step):
                old = w.ring(("t", "ct"), step)[1]
                if old:
                    name = "pt_act" if evacuator(old) == "a" else "pt_dve"
                    pe.wait_ge(S[name], w.at(name, *copied(old)))

            def turn_probs(w, p, i):
                head, kt = i // KT, i % KT
                if kt == 0:
                    pe.wait_ge(S["exp_made"], w.at("exp_made", "exp", p, head * QT + QT - 1))
                claim_t(w, "t", p, i)
                for t in range(QT):
                    ins = pe.transpose(t_of(w, "t", p, i)[:, t * P:(t + 1) * P],
                                       probs[:, tile(p, head, t), kt * P:(kt + 1) * P], ident[:, :])
                ins.then_inc(S["t_full"], 1)

            def weigh(w, p, k):
                if k == 0:
                    if p in (0, PAIRS // 2):
                        last = KT * (1 + 2 * p // PAIRS) - 1
                        pe.wait_ge(S["v_act"], w.at("v_act", "v", last - 1))
                        pe.wait_ge(S["v_dve"], w.at("v_dve", "v", last))
                    if w.has("o", p - 1):
                        pe.wait_ge(S["o_made"], w.at("o_made", "o", p - 1))
                for name, engine in (("pt_act", "a"), ("pt_dve", "v")):
                    mine = [i for i in (k, KT + k) if EVACUATE[i] == engine]
                    if mine:
                        pe.wait_ge(S[name], w.at(name, "t_copy", p, mine[-1]))
                for head in range(2):
                    h = 2 * (p % PAIRS) + head
                    ins = pe.matmul(o_bank[DH * head:DH * head + DH, :], v_sb[:, k, h * DH:(h + 1) * DH],
                                    probsT[:, KT * head + k, :], start=(k == 0), stop=(k == KT - 1))
                ins.then_inc(S["av_done"], 1)

            def out_rows(w, t):
                if t == 0:
                    pe.wait_ge(S["o_made"], w.at("o_made", "o", -1))
                for g in range(PAIRS):
                    ins = pe.matmul(acc_bank[:, t * P:(t + 1) * P], oT[:, g, t * P:(t + 1) * P], wo[:, g, :],
                                    start=(g == 0), stop=(g == PAIRS - 1))
                if t == QT - 1:
                    ins.then_inc(S["acc_full"], 1)

            def cross_scores(w, u):
                claim_s(w, "cs", u)
                if rope:
                    pe.wait_ge(S["rope_add"], w.at("rope_add", "rot_cq", 2 * u + 1))
                    pe.wait_ge(S["diag_made"], w.at("diag_made", "load", 0))
                    for t in range(QT):
                        for j in range(2):
                            ins = pe.matmul(s_of(w, "cs", u)[:, t * P:(t + 1) * P], cqT[:, j, t * P:(t + 1) * P],
                                            e["k_diag"][:, 2 * u + j, :], start=(j == 0), stop=(j == 1))
                    ins.then_inc(S["s_full"], 1)
                else:
                    pe.wait_ge(S["h_lo_made"], w.at("h_lo_made", "turn", 1))
                    kwh, kwl = (e[n][:, bass.ds(w.b - 1, 1), :].rearrange("p b n -> p (b n)")
                                for n in ("kw_hi", "kw_lo"))
                    ts = slice(u * P, u * P + P)
                    three(s_of(w, "cs", u)[:, :], h2_hi[:, ts], h2_lo[:, ts], kwh, kwl).then_inc(S["s_full"], 1)

            def turn_cross(w, u):
                pe.wait_ge(S["c_norm"], w.at("c_norm", "csum", u))
                claim_t(w, "ct", u)
                for j in range(4):
                    ins = pe.transpose(t_of(w, "ct", u)[:, j * P:(j + 1) * P],
                                       c_probs[:, u % 2, j * P:(j + 1) * P], ident[:, :])
                ins.then_inc(S["t_full"], 1)

            def cross_out(w, u):
                if u == 0:
                    pe.wait_ge(S["added"], w.at("added", "res", 0))
                name = "pt_act" if evacuator(("ct", u)) == "a" else "pt_dve"
                pe.wait_ge(S[name], w.at(name, "ct_copy", u))
                for j in range(4):
                    t, g = (j, u) if rope else (u, j)
                    first, last = (u == 0 and j == 0, u == QT - 1) if rope else (j == 0, j == 3)
                    ins = pe.matmul(acc_bank[:, t * P:(t + 1) * P], c_probsT[:, u % 2, j * P:(j + 1) * P],
                                    vw[:, bass.ds(w.b - 1, 1), g, :].rearrange("p b d -> p (b d)"),
                                    start=first, stop=last, skip_group_check=rope)
                if u == QT - 1:
                    ins.then_inc(S["acc_full"], 1)
                else:
                    ins.then_inc(S["c_done"], 1)

            def ff_out(w, i):
                if i == 0:
                    pe.wait_ge(S["added"], w.at("added", "res", 1))
                pe.wait_ge(S["gelu_made" if rope else "hid_made"],
                           w.at("gelu_made", "gate", i) if rope else w.at("hid_made", "up", i))
                for t in range(QT):
                    ins = pe.matmul(acc_bank[:, t * P:(t + 1) * P], hidden(i)[:, t * P:(t + 1) * P], f2[:, i, :],
                                    start=(i == 0 and t == 0), stop=(i == FC - 1), skip_group_check=True)
                if i == FC - 1:
                    ins.then_inc(S["acc_full"], 1)

            def run(w):
                for step in w.plan:
                    kind, i = step[0], step[1]
                    if kind == "turn":
                        turn_norm(w, i)
                    elif kind == "v":
                        values(w, i)
                    elif kind in ("q", "k", "cq"):
                        project(w, step, kind, i)
                    elif kind == "s":
                        scores(w, i, step[2])
                    elif kind == "t":
                        turn_probs(w, i, step[2])
                    elif kind == "av":
                        weigh(w, i, step[2])
                    elif kind == "r":
                        recip_rows(w, i)
                    elif kind == "out":
                        out_rows(w, i)
                    elif kind == "cs":
                        cross_scores(w, i)
                    elif kind == "ct":
                        turn_cross(w, i)
                    elif kind == "cout":
                        cross_out(w, i)
                    elif kind == "gate":
                        project(w, step, "f", i if rope else FC + i)
                    elif kind == "up":
                        project(w, step, "f", i)
                    elif kind == "fout":
                        ff_out(w, i)

            passes(pe, run)

        def blocks_out(eng, w, step):
            made = (step[0][:-5],) + step[1:]
            eng.wait_ge(S["t_full"], w.at("t_full", *made))
            bank = t_of(w, *made)[:, :]
            if step[0] == "ct_copy":
                u = step[1]
                if u >= 2:
                    eng.wait_ge(S["c_done"], w.at("c_done", "cout", u - 2))
                return c_probsT[:, u % 2, :], bank
            p, i = step[1], step[2]
            if w.has("av", p - 1, i % KT):
                eng.wait_ge(S["av_done"], w.at("av_done", "av", p - 1, i % KT))
            return probsT[:, i, :], bank

        def value_slot(eng, w, j):
            eng.wait_ge(S["pj_full"], w.at("pj_full", "v", j))
            if w.prev:
                last_pair = (j // KT + 1) * PAIRS // 2 - 1 - PAIRS
                eng.wait_ge(S["av_done"], w.at("av_done", "av", last_pair, KT - 1))
            return v_sb[:, j % KT, j // KT * N:(j // KT + 1) * N]

        @block.scalar
        def _(act):
            def norm_hi(w, n):
                f, hi = (h_f, h_hi) if n == 0 else (h2_f, h2_hi)
                act.wait_ge(S["h_full"], w.at("h_full", "turn", n))
                act.copy(hi[:, :], f[:, :]).then_inc(S["h_hi_made"], 1)

            def high(w, step):
                kind, c = step[:2]
                x = kind[-1]
                if w.has("s", c - 2, TILES - 1):
                    act.wait_ge(S["s_full"], w.at("s_full", "s", c - 2, TILES - 1))
                if rope:
                    act.wait_ge(S["rope_add"], w.at("rope_add", f"rot_{x}", c))
                    full = rotated((f"rot_{x}", c))
                else:
                    act.wait_ge(S["pj_full"], w.at("pj_full", x, c))
                    full = pj(w, x, c)[:, :]
                if x == "q":
                    act.mul(q_hi[:, c % 2, :], full, SCALE).then_inc(S["qk_hi"], 1)
                else:
                    head = step[2]
                    rows = slice(DH * head, DH * head + DH)
                    act.copy(k_hi[rows, c % 2, head, :], full[rows, :]).then_inc(S["qk_hi"], 1)

            def exps(w, c, s):
                n, head, qt = c * TILES + s, s // QT, s % QT
                if qt == 0:
                    old = next(g for g in range(2 * c + head - 1, -PAIRS * 4, -1)
                               if SLOT_GROUP[g % H] == SLOT_GROUP[(2 * c + head) % H])
                    if w.has("t", old // 2, old % 2 * KT + KT - 1):
                        act.wait_ge(S["t_full"], w.at("t_full", "t", old // 2, old % 2 * KT + KT - 1))
                if s == 0 and w.has("recip", c - 2):
                    act.wait_ge(S["recip_made"], w.at("recip_made", "recip", c - 2))
                act.wait_ge(S["max_made"], w.at("max_made", "max", c, s))
                act.activation(probs[:, tile(c, head, qt), :], s_of(w, "s", c, s)[:, :], ACT.Exp,
                               bias=negmax[:, n % NM:n % NM + 1],
                               accum_out=sums[:, c % 2, s:s + 1]).then_inc(S["exp_made"], 1)

            def gelu(w, i):
                act.wait_ge(S["pj_full"], w.at("pj_full", "gate", i))
                out = hidden(i) if rope else (c_probs, c_probsT)[i // 2][:, i % 2, :]
                col = 8 + i if rope else 6 + FC + i
                act.activation(out, pj(w, "gate", i)[:, :], ACT.Gelu, bias=cols[:, col:col + 1]
                               ).then_inc(S["gelu_made"], 1)

            def run(w):
                for step in w.plan:
                    kind, i = step[0], step[1]
                    if kind == "turn":
                        norm_hi(w, i)
                    elif kind == "v" and i % 2 == 0:
                        act.copy(value_slot(act, w, i), pj(w, "v", i)[:, :]).then_inc(S["v_act"], 1)
                    elif kind in ("hi_q", "hi_k"):
                        high(w, step)
                    elif kind == "exp":
                        exps(w, i, step[2])
                    elif kind in ("t_copy", "ct_copy") and evacuator(step) == "a":
                        act.copy(*blocks_out(act, w, step)).then_inc(S["pt_act"], 1)
                    elif kind == "r":
                        act.wait_ge(S["pj_full"], w.at("pj_full", "r", i))
                        if w.has("o", i - 1):
                            act.wait_ge(S["o_made"], w.at("o_made", "o", i - 1))
                        act.copy(r_sb[:, :], pj(w, "r", i)[:, :]).then_inc(S["r_made"], 1)
                    elif kind == "cexp":
                        act.wait_ge(S["c_sub"], w.at("c_sub", "cmax", i))
                        act.activation(c_probs[:, i % 2, :], c_probs[:, i % 2, :], ACT.Exp).then_inc(S["c_exp"], 1)
                    elif kind == "gate":
                        gelu(w, i)

            passes(act, run)

        @block.vector
        def _(dve):
            def norm(w, n):
                x, out = (x_sb, xn) if n == 0 else (x_new, xn2)
                if n == 0:
                    dve.wait_ge(x_loaded, w.b * 16 + 16)
                else:
                    dve.wait_ge(S["added"], w.at("added", "res", n - 1))
                for t in range(QT):
                    dve.bn_stats(stats[:, t, :], x[:, t, :])
                dve.drain()
                for t in range(QT):
                    ins = dve.bn_aggr(mv[:, t, :], stats[:, t, :])
                ins.then_inc(S["chain"], 1)
                inverse_root(dve, mv[:, :, 1], var_eps[:, :], half_var[:, :], sq[:, :], rstd[:, :], S["chain"],
                             w.at("chain", "norm", n) - CHAIN + 1)
                for t in range(QT):
                    ins = dve.tensor_scalar(out[:, t, :], x[:, t, :], mv[:, t, 0:1], rstd[:, t:t + 1],
                                            ALU.subtract, ALU.mult)
                ins.then_inc(S["xn_made"], 1)

            def scale_shift(w, n):
                f, hi, lo = (h_f, h_hi, h_lo) if n == 0 else (h2_f, h2_hi, h2_lo)
                vec = vec_own[:, 0:2] if n == 0 else vec_prev[:, 2 * n - 2:2 * n]
                dve.wait_ge(S["pj_full"], w.at("pj_full", "turn", n))
                dve.tensor_scalar(f[:, :], pj(w, "turn", n)[:, :], vec[:, 0:1], vec[:, 1:2],
                                  ALU.mult, ALU.add).then_inc(S["h_full"], 1)
                dve.wait_ge(S["h_hi_made"], w.at("h_hi_made", "turn", n))
                dve.tensor_tensor(lo[:, :], f[:, :], hi[:, :].bitcast(F32), ALU.subtract).then_inc(S["h_lo_made"], 1)

            def rotate(w, step):
                kind, c = step
                j, old = w.ring(ROTATIONS, step)
                name = kind[4:]
                a, b2, bank = rotated(step), e["rot_b"][:, j, :], pj(w, name, c)
                dve.wait_ge(S["pj_full"], w.at("pj_full", name, c))
                if old:
                    dve.wait_ge(S["rope_add"], w.at("rope_add", *old))
                if kind == "rot_cq" and c >= 2:
                    dve.wait_ge(S["s_full"], w.at("s_full", "cs", c // 2 - 1))
                dve.tensor_tensor(a, bank[:, :], e["rope_cs"][:, 0, :], ALU.mult)
                shuffle = dve.stream_shuffle(b2, bank[:, :], SWAP)
                if kind == "rot_cq":
                    shuffle.then_inc(S["shuffled"], 1)
                    dve.wait_ge(S["shuffled"], w.at("shuffled", *step))
                    dve.tensor_tensor(b2, b2, e["rope_cs"][:, 1, :], ALU.mult).then_inc(S["rope_mul"], 1)
                else:
                    shuffle.then_inc(S["rope_mul"], 1)

            def low(w, step):
                kind, c = step[:2]
                x = kind[-1]
                dve.wait_ge(S["qk_hi"], w.at("qk_hi", "hi_" + x, *step[1:]))
                full = rotated((f"rot_{x}", c)) if rope else pj(w, x, c)[:, :]
                if x == "q":
                    dve.scalar_tensor_tensor(out=q_lo[:, c % 2, :], in0=full, scalar=SCALE,
                                             in1=q_hi[:, c % 2, :].bitcast(F32), op0=ALU.mult, op1=ALU.subtract
                                             ).then_inc(S["qk_lo"], 1)
                else:
                    head = step[2]
                    rows = slice(DH * head, DH * head + DH)
                    dve.tensor_tensor(k_lo[rows, c % 2, head, :], full[rows, :],
                                      k_hi[rows, c % 2, head, :].bitcast(F32), ALU.subtract
                                      ).then_inc(S["qk_lo"], 1)

            def invert(w, p):
                dve.wait_ge(S["exp_made"], w.at("exp_made", "exp", p, TILES - 1))
                if w.has("recip", p - 1):
                    dve.wait_ge(S["r_in_made"], w.at("r_in_made", "recip", p - 1))
                dve.reciprocal(recips[:, :], sums[:, p % 2, :]).then_inc(S["recip_made"], 1)

            def divide(w, p):
                dve.wait_ge(S["av_done"], w.at("av_done", "av", p, KT - 1))
                dve.wait_ge(S["r_made"], w.at("r_made", "r", p))
                dve.tensor_tensor(oT[:, p % PAIRS, :], o_bank[:, :], r_sb[:, :], ALU.mult).then_inc(S["o_made"], 1)

            def cross_max(w, u):
                dve.wait_ge(S["s_full"], w.at("s_full", "cs", u))
                if u >= 2:
                    dve.wait_ge(S["t_full"], w.at("t_full", "ct", u - 2))
                sv = s_of(w, "cs", u)[:, :].rearrange("p (h k) -> p h k", k=J)
                dve.tensor_reduce(c_negmax[:, u, :], sv, AX_X, ALU.max, negate=True).then_inc(S["c_max"], 1)
                dve.wait_ge(S["c_max"], w.at("c_max", "cmax", u))
                dve.tensor_tensor(c_probs[:, u % 2, :].rearrange("p (h k) -> p h k", k=J), sv,
                                  c_negmax[:, u, :].unsqueeze(2).broadcast_to([P, H, J]), ALU.add
                                  ).then_inc(S["c_sub"], 1)

            def cross_sum(w, u):
                dve.wait_ge(S["c_exp"], w.at("c_exp", "cexp", u))
                dve.tensor_reduce(c_sum[:, u, :], c_probs[:, u % 2, :].rearrange("p (h k) -> p h k", k=J), AX_X,
                                  ALU.add).then_inc(S["c_summed"], 1)
                dve.wait_ge(S["c_summed"], w.at("c_summed", "csum", u))
                dve.reciprocal(c_recip[:, u, :], c_sum[:, u, :]).then_inc(S["c_inv"], 1)

            def add_residual(w, n):
                dve.wait_ge(S["acc_full"], w.before("acc_full") + n + 1)
                if n == 0:
                    dve.wait_ge(S["bias0_made"], w.before("bias0_made"))
                    dve.wait_ge(x_new_free, w.b * 16)
                else:
                    dve.wait_ge(S["biased"], w.at("biased", "bias", n))
                x = x_res if n == 0 else x_new
                dve.tensor_tensor(x_new[:, :, :], acc_bank[:, :].rearrange("p (t d) -> p t d", d=D), x[:, :, :],
                                  ALU.add).then_inc(S["added"], 1)

            def run(w):
                if w.own:
                    dve.tensor_copy(vec_own[:, :], vecs[:, bass.ds(w.b, 1), 0:2].rearrange("p b n -> p (b n)"))
                if w.prev:
                    dve.tensor_copy(vec_prev[:, :], vecs[:, bass.ds(w.b - 1, 1), 2:6].rearrange("p b n -> p (b n)"))
                for step in w.plan:
                    kind, i = step[0], step[1]
                    if kind == "norm":
                        norm(w, i)
                    elif kind == "turn":
                        scale_shift(w, i)
                    elif kind == "v" and i % 2 == 1:
                        dve.tensor_copy(value_slot(dve, w, i), pj(w, "v", i)[:, :]).then_inc(S["v_dve"], 1)
                    elif kind.startswith("rot") and rope:
                        rotate(w, step)
                    elif kind in ("lo_q", "lo_k"):
                        low(w, step)
                    elif kind == "max":
                        n = i * TILES + step[2]
                        dve.wait_ge(S["s_full"], w.at("s_full", "s", *step[1:]))
                        dve.tensor_reduce(negmax[:, n % NM:n % NM + 1], s_of(w, "s", *step[1:])[:, :], AX_X, ALU.max,
                                          negate=True).then_inc(S["max_made"], 1)
                    elif kind in ("t_copy", "ct_copy") and evacuator(step) == "v":
                        dve.tensor_copy(*blocks_out(dve, w, step)).then_inc(S["pt_dve"], 1)
                    elif kind == "recip":
                        invert(w, i)
                    elif kind == "o":
                        divide(w, i)
                    elif kind == "load" and rope:
                        kd = e["k_diag"][:, :, :].rearrange("p (g o) n -> p g o n", o=2)
                        kc = e["kc"][:, :, bass.ds((w.b - 1) * J, J)].rearrange("p (g o) n -> p g o n", o=2)
                        for half in range(2):
                            r = slice(DH * half, DH * half + DH)
                            for o in range(2):
                                at = 2 * J * o + J * half
                                dve.tensor_copy(kd[r, :, o, at:at + J], kc[r, :, o, :]).then_inc(S["diag_made"], 1)
                    elif kind == "cmax":
                        cross_max(w, i)
                    elif kind == "csum":
                        cross_sum(w, i)
                    elif kind == "up":
                        dve.wait_ge(S["pj_full"], w.at("pj_full", "up", i))
                        dve.wait_ge(S["gelu_made"], w.at("gelu_made", "gate", i))
                        dve.scalar_tensor_tensor(out=hidden(i), in0=pj(w, "up", i)[:, :],
                                                 scalar=cols[:, 6 + i:7 + i],
                                                 in1=(c_probs, c_probsT)[i // 2][:, i % 2, :],
                                                 op0=ALU.add, op1=ALU.mult).then_inc(S["hid_made"], 1)
                    elif kind == "res":
                        add_residual(w, i)

            passes(dve, run)


def rope_tables():
    inv = (1.0 / np.float32(10000.0) ** (np.arange(0, DH, 2, dtype=np.float32) / np.float32(DH))).astype(np.float32)
    ang = np.arange(N, dtype=np.float32)[None, :] * inv[:, None]
    cos, sin = (np.repeat(f(ang).astype(np.float32), 2, axis=0) for f in (np.cos, np.sin))
    sin[0::2] *= -1
    return np.ascontiguousarray(np.concatenate([np.tile(cos, (2, 1)), np.tile(sin, (2, 1))], axis=1))


def kernel(**inputs):
    import numpy as _np
    import concourse.bacc as _bacc
    from concourse.bass_utils import run_bass_kernel_spmd as _run

    w = {k: _np.asarray(v) for k, v in inputs.items()}

    def l0(n):
        return w[f"L0_xcond_{n}"]

    def l1(n):
        return w[f"L1_xcond_{n}"]

    def stack(m):
        return m.reshape(-1, P, m.shape[1]).transpose(1, 0, 2).reshape(P, -1)

    def columns(*vs):
        return _np.concatenate([v.reshape(-1, P).T for v in vs], axis=1)

    arrays = {
        "x": w["x"],
        "ctx": w["ctx_768"].reshape(B * J, CD),
        "cond": w["cond_1024"].T,
        "tables": rope_tables(),
        "w128_0": _np.concatenate([
            l0("sa_wq"), l0("sa_wkv"), l0("ca_wq"), l0("ff_w1"),
            l0("g1_w"), l0("b1_w"), l0("g2_w"), l0("b2_w"), stack(l0("ca_wo")),
            stack(l0("sa_wo")), stack(l0("ff_w2"))], axis=1),
        "w128_1": _np.concatenate([
            l1("q1"), l1("k1"), l1("v1"), l1("ff_w1"),
            l1("n1_w"), l1("n2_w"), l1("n3_w"), stack(l1("o2_w")), l1("q2"),
            stack(l1("o1_w")), stack(l1("ff_w2"))], axis=1),
        "w96_0": l0("ca_wkv"),
        "w96_1": _np.concatenate([l1("k2"), l1("v2")], axis=1),
        "cols_0": columns(l0("ln1_w"), l0("ln1_b"), l0("g1_b"), l0("b1_b"),
                          l0("ln2_w"), l0("ln2_b"), l0("g2_b"), l0("b2_b"), l0("ff_b1")),
        "cols_1": columns(l1("n1_b"), l1("n2_b"), l1("n3_b"), l1("ff_b1")),
        "rows_0": _np.concatenate([l0("sa_bo"), l0("ca_bo"), l0("ff_b2"), l0("ca_lnc_w"), l0("ca_lnc_b")])[None],
        "rows_1": _np.concatenate([l1("o1_b"), l1("o2_b"), l1("ff_b2")])[None],
    }
    arrays = {k: _np.ascontiguousarray(v) for k, v in arrays.items()}
    nc = _bacc.Bacc("TRN2", target_bir_lowering=False, num_devices=1)
    ap = {k: nc.dram_tensor(k, v.shape, F32, kind="ExternalInput").ap() for k, v in arrays.items()}
    mid = nc.dram_tensor("x_mid", (B, N, D), F32, kind="Internal").ap()
    out = nc.dram_tensor("out", (B, N, D), F32, kind="ExternalOutput").ap()
    build(nc, ap["x"], mid, out, ap["ctx"], ap["cond"], ap["tables"], (ap["w128_0"], ap["w128_1"]),
          (ap["w96_0"], ap["w96_1"]), (ap["cols_0"], ap["cols_1"]), (ap["rows_0"], ap["rows_1"]))
    r = _run(nc, [arrays], core_ids=[0])
    return r.results[0]["out"]
```

```python
from contextlib import ExitStack

import numpy as np

import concourse.bass as bass
from concourse import mybir

F32 = mybir.dt.float32
F32R = mybir.dt.float32r
ALU = mybir.AluOpType
ACT = mybir.ActivationFunctionType
AX_X = mybir.AxisListType.X

B, N, D = 4, 512, 128
H, DH = 16, 64
J, CD = 32, 96
P = 128
QT = N // P
KT = N // P
MID = H * DH
PAIRS = H // 2
FC = 4
TILES = 2 * QT
CG = H * J // P
SCALE = float(DH) ** -0.5
EPS = 1e-5

S_BANKS = 2
P_SLOTS = 12
NM = 16

SPLIT = ([("q", MID), ("k", MID), ("v", MID), ("cq", MID), ("f", FC * P)],
         [("q", MID), ("k", MID), ("v", MID), ("f", 2 * FC * P)])
SETUP = ([("ada", 4 * D), ("co", PAIRS * D)],
         [("ada", 6 * D), ("co", PAIRS * D), ("cq", MID)])
KEEP = [("wo", PAIRS * D), ("f2", FC * D)]
CTXW = [("ck", MID), ("cv", MID)]
N_COLS = (8 + FC, 6 + 2 * FC)
N_ROWS = (3 * D + 2 * CD, 3 * D)


def spans(parts):
    out, at = {}, 0
    for name, n in parts:
        out[name] = (at, n)
        at += n
    return out, at


PAIR_STEPS = TILES
TIMES = {
    True: (
        -7.5,
        {
            "s": (0.3, 1.3, 2, 3, 4, 5.2, 6.55, 7),
            "max": (0.15, 1.35, 2.05, 3, 4.1, 4.95, 6.15, 7.2),
            "exp": (0.4, 2.2, 2.9, 3.6, 4.65, 5.85, 6.4, 6.8),
            "t": (4.75, 6.55, 6.95, 7.7, 9, 10.35, 11.25, 12.25),
            "av": (10.65, 12.05, 12.3, 14.1),
            "recip": (11.15,),
            "r": (13.25,),
            "o": (13.6,),
            "q": (-7.7,),
            "rot_q": (-6.9,),
            "k": (-6.15,),
            "rot_k": (-5.25,),
            "hi_q": (-4.85, -4.2),
            "lo_q": (-4.6, -3.2),
            "hi_k": (-3.75, -1.85),
            "lo_k": (-1.35, -0.05),
            "twice_k": (-1.15, -0.3),
            "t_act": (4.85, 6.25, 6.65, 7.65, 9, 10.7, 11.4, 12.2),
            "t_dve": (None, None, None, None, None, None, None, None),
        },
        {
            "q": (-4.6,),
            "rot_q": (-4.2,),
            "k": (-4,),
            "rot_k": (-3.45,),
            "hi_q": (-3.1, -2.55),
            "lo_q": (-2.45, -1.2),
            "hi_k": (-1.8, 0),
            "lo_k": (-0.75, 1.75),
            "twice_k": (2.65, 5.65),
        },
        {
            "norm": (-7.14,),
            "turn": (-5.6,),
            "v": (-1.5, -0.7, 3.3, 6.5, 11.2, 11.8, 12.05, 13.55),
            "bias": (19.2,),
            "root": (-7.13, -7.12, -7.11, -7.1),
            "normalise": (-7.08,),
        },
        {
            "load": (6.6,),
            "out": (6.55, 7.45, 8.15, 9.5),
            "res": (9.7, 35.5, 49.15),
            "norm": (None, 9.95, 35.8),
            "turn": (None, 14.25, 41.8),
            "bias": (None, 21.55, 48.75),
            "cq": (15.75, 16.75, 16.95, 20.95, 22.45, 23.45, 25.95, 27.85),
            "rot_cq": (15.7, 17.15, 20.3, 20.7, 23.4, 23.5, 27.5, 28.65),
            "cs": (19.6, 23.6, 27.55, 31.45),
            "cmax": (20.66, 24.96, 27.86, 32.11),
            "cexp": (20.35, 25.65, 28.25, 31.85),
            "csum": (22.4, 25.6, 30.8, 32.3),
            "ct": (23.9, 28.5, 33, 34.65),
            "cout": (25.65, 30.6, 34.1, 35.4),
            "gate": (43.65, 43.72, 44.34, 44.61),
            "fout": (45.1, 46.4, 47.35, 49.05),
            "ct_act": (24.55, 29.35, 33.4, 35.1),
            "ct_dve": (None, None, None, None),
            "root": (None, None, None, None, 11.71, 12.37, 12.38, 12.39, 36.71, 36.72, 36.73, 36.74),
            "normalise": (None, 12.91, 37.66),
        },
    ),
    False: (
        -8,
        {
            "s": (0.2, 1.1, 1.9, 2.75, 3.45, 4.8, 5.8, 6.9),
            "max": (0.7, 1, 1.75, 3.75, 4.15, 4.65, 5.95, 7.35),
            "exp": (0.95, 1.8, 2.05, 3.8, 4.65, 4.85, 7.4, 7.8),
            "t": (5.6, 6, 7.5, 8.15, 8.5, 8.55, 10.2, 11.85),
            "av": (10.1, 11.25, 12.65, 13.25),
            "recip": (10.65,),
            "r": (12.65,),
            "o": (12.95,),
            "q": (-7.7,),
            "hi_q": (-6.6, -6.4),
            "lo_q": (-6.1, -5.8),
            "k": (-5.35,),
            "hi_k": (-5.8, -5.1),
            "lo_k": (-4.2, -4.15),
            "twice_k": (-0.45, 1.4),
            "t_act": (4.85, 6.7, 7.5, 8.3, 9.05, 9.85, 10.85, 12.35),
            "t_dve": (None, None, None, None, None, None, None, None),
        },
        {
            "q": (-5.15,),
            "hi_q": (-5.95, -4.85),
            "lo_q": (-4.7, -4.15),
            "k": (-5.1,),
            "hi_k": (-5.65, -3.6),
            "lo_k": (-3.95, -3.15),
            "twice_k": (-1.15, 7.45),
        },
        {
            "norm": (-7.99,),
            "turn": (-6.4,),
            "v": (0.15, 4.7, 5.45, 6.25, 12.95, 15.8, 18.05, 22.85),
            "bias": (21.3,),
            "root": (-7.68, -7.67, -7.66, -7.6),
            "normalise": (-7.03,),
        },
        {
            "out": (7.15, 9.25, 9.7, 9.95),
            "res": (10.3, 30.95, 49.8),
            "norm": (None, 10.4, 32.6),
            "turn": (None, 12.8, 36.6),
            "bias": (None, 27.4, 43),
            "cs": (15.9, 18.2, 21.6, 24.4),
            "cmax": (16.56, 18.56, 21.16, 24.71),
            "cexp": (16.75, 19.5, 21.3, 27.25),
            "csum": (17.5, 20, 24.2, 28.3),
            "ct": (18.2, 22.2, 28.9, 29.7),
            "cout": (22.8, 25.1, 29.6, 30.4),
            "gate": (37.45, 38.47, 39.19, 43.31),
            "up": (39.41, 39.73, 39.85, 44.12),
            "fout": (41.9, 44.4, 44.75, 47.5),
            "ct_act": (19.75, None, 28.65, 29.45),
            "ct_dve": (None, 22.7, None, None),
            "root": (None, None, None, None, 10.71, 10.72, 10.73, 10.74, 32.91, 32.92, 32.93, 33.44),
            "normalise": (None, 11.71, 34.66),
        },
    ),
}
SLOT_GROUP = [g % 3 for g in range(H - 1)] + [1]
CHAIN = 12


def shape(variant):
    return variant != "last", variant != "first"


def make_plan(rope, variant):
    own, prev = shape(variant)
    steps = []

    def add(t, *step):
        steps.append((t, len(steps), step))

    start, pair, first_pair, entry, rest = TIMES[rope]
    for p in range(-3, PAIRS):
        for name, times in pair.items():
            if p == 0:
                times = first_pair.get(name, times)
            for i, t in enumerate(times):
                if t is None:
                    continue
                t += PAIR_STEPS * p
                if start <= t < start + PAIR_STEPS * PAIRS and (own if p >= 0 else prev):
                    add(t, name, p, *([i] if len(times) > 1 else []))
    for there, steps_of in ((own, entry), (prev, rest)):
        for name, times in steps_of.items():
            for i, t in enumerate(times):
                if there and t is not None:
                    add(t, name, i)
    return [step for _, _, step in sorted(steps)]


def copier(rope, step):
    _, pair, _, _, rest = TIMES[rope]
    times = pair["t_act"] if step[0] == "t" else rest["ct_act"]
    return "act" if times[step[-1]] is not None else "dve"


SIGNALS = {
    "pj_full": lambda s: s[0] in ("turn", "v", "q", "k", "r", "cq", "gate", "up"),
    "acc_full": lambda s: (s[0] == "out" and s[1] == QT - 1) or (s[0] == "cout" and s[1] == QT - 1)
    or (s[0] == "fout" and s[1] == FC - 1),
    "chain": lambda s: (s[0] == "norm") + (s[0] == "root") * (3 if s[1] % 4 else 2),
    "xn_made": lambda s: s[0] == "normalise",
    "h_full": lambda s: s[0] == "turn",
    "h_hi_made": lambda s: s[0] == "turn",
    "h_lo_made": lambda s: s[0] == "turn",
    "v_act": lambda s: s[0] == "v" and s[1] % 2 == 0,
    "v_dve": lambda s: s[0] == "v" and s[1] % 2 == 1,
    "sin_mul": lambda s: s[0].startswith("rot"),
    "rope_mul": lambda s: s[0].startswith("rot"),
    "rope_add": lambda s: s[0].startswith("rot"),
    "qk_hi": lambda s: s[0] in ("hi_q", "hi_k"),
    **{f"k_twice{i}": lambda s, i=i: 16 * (s[0] == "twice_k" and s[1] % 2 * 2 + s[2] == i) for i in range(4)},
    "qk_lo": lambda s: s[0] in ("lo_q", "lo_k"),
    "s_full": lambda s: s[0] in ("s", "cs"),
    "max_made": lambda s: s[0] == "max",
    "exp_made": lambda s: s[0] == "exp",
    "t_full": lambda s: s[0] in ("t", "ct"),
    "pt_act": lambda s: s[0] in ("t_act", "ct_act"),
    "pt_dve": lambda s: s[0] in ("t_dve", "ct_dve"),
    "recip_made": lambda s: s[0] == "recip",
    "r_in_made": lambda s: s[0] == "recip",
    "r_made": lambda s: s[0] == "r",
    "av_done": lambda s: s[0] == "av",
    "o_made": lambda s: s[0] == "o",
    "added": lambda s: s[0] == "res",
    "bias0_made": lambda s: s == ("bias", 0),
    "biased": lambda s: s[0] == "bias" and s[1] > 0,
    "diag_made": lambda s: 4 * (s[0] == "load"),
    "c_max": lambda s: s[0] == "cmax",
    "c_sub": lambda s: s[0] == "cmax",
    "c_exp": lambda s: s[0] == "cexp",
    "c_summed": lambda s: s[0] == "csum",
    "c_inv": lambda s: s[0] == "csum",
    "c_norm": lambda s: s[0] == "csum",
    "c_done": lambda s: s[0] == "cout" and s[1] < QT - 1,
    "gelu_made": lambda s: s[0] == "gate",
    "hid_made": lambda s: s[0] == "up",
}


class Pass:

    def __init__(self, plans, variant, b):
        self.plan, self.b, self.variant, self.plans = plans[variant], b, variant, plans
        self.more = not (isinstance(b, int) and b == B - 1)
        self.own, self.prev = shape(variant)
        self.per_pass = {}
        for name, count in SIGNALS.items():
            first, full = (sum(int(count(s)) for s in plans[v]) for v in ("first", "full"))
            self.per_pass[name] = (first, full)

    def before(self, name):
        first, full = self.per_pass[name]
        if self.variant == "first":
            return 0
        return (self.b - 1) * full + first

    def at(self, name, *step):
        if step not in self.plan:
            assert self.has(*step) and self.per_pass[name][0] > 0, step
            return self.before(name)
        n = sum(int(SIGNALS[name](s)) for s in self.plan[:self.plan.index(step) + 1])
        return self.before(name) + n

    def has(self, *step):
        return step in self.plan or (self.prev and step[1] < 0)

    def ring(self, kinds, step):
        these, first, full = ([s for s in plan if s[0] in kinds]
                              for plan in (self.plan, self.plans["first"], self.plans["full"]))
        shift = (len(full) - len(first)) % 2 if self.variant == "first" else 0
        i = these.index(step)
        buffer = (i + shift) % 2
        if i >= 2:
            return buffer, these[i - 2]
        if not self.prev:
            return buffer, None
        assert first[-2:] == full[-2:]
        old = full[-1] if (len(full) - 1) % 2 == buffer else full[-2]
        return buffer, (old[0], old[1] - PAIRS) + old[2:]


PJ_KINDS = ("turn", "v", "q", "k", "r", "cq", "gate", "up")
ROTATIONS = ("rot_q", "rot_k", "rot_cq")


def build(nc, x_in, x_mid, x_out, ctx_in, cond_in, tables, w128, w96, colp, rowp):
    with ExitStack() as top:
        def sb(name, shape, dt=F32, stack=top):
            return stack.enter_context(nc.sbuf_tensor(name, shape, dt))

        ident = sb("ident", [P, P])
        arena = sb("arena", [P, 20, N])
        probs = arena[:, 0:P_SLOTS, :]
        probsT = arena[:, P_SLOTS:P_SLOTS + 8, :]
        raw = arena[:, :, :].rearrange("p a n -> p (a n)")
        v_sb = sb("v_sb", [P, KT, MID])
        oT = sb("oT", [P, PAIRS, N])
        h_f = sb("h_f", [P, N])
        xn = h_f[:, :].rearrange("p (t d) -> p t d", t=QT)
        h_hi = sb("h_hi", [P, N], F32R)
        h_lo = sb("h_lo", [P, N], F32R)
        q_both = sb("q_both", [P, 2, 2, N], F32R)
        k_hi = sb("k_hi", [P, 2, 2, N], F32R)
        k_lo = sb("k_lo", [P, 2, 2, N], F32R)
        x_sb = sb("x_sb", [P, QT, D])
        x_new = sb("x_new", [P, QT, D])
        x_res = sb("x_res", [P, QT, D])
        h2_f = sb("h2_f", [P, N])
        xn2 = h2_f[:, :].rearrange("p (t d) -> p t d", t=QT)
        h2_hi = sb("h2_hi", [P, N], F32R)
        h2_lo = sb("h2_lo", [P, N], F32R)
        c_probs = sb("c_probs", [P, 2, N])
        c_probsT = sb("c_probsT", [P, 2, N])
        r_in = sb("r_in", [P, QT, 2, DH])
        r_sb = sb("r_sb", [P, N])
        condT = sb("condT", [P, B])
        stats = sb("stats", [P, QT, 6])
        mv = sb("mv", [P, QT, 2])
        rstd = sb("rstd", [P, QT])
        var_eps = sb("var_eps", [P, QT])
        half_var = sb("half_var", [P, QT])
        sq = sb("sq", [P, QT])
        negmax = sb("negmax", [P, NM])
        sums = sb("sums", [P, 2, TILES])
        recips = sb("recips", [P, TILES])
        c_negmax = sb("c_negmax", [P, QT, H])
        c_sum = sb("c_sum", [P, QT, H])
        c_recip = sb("c_recip", [P, QT, H])
        vec_own = sb("vec_own", [P, 2])
        vec_prev = sb("vec_prev", [P, 4])
        ones = sb("ones", [P, 1])

        def bank(name):
            return top.enter_context(nc.psum_tensor(name, [P, N], F32))

        s_bank = [bank(f"s_bank{i}") for i in range(S_BANKS)]
        acc_bank = bank("acc_bank")
        t_bank = [bank(f"t_bank{i}") for i in range(2)]
        pj_bank = [bank(f"pj_bank{i}") for i in range(2)]
        o_bank = bank("o_bank")

        ctx_sb = v_sb[:, 0, 0:CD]
        vw_rows = oT[:, 0:4, :].rearrange("p c (h d) -> p (c h) d", d=D)

        def sem(name):
            return top.enter_context(nc.semaphore(name))

        loads = [{n: sem(f"l{li}_{n}") for n in ("small_in", "ctx_in", "kv_in", "setup_in", "keep_in")}
                 for li in range(2)]
        for li in range(2):
            loads[li]["w_in"] = {n: sem(f"l{li}_w_in_{n}") for n, _ in SPLIT[li]}
        x_loaded = [sem(f"l{li}_x_loaded") for li in range(2)]

        for li in range(2):
            with ExitStack() as lay:
                rope = li == 0

                def lsb(name, shape, dt=F32):
                    return sb(f"l{li}_{name}", shape, dt, lay)

                w_hi = {n: lsb(f"{n}_hi", [P, c], F32R) for n, c in SPLIT[li]}
                w_lo = {n: lsb(f"{n}_lo", [P, c], F32R) for n, c in SPLIT[li]}
                wo = lsb("wo", [P, PAIRS, D])
                f2 = lsb("f2", [P, FC, D])
                cols = lsb("cols", [P, N_COLS[li]])
                bias_rows = lsb("bias_rows", [P, 3, D])
                vecs = lsb("vecs", [P, B, 6])
                vw = lsb("vw", [P, B, CG, D])
                env = dict(locals())
                env.pop("env", None)
                if rope:
                    env["rope_cs"] = lsb("rope_cs", [P, 2, N])
                    env["rot_a"] = lsb("rot_a", [P, 2, N])
                    env["rot_b"] = lsb("rot_b", [P, 2, N])
                    env["cqT"] = lsb("cqT", [P, 2, N])
                    env["kc"] = lsb("kc", [P, PAIRS, B * J])
                    env["k_diag"] = lsb("k_diag", [P, PAIRS, P])
                else:
                    env["cqT"] = lsb("cqT", [P, 4, N])
                    env["kw_hi"] = lsb("kw_hi", [P, B, H * J], F32R)
                    env["kw_lo"] = lsb("kw_lo", [P, B, H * J], F32R)
                src = (x_in, x_mid)[li]
                dst = (x_mid, x_out)[li]
                setup(nc, li, rope, env, src, ctx_in, cond_in, tables, w128[li], w96[li], colp[li], rowp[li])
                batch_loop(nc, li, rope, env, src, dst, ctx_in, w128, w96)


SWAP = [i ^ 1 for i in range(32)]


def root_start(dve, var, var_eps, half_var, y, step, n):
    dve.wait_ge(step, n)
    dve.tensor_scalar(var_eps, var, EPS, None, ALU.add).then_inc(step, 1)
    dve.wait_ge(step, n + 1)
    dve.tensor_scalar(y.bitcast(mybir.dt.int32), var_eps.bitcast(mybir.dt.int32), -0.5, float(0x5F3759DF),
                      ALU.mult, ALU.add)
    dve.tensor_scalar(half_var, var_eps, -0.5, None, ALU.mult).then_inc(step, 1)


def root_newton(dve, half_var, sq, y, step, n):
    dve.wait_ge(step, n)
    dve.tensor_tensor(sq, y, y, ALU.mult).then_inc(step, 1)
    dve.wait_ge(step, n + 1)
    dve.tensor_tensor(sq, sq, half_var, ALU.mult).then_inc(step, 1)
    dve.wait_ge(step, n + 2)
    dve.scalar_tensor_tensor(out=y, in0=sq, scalar=1.5, in1=y, op0=ALU.add, op1=ALU.mult).then_inc(step, 1)


def raw_columns(li, name):
    at, _ = spans(SPLIT[li] + SETUP[li] + CTXW)
    return slice(at[name][0], at[name][0] + at[name][1])


def kept_columns(li, name):
    at, _ = spans(SPLIT[li] + SETUP[li] + KEEP)
    return slice(at[name][0], at[name][0] + at[name][1])


def load_setup(eng, raw, w128, w96, li, loads):
    a, z = raw_columns(li, "ck").start, raw_columns(li, "cv").stop
    eng.dma_start(raw[0:CD, a:z], w96).then_inc(loads["kv_in"], 16)
    first = raw_columns(li, "ada").start
    eng.dma_start(raw[:, first:a], w128[:, first:a]).then_inc(loads["setup_in"], 16)


def load_split(eng, raw, w128, li, loads):
    for n, _ in SPLIT[li]:
        eng.dma_start(raw[:, raw_columns(li, n)], w128[:, raw_columns(li, n)]).then_inc(loads["w_in"][n], 16)


def setup(nc, li, rope, e, src, ctx_in, cond_in, tables, w128, w96, colp, rowp):
    raw, ident, v_sb, oT, condT = e["raw"], e["ident"], e["v_sb"], e["oT"], e["condT"]
    w_hi, w_lo, wo, f2, cols, bias_rows = e["w_hi"], e["w_lo"], e["wo"], e["f2"], e["cols"], e["bias_rows"]
    vecs, vw = e["vecs"], e["vw"]
    s_bank, t_bank, pj_bank, o_bank = e["s_bank"], e["t_bank"], e["pj_bank"], e["o_bank"]
    acc_bank = e["acc_bank"]
    loads = e["loads"][li]
    small_in, ctx_in_s, kv_in, setup_in, keep_in, w_in = (
        loads[n] for n in ("small_in", "ctx_in", "kv_in", "setup_in", "keep_in", "w_in"))

    def part(name):
        return raw[:, raw_columns(li, name)]

    ctx_sb = e["ctx_sb"]
    ctx_n = v_sb[:, 0, P:P + CD]
    ctxT = v_sb[:, 0, 2 * P:3 * P]
    lnc = v_sb[:, 0, 3 * P:3 * P + 2 * CD]
    vcT = v_sb[:, 1, :].rearrange("p (c n) -> p c n", c=PAIRS)
    wqT = v_sb[:, 2, :].rearrange("p (c n) -> p c n", c=PAIRS)
    kT = e["kc"] if rope else v_sb[:, 3, :].rearrange("p (c n) -> p c n", c=PAIRS)
    kT2 = v_sb[:, 2, :].rearrange("p (c n) -> p c n", c=PAIRS)
    vw_rows = e["vw_rows"]
    co = part("co").rearrange("p (c d) -> p c d", c=PAIRS)

    with ExitStack() as st:
        def sem(name):
            return st.enter_context(nc.semaphore(f"l{li}_{name}"))

        id_made = sem("id_made")
        hi_made, lo_made = sem("hi_made"), sem("lo_made")
        ctx_step, ctx_ready = sem("ctx_step"), sem("ctx_ready")
        ctxT_full, ctxT_made = sem("ctxT_full"), sem("ctxT_made")
        ada_full, ada_step = sem("ada_full"), sem("ada_step")
        kT_full, vT_full, wqT_full = sem("kT_full"), sem("vT_full"), sem("wqT_full")
        kT_step, vT_made, wqT_made = sem("kT_step"), sem("vT_made"), sem("wqT_made")
        vw_full, vw_made = sem("vw_full"), sem("vw_made")
        kw_full, kw_hi_made, kw_lo_made = sem("kw_full"), sem("kw_hi_made"), sem("kw_lo_made")

        block = st.enter_context(nc.Block())

        @block.sync
        def _(sp):
            if li == 0:
                sp.dma_start(ctx_sb, ctx_in).then_inc(ctx_in_s, 16)
            if rope:
                sp.dma_start(lnc, rowp[0:1, 3 * D:3 * D + 2 * CD].broadcast_to([P, 2 * CD])).then_inc(small_in, 16)
                sp.dma_start(e["rope_cs"][:, :, :], tables.rearrange("p (a n) -> p a n", a=2)).then_inc(small_in, 16)
            sp.dma_start(condT[:, :], cond_in).then_inc(small_in, 16)
            sp.dma_start(cols[:, :], colp).then_inc(small_in, 16)
            sp.dma_start(bias_rows[:, :, :].rearrange("p a d -> p (a d)"),
                         rowp[0:1, 0:3 * D].broadcast_to([P, 3 * D])).then_inc(small_in, 16)
            if li == 0:
                load_setup(sp, raw, w128, w96, li, loads)
            for weight, name in ((wo, "wo"), (f2, "f2")):
                sp.dma_start(weight[:, :, :].rearrange("p c d -> p (c d)"), w128[:, kept_columns(li, name)]
                             ).then_inc(keep_in, 16)
            sp.dma_start(e["x_sb"][:, :, :], src.rearrange("b (t p) d -> b p t d", p=P)[0]
                         ).then_inc(e["x_loaded"][li], 16)
            sp.wait_ge(keep_in, 32)
            sp.wait_ge(small_in, 16 * (5 if rope else 3))

        @block.gpsimd
        def _(pool):
            if li == 0:
                pool.memset(e["k_lo"][:, :, :, :].bitcast(F32), 0.0)
                pool.memset(e["k_diag"][:, :, :], 0.0)
                pool.memset(e["ones"][:, :], 1.0)
                pool.memset(ident[:, :], 0.0).then_inc(id_made, 1)
                pool.wait_ge(id_made, 1)
                pool.affine_select(out=ident[:, :], in_=ident[:, :], compare_op=ALU.not_equal, fill=1.0,
                                   base=0, pattern=[[-1, P]], channel_multiplier=1).then_inc(id_made, 1)

        @block.scalar
        def _(act):
            if li == 0:
                load_split(act, raw, w128, li, loads)
            act.wait_ge(ctxT_full, 1)
            act.copy(ctxT[0:CD, :], o_bank[0:CD, 0:P]).then_inc(ctxT_made, 1)
            act.wait_ge(vT_full, 1)
            for i in range(2):
                act.copy(vcT[:, 4 * i:4 * i + 4, :].rearrange("p c n -> p (c n)"), s_bank[i][:, :]).then_inc(vT_made, 1)
            if not rope:
                act.wait_ge(kT_full, 1)
                for i in range(2):
                    act.copy(kT[:, 4 * i:4 * i + 4, :].rearrange("p c n -> p (c n)"),
                             pj_bank[i][:, :]).then_inc(kT_step, 1)
                act.wait_ge(wqT_full, 1)
                for i in range(2):
                    act.mul(wqT[:, 4 * i:4 * i + 4, :].rearrange("p c n -> p (c n)"),
                            t_bank[i][:, :], SCALE).then_inc(wqT_made, 1)
            for n, _ in SPLIT[li]:
                act.wait_ge(w_in[n], 16)
                act.copy(w_hi[n][:, :], part(n)).then_inc(hi_made, 1)
            act.wait_ge(vw_full, 1)
            for i, bk in enumerate((pj_bank[0], pj_bank[1], t_bank[0], t_bank[1])):
                odd, half = i // 2, i % 2
                act.copy(vw_rows[:, 8 * half:8 * half + 8, :].rearrange("p (j o) d -> p j o d", o=2)[:, :, odd, :],
                         bk[:, :].rearrange("p (j d) -> p j d", d=D)).then_inc(vw_made, 1)
            if not rope:
                act.wait_ge(kw_full, 1)
                for i, bk in enumerate((s_bank[0], s_bank[1], acc_bank, o_bank)):
                    odd, half = i // 2, i % 2
                    for j in range(4):
                        h = 8 * half + 2 * j + odd
                        ins = act.copy(e["kw_hi"][:, :, h * J:(h + 1) * J],
                                       bk[:, j * P:(j + 1) * P].rearrange("p (b k) -> p b k", b=B))
                    ins.then_inc(kw_hi_made, 1)

        @block.vector
        def _(dve):
            if rope:
                dve.wait_ge(ctx_in_s, 16)
                dve.bn_stats(e["stats"][:, 0, :], ctx_sb).then_inc(ctx_step, 1)
                dve.wait_ge(ctx_step, 1)
                dve.bn_aggr(e["mv"][:, 0, :], e["stats"][:, 0, :]).then_inc(ctx_step, 1)
                half_var, sq, rstd = e["half_var"][:, 0:1], e["sq"][:, 0:1], e["rstd"][:, 0:1]
                root_start(dve, e["mv"][:, 0, 1:2], e["var_eps"][:, 0:1], half_var, rstd, ctx_step, 2)
                for k in range(3):
                    root_newton(dve, half_var, sq, rstd, ctx_step, 4 + 3 * k)
                dve.wait_ge(ctx_step, CHAIN + 1)
                dve.tensor_scalar(ctx_n, ctx_sb, e["mv"][:, 0, 0:1], e["rstd"][:, 0:1],
                                  ALU.subtract, ALU.mult).then_inc(ctx_step, 1)
                dve.wait_ge(ctx_step, CHAIN + 2)
                dve.wait_ge(small_in, 16 * 5)
                dve.tensor_tensor(ctx_n, ctx_n, lnc[:, 0:CD], ALU.mult).then_inc(ctx_step, 1)
                dve.wait_ge(ctx_step, CHAIN + 3)
                dve.tensor_tensor(ctx_n, ctx_n, lnc[:, CD:2 * CD], ALU.add).then_inc(ctx_ready, 1)
            dve.wait_ge(small_in, 16 * (5 if rope else 3))
            dve.wait_ge(ada_full, 1)
            A = acc_bank
            if rope:
                for m in range(2):
                    n = (0, 2)[m]
                    g, bt = A[:, 8 * m:8 * m + B], A[:, 8 * m + 4:8 * m + 4 + B]
                    lw, lb, gb, bb = (cols[:, 4 * m + i:4 * m + i + 1] for i in range(4))
                    sc, sh = vecs[:, :, 2 * n], vecs[:, :, 2 * n + 1]
                    dve.tensor_scalar(sc, g, gb, 1.0, ALU.add, ALU.add).then_inc(ada_step, 1)
                    dve.wait_ge(ada_step, 4 * m + 1)
                    dve.tensor_scalar(sh, sc, lb, bb, ALU.mult, ALU.add).then_inc(ada_step, 1)
                    dve.wait_ge(ada_step, 4 * m + 2)
                    dve.tensor_tensor(sh, sh, bt, ALU.add).then_inc(ada_step, 1)
                    dve.tensor_scalar(sc, sc, lw, None, ALU.mult).then_inc(ada_step, 1)
                    dve.wait_ge(ada_step, 4 * m + 4)
                dve.tensor_copy(vecs[:, :, 2:4], vecs[:, :, 0:2]).then_inc(ada_step, 1)
            else:
                for n in range(3):
                    dve.tensor_scalar(vecs[:, :, 2 * n], A[:, 8 * n:8 * n + B], cols[:, 2 * n:2 * n + 1], 1.0,
                                      ALU.add, ALU.add).then_inc(ada_step, 1)
                    dve.tensor_scalar(vecs[:, :, 2 * n + 1], A[:, 8 * n + 4:8 * n + 4 + B],
                                      cols[:, 2 * n + 1:2 * n + 2], None, ALU.add).then_inc(ada_step, 1)
            if rope:
                dve.wait_ge(kT_full, 1)
                cos, sin = (e["rope_cs"][:, i, 0:J].unsqueeze(1).broadcast_to([P, 4 * B, J]) for i in range(2))
                for i in range(2):
                    a = kT[:, 4 * i:4 * i + 4, :].rearrange("p c (b k) -> p (c b) k", k=J)
                    dve.tensor_tensor(a, pj_bank[i][:, :].rearrange("p (m k) -> p m k", k=J), cos,
                                      ALU.mult).then_inc(kT_step, 1)
                    dve.stream_shuffle(kT2[:, 4 * i:4 * i + 4, :].rearrange("p c n -> p (c n)"),
                                       pj_bank[i][:, :], SWAP).then_inc(kT_step, 1)
                for i in range(2):
                    b_ = kT2[:, 4 * i:4 * i + 4, :].rearrange("p c (b k) -> p (c b) k", k=J)
                    dve.wait_ge(kT_step, 4 + i)
                    dve.tensor_tensor(b_, b_, sin, ALU.mult).then_inc(kT_step, 1)
                dve.wait_ge(kT_step, 6)
                dve.tensor_tensor(kT[:, :, :], kT[:, :, :], kT2[:, :, :], ALU.add).then_inc(kT_step, 1)
                dve.wait_ge(kT_step, 7)
                dve.tensor_scalar(kT[:, :, :], kT[:, :, :], SCALE, None, ALU.mult).then_inc(kT_step, 1)
            for i, (n, _) in enumerate(SPLIT[li]):
                dve.wait_ge(hi_made, i + 1)
                dve.tensor_tensor(w_lo[n][:, :], part(n), w_hi[n][:, :].bitcast(F32), ALU.subtract).then_inc(lo_made, 1)
            if not rope:
                for i, bk in enumerate((s_bank[0], s_bank[1], acc_bank, o_bank)):
                    odd, half = i // 2, i % 2
                    dve.wait_ge(kw_hi_made, i + 1)
                    for j in range(4):
                        h = 8 * half + 2 * j + odd
                        ins = dve.tensor_tensor(e["kw_lo"][:, :, h * J:(h + 1) * J],
                                                bk[:, j * P:(j + 1) * P].rearrange("p (b k) -> p b k", b=B),
                                                e["kw_hi"][:, :, h * J:(h + 1) * J].bitcast(F32), ALU.subtract)
                    ins.then_inc(kw_lo_made, 1)

        @block.tensor
        def _(pe):
            if li == 0:
                pe.wait_ge(id_made, 2)
            if rope:
                pe.wait_ge(ctx_ready, 1)
            else:
                pe.wait_ge(ctx_in_s, 16)
            pe.transpose(o_bank[0:CD, 0:P], ctx_n if rope else ctx_sb, ident[:, :]).then_inc(ctxT_full, 1)
            pe.wait_ge(setup_in, 16)
            pe.wait_ge(small_in, 16 * (5 if rope else 3))
            ada = part("ada")
            for m in range(SETUP[li][0][1] // D):
                ins = pe.matmul(acc_bank[:, 4 * m:4 * m + B], ada[:, m * D:(m + 1) * D], condT[:, :],
                                start=True, stop=True)
            ins.then_inc(ada_full, 1)
            pe.wait_ge(ctxT_made, 1)
            pe.wait_ge(kv_in, 16)
            ck, cv = part("ck"), part("cv")
            for c in range(PAIRS):
                ins = pe.matmul(s_bank[c // 4][:, (c % 4) * P:(c % 4 + 1) * P], cv[0:CD, c * P:(c + 1) * P],
                                ctxT[0:CD, :], start=True, stop=True)
            ins.then_inc(vT_full, 1)
            for c in range(PAIRS):
                ins = pe.matmul(pj_bank[c // 4][:, (c % 4) * P:(c % 4 + 1) * P], ck[0:CD, c * P:(c + 1) * P],
                                ctxT[0:CD, :], start=True, stop=True)
            ins.then_inc(kT_full, 1)
            if not rope:
                cq = part("cq")
                for c in range(PAIRS):
                    ins = pe.transpose(t_bank[c // 4][:, (c % 4) * P:(c % 4 + 1) * P], cq[:, c * P:(c + 1) * P],
                                       ident[:, :])
                ins.then_inc(wqT_full, 1)
            pe.wait_ge(vT_made, 2)
            if rope:
                pe.wait_ge(kT_step, 4)
            else:
                pe.wait_ge(kT_step, 2)
                pe.wait_ge(wqT_made, 2)
            for odd in range(2):
                r = slice(DH * odd, DH * odd + DH)
                for c in range(PAIRS):
                    bk = (t_bank if odd else pj_bank)[c // 4]
                    ins = pe.matmul(bk[:, (c % 4) * P:(c % 4 + 1) * P], vcT[r, c, :], co[r, c, :],
                                    start=True, stop=True)
            ins.then_inc(vw_full, 1)
            if not rope:
                pe.wait_ge(ada_step, 6)
                for odd in range(2):
                    r = slice(DH * odd, DH * odd + DH)
                    for c in range(PAIRS):
                        bk = (s_bank[0], s_bank[1], acc_bank, o_bank)[2 * odd + c // 4]
                        ins = pe.matmul(bk[:, (c % 4) * P:(c % 4 + 1) * P], wqT[r, c, :], kT[r, c, :],
                                        start=True, stop=True)
                ins.then_inc(kw_full, 1)


def batch_loop(nc, li, rope, e, src, dst, ctx_in, w128, w96):
    ident, v_sb, oT, probs, probsT = e["ident"], e["v_sb"], e["oT"], e["probs"], e["probsT"]
    h_f, xn, h_hi, h_lo = e["h_f"], e["xn"], e["h_hi"], e["h_lo"]
    h2_f, xn2, h2_hi, h2_lo = e["h2_f"], e["xn2"], e["h2_hi"], e["h2_lo"]
    q_both, k_hi, k_lo = e["q_both"], e["k_hi"], e["k_lo"]
    x_sb, x_new, x_res, r_in, r_sb = e["x_sb"], e["x_new"], e["x_res"], e["r_in"], e["r_sb"]
    stats, mv, rstd, negmax = e["stats"], e["mv"], e["rstd"], e["negmax"]
    var_eps, half_var, sq = e["var_eps"], e["half_var"], e["sq"]
    sums, recips, c_negmax, c_sum, c_recip = e["sums"], e["recips"], e["c_negmax"], e["c_sum"], e["c_recip"]
    vec_own, vec_prev, vecs, vw = e["vec_own"], e["vec_prev"], e["vecs"], e["vw"]
    cols, bias_rows, cqT, c_probs, c_probsT = e["cols"], e["bias_rows"], e["cqT"], e["c_probs"], e["c_probsT"]
    w_hi, w_lo, wo, f2 = e["w_hi"], e["w_lo"], e["wo"], e["f2"]
    s_bank, t_bank, pj_bank = e["s_bank"], e["t_bank"], e["pj_bank"]
    o_bank, acc_bank = e["o_bank"], e["acc_bank"]
    plans = {v: make_plan(rope, v) for v in ("first", "full", "last")}

    with ExitStack() as st:
        def sem(name):
            return st.enter_context(nc.semaphore(f"l{li}_{name}"))

        S = {name: sem(name) for name in SIGNALS}
        x_loaded, x_new_free, vw_moved = e["x_loaded"][li], sem("x_new_free"), sem("vw_moved")

        def passes(eng, run):
            run(Pass(plans, "first", 0))
            with eng.Fori(1, B) as b:
                run(Pass(plans, "full", b))
            run(Pass(plans, "last", B))

        def pj(w, *step):
            return pj_bank[w.ring(PJ_KINDS, step)[0]]

        def t_of(w, *step):
            return t_bank[w.ring(("t", "ct"), step)[0]]

        def s_of(w, *step):
            return s_bank[w.ring(("s", "cs"), step)[0]]

        def tile(p, head, qt):
            return SLOT_GROUP[2 * (p % PAIRS) + head] * QT + qt

        def copied(step):
            engine = copier(rope, step)
            return ("pt_" + engine, f"{step[0]}_{engine}") + step[1:]

        def rotated(step):
            kind, c = step
            return cqT[:, c % 2, :] if kind == "rot_cq" else e["rot_a"][:, kind == "rot_k", :]

        def hidden(i):
            return (cqT, c_probs)[i // 2][:, i % 2, :] if rope else cqT[:, i, :]

        def reader(w, step):
            kind, i = step
            if kind in ("q", "k"):
                if rope:
                    return "rope_mul", "rot_" + kind, i
                return ("qk_lo", "lo_q", i, 1) if kind == "q" else ("qk_lo", "lo_k", i, 1)
            return {"turn": ("h_full", "turn", i), "v": ("v_dve" if i % 2 else "v_act", "v", i),
                    "r": ("r_made", "r", i), "cq": ("rope_mul", "rot_cq", i),
                    "gate": ("gelu_made", "gate", i), "up": ("hid_made", "up", i)}[kind]

        block = st.enter_context(nc.Block())

        @block.sync
        def _(sp):
            rows_of = "b (t p) d -> b p t d"
            flat = "b p t d -> (b p) t d"
            sp.sem_inc(x_new_free, 16)

            def run(w):
                for step in w.plan:
                    if step[0] == "twice_k":
                        c, head = step[1:]
                        rows, others = (slice(DH * h, DH * h + DH) for h in (head, 1 - head))
                        sp.wait_ge(S["qk_hi"], w.at("qk_hi", "hi_k", c, head))
                        sp.dma_start(k_hi[others, c % 2, head, :].bitcast(F32), k_hi[rows, c % 2, head, :].bitcast(F32)
                                     ).then_inc(S[f"k_twice{c % 2 * 2 + head}"], 16)
                        if w.variant == "first" and (c, head) == (0, 1):
                            regroup()
                    elif step == ("bias", 0) and w.more:
                        sp.wait_ge(S["bias0_made"], w.at("bias0_made", "bias", 0))
                        sp.dma_start(x_sb[:, :, :], src.rearrange(rows_of, p=P)[bass.ds(w.b + 1, 1)].rearrange(flat)
                                     ).then_inc(x_loaded, 16)
                    elif step == ("res", 2):
                        sp.wait_ge(S["added"], w.at("added", "res", 2))
                        sp.dma_start(dst.rearrange(rows_of, p=P)[bass.ds(w.b - 1, 1)].rearrange(flat),
                                     x_new[:, :, :]).then_inc(x_new_free, 16)
                    elif step == ("av", -1, KT - 1) and w.variant == "last" and li == 0:
                        sp.wait_ge(S["av_done"], w.at("av_done", "av", -1, KT - 1))
                        sp.dma_start(e["ctx_sb"], ctx_in).then_inc(e["loads"][1]["ctx_in"], 16)
                        load_setup(sp, e["raw"], w128[1], w96[1], 1, e["loads"][1])
                        load_split(sp, e["raw"], w128[1], 1, e["loads"][1])

            def regroup():
                for b in range(B):
                    for r in range(P // J):
                        sp.dma_start(vw[r * J:(r + 1) * J, b, :, :],
                                     e["vw_rows"][b * J:(b + 1) * J, :, :].rearrange(
                                         "p (g r) d -> p g r d", r=P // J)[:, :, r, :]).then_inc(vw_moved, 16)

            run(Pass(plans, "first", 0))
            with sp.Fori(1, B - 1) as b:
                run(Pass(plans, "full", b))
            run(Pass(plans, "full", B - 1))
            run(Pass(plans, "last", B))
            sp.wait_ge(x_new_free, 16 * (B + 1))

        @block.gpsimd
        def _(pool):
            def bias(w, n):
                pool.wait_ge(S["xn_made"], w.at("xn_made", "normalise", n))
                if n == 0 and w.prev:
                    pool.wait_ge(S["added"], w.at("added", "res", 0))
                x, out, made = (x_sb, x_res, "bias0_made") if n == 0 else (x_new, x_new, "biased")
                pool.tensor_tensor(out[:, :, :], x[:, :, :], bias_rows[:, n, :].unsqueeze(1).broadcast_to([P, QT, D]),
                                   ALU.add).then_inc(S[made], 1)

            def rope_sum(w, step):
                pool.wait_ge(S["rope_mul"], w.at("rope_mul", *step))
                out, swapped = rotated(step), e["rot_b"][:, w.ring(ROTATIONS, step)[0], :]
                pool.tensor_tensor(swapped, swapped, e["rope_cs"][:, 1, :], ALU.mult).then_inc(S["sin_mul"], 1)
                pool.wait_ge(S["sin_mul"], w.at("sin_mul", *step))
                pool.tensor_tensor(out, out, swapped, ALU.add).then_inc(S["rope_add"], 1)

            def spread(w, p):
                if w.has("r", p - 1):
                    pool.wait_ge(S["pj_full"], w.at("pj_full", "r", p - 1))
                pool.wait_ge(S["recip_made"], w.at("recip_made", "recip", p))
                shape4 = [P, 2, QT, DH]
                pool.tensor_tensor(r_in[:, :, :, :].rearrange("p t h d -> p h t d"),
                                   recips[:, :].rearrange("p (h t) -> p h t", h=2).unsqueeze(3).broadcast_to(shape4),
                                   e["ones"][:, 0:1].unsqueeze(2).unsqueeze(3).broadcast_to(shape4),
                                   ALU.mult).then_inc(S["r_in_made"], 1)

            def cross_norm(w, u):
                pool.wait_ge(S["c_inv"], w.at("c_inv", "csum", u))
                p4 = c_probs[:, u % 2, :].rearrange("p (h k) -> p h k", k=J)
                pool.tensor_tensor(p4, p4, c_recip[:, u, :].unsqueeze(2).broadcast_to([P, H, J]),
                                   ALU.mult).then_inc(S["c_norm"], 1)

            def run(w):
                for step in w.plan:
                    kind = step[0]
                    if kind == "bias":
                        bias(w, step[1])
                    elif kind.startswith("rot") and rope:
                        rope_sum(w, step)
                    elif kind == "recip":
                        spread(w, step[1])
                    elif kind == "csum":
                        cross_norm(w, step[1])

            passes(pool, run)

        @block.tensor
        def _(pe):
            def claim(w, *step):
                old = w.ring(PJ_KINDS, step)[1]
                if old:
                    name, *read = reader(w, old)
                    pe.wait_ge(S[name], w.at(name, *read))

            def three(out, a_hi, a_lo, b_hi, b_lo):
                pe.matmul(out, a_hi, b_hi, start=True, stop=False)
                pe.matmul(out, a_lo, b_hi, start=False, stop=False)
                return pe.matmul(out, a_hi, b_lo, start=False, stop=True)

            def turn_norm(w, n):
                pe.wait_ge(S["xn_made"], w.at("xn_made", "normalise", n))
                claim(w, "turn", n)
                x = xn if n == 0 else xn2
                for t in range(QT):
                    ins = pe.transpose(pj(w, "turn", n)[:, t * P:(t + 1) * P], x[:, t, :], ident[:, :])
                ins.then_inc(S["pj_full"], 1)

            def project(w, step, weight, chunk):
                norm = {"q": 0, "k": 0, "cq": 1, "f": 2}[weight]
                pe.wait_ge(S["h_lo_made"], w.at("h_lo_made", "turn", norm))
                claim(w, *step)
                cs = slice(chunk * P, chunk * P + P)
                hh, hl = (h_hi, h_lo) if norm == 0 else (h2_hi, h2_lo)
                three(pj(w, *step)[:, :], w_hi[weight][:, cs], w_lo[weight][:, cs], hh[:, :], hl[:, :]
                      ).then_inc(S["pj_full"], 1)

            def values(w, j):
                half, kt = j // KT, j % KT
                pe.wait_ge(S["h_lo_made"], w.at("h_lo_made", "turn", 0))
                claim(w, "v", j)
                ts, cs = slice(kt * P, kt * P + P), slice(half * N, half * N + N)
                three(pj(w, "v", j)[:, :], h_hi[:, ts], h_lo[:, ts], w_hi["v"][:, cs], w_lo["v"][:, cs]
                      ).then_inc(S["pj_full"], 1)

            def recip_rows(w, p):
                pe.wait_ge(S["r_in_made"], w.at("r_in_made", "recip", p))
                claim(w, "r", p)
                for t in range(QT):
                    ins = pe.transpose(pj(w, "r", p)[:, t * P:(t + 1) * P],
                                       r_in[:, t, :, :].rearrange("p h d -> p (h d)"), ident[:, :])
                ins.then_inc(S["pj_full"], 1)

            def claim_s(w, *step):
                old = w.ring(("s", "cs"), step)[1]
                if old:
                    if old[0] == "s":
                        pe.wait_ge(S["exp_made"], w.at("exp_made", "exp", *old[1:]))
                    else:
                        pe.wait_ge(S["c_sub"], w.at("c_sub", "cmax", old[1]))

            def scores(w, c, s):
                head, qt = s // QT, s % QT
                if qt == 0:
                    pe.wait_ge(S["qk_lo"], w.at("qk_lo", "lo_k", c, head))
                    twice = f"k_twice{c % 2 * 2 + head}"
                    pe.wait_ge(S[twice], w.at(twice, "twice_k", c, head))
                claim_s(w, "s", c, s)
                ts = slice(qt * P, qt * P + P)
                out, q = s_of(w, "s", c, s)[:, :], q_both[:, c % 2, head, ts]
                pe.matmul(out, q, k_hi[:, c % 2, head, :], start=True, stop=False)
                pe.matmul(out, q, k_lo[:, c % 2, head, :], start=False, stop=True).then_inc(S["s_full"], 1)

            def claim_t(w, *step):
                old = w.ring(("t", "ct"), step)[1]
                if old:
                    name, *copy = copied(old)
                    pe.wait_ge(S[name], w.at(name, *copy))

            def turn_probs(w, p, i):
                head, kt = i // KT, i % KT
                if kt == 0:
                    pe.wait_ge(S["exp_made"], w.at("exp_made", "exp", p, head * QT + QT - 1))
                claim_t(w, "t", p, i)
                for t in range(QT):
                    ins = pe.transpose(t_of(w, "t", p, i)[:, t * P:(t + 1) * P],
                                       probs[:, tile(p, head, t), kt * P:(kt + 1) * P], ident[:, :])
                ins.then_inc(S["t_full"], 1)

            def weigh(w, p, k):
                if k == 0:
                    if p in (0, PAIRS // 2):
                        last = KT * (1 + 2 * p // PAIRS) - 1
                        pe.wait_ge(S["v_act"], w.at("v_act", "v", last - 1))
                        pe.wait_ge(S["v_dve"], w.at("v_dve", "v", last))
                    if w.has("o", p - 1):
                        pe.wait_ge(S["o_made"], w.at("o_made", "o", p - 1))
                blocks = {copied(("t", p, i))[0]: copied(("t", p, i))[1:] for i in (k, KT + k)}
                for name, copy in blocks.items():
                    pe.wait_ge(S[name], w.at(name, *copy))
                for head in range(2):
                    h = 2 * (p % PAIRS) + head
                    ins = pe.matmul(o_bank[DH * head:DH * head + DH, :], v_sb[:, k, h * DH:(h + 1) * DH],
                                    probsT[:, KT * head + k, :], start=(k == 0), stop=(k == KT - 1))
                ins.then_inc(S["av_done"], 1)

            def out_rows(w, t):
                if t == 0:
                    pe.wait_ge(S["o_made"], w.at("o_made", "o", -1))
                for g in range(PAIRS):
                    ins = pe.matmul(acc_bank[:, t * P:(t + 1) * P], oT[:, g, t * P:(t + 1) * P], wo[:, g, :],
                                    start=(g == 0), stop=(g == PAIRS - 1))
                if t == QT - 1:
                    ins.then_inc(S["acc_full"], 1)

            def cross_scores(w, u):
                claim_s(w, "cs", u)
                if rope:
                    pe.wait_ge(S["rope_add"], w.at("rope_add", "rot_cq", 2 * u + 1))
                    pe.wait_ge(S["diag_made"], w.at("diag_made", "load", 0))
                    for t in range(QT):
                        for j in range(2):
                            ins = pe.matmul(s_of(w, "cs", u)[:, t * P:(t + 1) * P], cqT[:, j, t * P:(t + 1) * P],
                                            e["k_diag"][:, 2 * u + j, :], start=(j == 0), stop=(j == 1))
                    ins.then_inc(S["s_full"], 1)
                else:
                    pe.wait_ge(S["h_lo_made"], w.at("h_lo_made", "turn", 1))
                    kwh, kwl = (e[n][:, bass.ds(w.b - 1, 1), :].rearrange("p b n -> p (b n)")
                                for n in ("kw_hi", "kw_lo"))
                    ts = slice(u * P, u * P + P)
                    three(s_of(w, "cs", u)[:, :], h2_hi[:, ts], h2_lo[:, ts], kwh, kwl).then_inc(S["s_full"], 1)

            def turn_cross(w, u):
                pe.wait_ge(S["c_norm"], w.at("c_norm", "csum", u))
                claim_t(w, "ct", u)
                for j in range(4):
                    ins = pe.transpose(t_of(w, "ct", u)[:, j * P:(j + 1) * P],
                                       c_probs[:, u % 2, j * P:(j + 1) * P], ident[:, :])
                ins.then_inc(S["t_full"], 1)

            def cross_out(w, u):
                if u == 0:
                    pe.wait_ge(S["added"], w.at("added", "res", 0))
                name, *copy = copied(("ct", u))
                pe.wait_ge(S[name], w.at(name, *copy))
                for j in range(4):
                    t, g = (j, u) if rope else (u, j)
                    first, last = (u == 0 and j == 0, u == QT - 1) if rope else (j == 0, j == 3)
                    ins = pe.matmul(acc_bank[:, t * P:(t + 1) * P], c_probsT[:, u % 2, j * P:(j + 1) * P],
                                    vw[:, bass.ds(w.b - 1, 1), g, :].rearrange("p b d -> p (b d)"),
                                    start=first, stop=last, skip_group_check=rope)
                if u == QT - 1:
                    ins.then_inc(S["acc_full"], 1)
                else:
                    ins.then_inc(S["c_done"], 1)

            def ff_out(w, i):
                if i == 0:
                    pe.wait_ge(S["added"], w.at("added", "res", 1))
                pe.wait_ge(S["gelu_made" if rope else "hid_made"],
                           w.at("gelu_made", "gate", i) if rope else w.at("hid_made", "up", i))
                for t in range(QT):
                    ins = pe.matmul(acc_bank[:, t * P:(t + 1) * P], hidden(i)[:, t * P:(t + 1) * P], f2[:, i, :],
                                    start=(i == 0 and t == 0), stop=(i == FC - 1), skip_group_check=True)
                if i == FC - 1:
                    ins.then_inc(S["acc_full"], 1)

            def run(w):
                for step in w.plan:
                    kind, i = step[0], step[1]
                    if kind == "turn":
                        turn_norm(w, i)
                    elif kind == "v":
                        values(w, i)
                    elif kind in ("q", "k", "cq"):
                        project(w, step, kind, i)
                    elif kind == "s":
                        scores(w, i, step[2])
                    elif kind == "t":
                        turn_probs(w, i, step[2])
                    elif kind == "av":
                        weigh(w, i, step[2])
                    elif kind == "r":
                        recip_rows(w, i)
                    elif kind == "out":
                        out_rows(w, i)
                    elif kind == "cs":
                        cross_scores(w, i)
                    elif kind == "ct":
                        turn_cross(w, i)
                    elif kind == "cout":
                        cross_out(w, i)
                    elif kind == "gate":
                        project(w, step, "f", i if rope else FC + i)
                    elif kind == "up":
                        project(w, step, "f", i)
                    elif kind == "fout":
                        ff_out(w, i)

            passes(pe, run)

        def blocks_out(eng, w, step):
            made = (step[0].split("_")[0],) + step[1:]
            eng.wait_ge(S["t_full"], w.at("t_full", *made))
            bank = t_of(w, *made)[:, :]
            if made[0] == "ct":
                u = step[1]
                if u >= 2:
                    eng.wait_ge(S["c_done"], w.at("c_done", "cout", u - 2))
                return c_probsT[:, u % 2, :], bank
            p, i = step[1], step[2]
            if w.has("av", p - 1, i % KT):
                eng.wait_ge(S["av_done"], w.at("av_done", "av", p - 1, i % KT))
            return probsT[:, i, :], bank

        def value_slot(eng, w, j):
            eng.wait_ge(S["pj_full"], w.at("pj_full", "v", j))
            if w.prev:
                last_pair = (j // KT + 1) * PAIRS // 2 - 1 - PAIRS
                eng.wait_ge(S["av_done"], w.at("av_done", "av", last_pair, KT - 1))
            return v_sb[:, j % KT, j // KT * N:(j // KT + 1) * N]

        @block.scalar
        def _(act):
            def norm_hi(w, n):
                f, hi = (h_f, h_hi) if n == 0 else (h2_f, h2_hi)
                act.wait_ge(S["h_full"], w.at("h_full", "turn", n))
                act.copy(hi[:, :], f[:, :]).then_inc(S["h_hi_made"], 1)

            def high(w, step):
                kind, c = step[:2]
                x = kind[-1]
                if w.has("s", c - 2, TILES - 1):
                    act.wait_ge(S["s_full"], w.at("s_full", "s", c - 2, TILES - 1))
                if rope:
                    act.wait_ge(S["rope_add"], w.at("rope_add", f"rot_{x}", c))
                    full = rotated((f"rot_{x}", c))
                else:
                    act.wait_ge(S["pj_full"], w.at("pj_full", x, c))
                    full = pj(w, x, c)[:, :]
                head = step[2]
                rows = slice(DH * head, DH * head + DH)
                if x == "q":
                    act.mul(q_both[rows, c % 2, head, :], full[rows, :], SCALE).then_inc(S["qk_hi"], 1)
                else:
                    act.copy(k_hi[rows, c % 2, head, :], full[rows, :]).then_inc(S["qk_hi"], 1)

            def exps(w, c, s):
                n, head, qt = c * TILES + s, s // QT, s % QT
                if qt == 0:
                    old = next(g for g in range(2 * c + head - 1, -PAIRS * 4, -1)
                               if SLOT_GROUP[g % H] == SLOT_GROUP[(2 * c + head) % H])
                    if w.has("t", old // 2, old % 2 * KT + KT - 1):
                        act.wait_ge(S["t_full"], w.at("t_full", "t", old // 2, old % 2 * KT + KT - 1))
                if s == 0 and w.has("recip", c - 2):
                    act.wait_ge(S["recip_made"], w.at("recip_made", "recip", c - 2))
                act.wait_ge(S["max_made"], w.at("max_made", "max", c, s))
                act.activation(probs[:, tile(c, head, qt), :], s_of(w, "s", c, s)[:, :], ACT.Exp,
                               bias=negmax[:, n % NM:n % NM + 1],
                               accum_out=sums[:, c % 2, s:s + 1]).then_inc(S["exp_made"], 1)

            def gelu(w, i):
                act.wait_ge(S["pj_full"], w.at("pj_full", "gate", i))
                out = hidden(i) if rope else (c_probs, c_probsT)[i // 2][:, i % 2, :]
                col = 8 + i if rope else 6 + FC + i
                act.activation(out, pj(w, "gate", i)[:, :], ACT.Gelu, bias=cols[:, col:col + 1]
                               ).then_inc(S["gelu_made"], 1)

            def run(w):
                for step in w.plan:
                    kind, i = step[0], step[1]
                    if kind == "turn":
                        norm_hi(w, i)
                    elif kind == "v" and i % 2 == 0:
                        act.copy(value_slot(act, w, i), pj(w, "v", i)[:, :]).then_inc(S["v_act"], 1)
                    elif kind in ("hi_q", "hi_k"):
                        high(w, step)
                    elif kind == "exp":
                        exps(w, i, step[2])
                    elif kind in ("t_act", "ct_act"):
                        act.copy(*blocks_out(act, w, step)).then_inc(S["pt_act"], 1)
                    elif kind == "r":
                        act.wait_ge(S["pj_full"], w.at("pj_full", "r", i))
                        if w.has("o", i - 1):
                            act.wait_ge(S["o_made"], w.at("o_made", "o", i - 1))
                        act.copy(r_sb[:, :], pj(w, "r", i)[:, :]).then_inc(S["r_made"], 1)
                    elif kind == "cexp":
                        act.wait_ge(S["c_sub"], w.at("c_sub", "cmax", i))
                        act.activation(c_probs[:, i % 2, :], c_probs[:, i % 2, :], ACT.Exp).then_inc(S["c_exp"], 1)
                    elif kind == "gate":
                        gelu(w, i)

            passes(act, run)

        @block.vector
        def _(dve):
            def norm(w, n):
                x = x_sb if n == 0 else x_new
                if n == 0:
                    dve.wait_ge(x_loaded, w.b * 16 + 16)
                else:
                    dve.wait_ge(S["added"], w.at("added", "res", n - 1))
                for t in range(QT):
                    dve.bn_stats(stats[:, t, :], x[:, t, :])
                dve.drain()
                for t in range(QT):
                    ins = dve.bn_aggr(mv[:, t, :], stats[:, t, :])
                ins.then_inc(S["chain"], 1)

            def root(w, m):
                n, part = m // 4, m % 4
                if part == 0:
                    root_start(dve, mv[:, :, 1], var_eps[:, :], half_var[:, :], rstd[:, :], S["chain"],
                               w.at("chain", "norm", n))
                else:
                    root_newton(dve, half_var[:, :], sq[:, :], rstd[:, :], S["chain"], w.at("chain", "root", m - 1))

            def normalise(w, n):
                x, out = (x_sb, xn) if n == 0 else (x_new, xn2)
                dve.wait_ge(S["chain"], w.at("chain", "root", 4 * n + 3))
                for t in range(QT):
                    ins = dve.tensor_scalar(out[:, t, :], x[:, t, :], mv[:, t, 0:1], rstd[:, t:t + 1],
                                            ALU.subtract, ALU.mult)
                ins.then_inc(S["xn_made"], 1)

            def scale_shift(w, n):
                f, hi, lo = (h_f, h_hi, h_lo) if n == 0 else (h2_f, h2_hi, h2_lo)
                vec = vec_own[:, 0:2] if n == 0 else vec_prev[:, 2 * n - 2:2 * n]
                dve.wait_ge(S["pj_full"], w.at("pj_full", "turn", n))
                dve.tensor_scalar(f[:, :], pj(w, "turn", n)[:, :], vec[:, 0:1], vec[:, 1:2],
                                  ALU.mult, ALU.add).then_inc(S["h_full"], 1)
                dve.wait_ge(S["h_hi_made"], w.at("h_hi_made", "turn", n))
                dve.tensor_tensor(lo[:, :], f[:, :], hi[:, :].bitcast(F32), ALU.subtract).then_inc(S["h_lo_made"], 1)

            def rotate(w, step):
                kind, c = step
                j, old = w.ring(ROTATIONS, step)
                name = kind[4:]
                a, b2, bank = rotated(step), e["rot_b"][:, j, :], pj(w, name, c)
                dve.wait_ge(S["pj_full"], w.at("pj_full", name, c))
                if old:
                    dve.wait_ge(S["rope_add"], w.at("rope_add", *old))
                if kind != "rot_cq" and w.has("lo_" + name, c - 1, 1):
                    dve.wait_ge(S["qk_lo"], w.at("qk_lo", "lo_" + name, c - 1, 1))
                if kind == "rot_cq" and c >= 2:
                    dve.wait_ge(S["s_full"], w.at("s_full", "cs", c // 2 - 1))
                dve.tensor_tensor(a, bank[:, :], e["rope_cs"][:, 0, :], ALU.mult)
                dve.stream_shuffle(b2, bank[:, :], SWAP).then_inc(S["rope_mul"], 1)

            def low(w, step):
                kind, c = step[:2]
                x = kind[-1]
                dve.wait_ge(S["qk_hi"], w.at("qk_hi", "hi_" + x, *step[1:]))
                full = rotated((f"rot_{x}", c)) if rope else pj(w, x, c)[:, :]
                head = step[2]
                rows, others = (slice(DH * h, DH * h + DH) for h in (head, 1 - head))
                if x == "q":
                    dve.scalar_tensor_tensor(out=q_both[others, c % 2, head, :], in0=full[rows, :], scalar=SCALE,
                                             in1=q_both[rows, c % 2, head, :].bitcast(F32),
                                             op0=ALU.mult, op1=ALU.subtract).then_inc(S["qk_lo"], 1)
                else:
                    dve.tensor_tensor(k_lo[rows, c % 2, head, :], full[rows, :],
                                      k_hi[rows, c % 2, head, :].bitcast(F32), ALU.subtract
                                      ).then_inc(S["qk_lo"], 1)

            def invert(w, p):
                dve.wait_ge(S["exp_made"], w.at("exp_made", "exp", p, TILES - 1))
                if w.has("recip", p - 1):
                    dve.wait_ge(S["r_in_made"], w.at("r_in_made", "recip", p - 1))
                dve.reciprocal(recips[:, :], sums[:, p % 2, :]).then_inc(S["recip_made"], 1)

            def divide(w, p):
                dve.wait_ge(S["av_done"], w.at("av_done", "av", p, KT - 1))
                dve.wait_ge(S["r_made"], w.at("r_made", "r", p))
                if w.variant == "first" and p == 0:
                    dve.wait_ge(vw_moved, 16 * B * (P // J))
                dve.tensor_tensor(oT[:, p % PAIRS, :], o_bank[:, :], r_sb[:, :], ALU.mult).then_inc(S["o_made"], 1)

            def cross_max(w, u):
                dve.wait_ge(S["s_full"], w.at("s_full", "cs", u))
                if u >= 2:
                    dve.wait_ge(S["t_full"], w.at("t_full", "ct", u - 2))
                sv = s_of(w, "cs", u)[:, :].rearrange("p (h k) -> p h k", k=J)
                dve.tensor_reduce(c_negmax[:, u, :], sv, AX_X, ALU.max, negate=True).then_inc(S["c_max"], 1)
                dve.wait_ge(S["c_max"], w.at("c_max", "cmax", u))
                dve.tensor_tensor(c_probs[:, u % 2, :].rearrange("p (h k) -> p h k", k=J), sv,
                                  c_negmax[:, u, :].unsqueeze(2).broadcast_to([P, H, J]), ALU.add
                                  ).then_inc(S["c_sub"], 1)

            def cross_sum(w, u):
                dve.wait_ge(S["c_exp"], w.at("c_exp", "cexp", u))
                dve.tensor_reduce(c_sum[:, u, :], c_probs[:, u % 2, :].rearrange("p (h k) -> p h k", k=J), AX_X,
                                  ALU.add).then_inc(S["c_summed"], 1)
                dve.wait_ge(S["c_summed"], w.at("c_summed", "csum", u))
                dve.reciprocal(c_recip[:, u, :], c_sum[:, u, :]).then_inc(S["c_inv"], 1)

            def add_residual(w, n):
                dve.wait_ge(S["acc_full"], w.before("acc_full") + n + 1)
                if n == 0:
                    dve.wait_ge(S["bias0_made"], w.before("bias0_made"))
                    dve.wait_ge(x_new_free, w.b * 16)
                else:
                    dve.wait_ge(S["biased"], w.at("biased", "bias", n))
                x = x_res if n == 0 else x_new
                dve.tensor_tensor(x_new[:, :, :], acc_bank[:, :].rearrange("p (t d) -> p t d", d=D), x[:, :, :],
                                  ALU.add).then_inc(S["added"], 1)

            def run(w):
                if w.own:
                    dve.tensor_copy(vec_own[:, :], vecs[:, bass.ds(w.b, 1), 0:2].rearrange("p b n -> p (b n)"))
                if w.prev:
                    dve.tensor_copy(vec_prev[:, :], vecs[:, bass.ds(w.b - 1, 1), 2:6].rearrange("p b n -> p (b n)"))
                for step in w.plan:
                    kind, i = step[0], step[1]
                    if kind == "norm":
                        norm(w, i)
                    elif kind == "root":
                        root(w, i)
                    elif kind == "normalise":
                        normalise(w, i)
                    elif kind == "turn":
                        scale_shift(w, i)
                    elif kind == "v" and i % 2 == 1:
                        dve.tensor_copy(value_slot(dve, w, i), pj(w, "v", i)[:, :]).then_inc(S["v_dve"], 1)
                    elif kind.startswith("rot") and rope:
                        rotate(w, step)
                    elif kind in ("lo_q", "lo_k"):
                        low(w, step)
                    elif kind == "max":
                        n = i * TILES + step[2]
                        dve.wait_ge(S["s_full"], w.at("s_full", "s", *step[1:]))
                        dve.tensor_reduce(negmax[:, n % NM:n % NM + 1], s_of(w, "s", *step[1:])[:, :], AX_X, ALU.max,
                                          negate=True).then_inc(S["max_made"], 1)
                    elif kind in ("t_dve", "ct_dve"):
                        dve.tensor_copy(*blocks_out(dve, w, step)).then_inc(S["pt_dve"], 1)
                    elif kind == "recip":
                        invert(w, i)
                    elif kind == "o":
                        divide(w, i)
                    elif kind == "load" and rope:
                        kd = e["k_diag"][:, :, :].rearrange("p (g o) n -> p g o n", o=2)
                        kc = e["kc"][:, :, bass.ds((w.b - 1) * J, J)].rearrange("p (g o) n -> p g o n", o=2)
                        for half in range(2):
                            r = slice(DH * half, DH * half + DH)
                            for o in range(2):
                                at = 2 * J * o + J * half
                                dve.tensor_copy(kd[r, :, o, at:at + J], kc[r, :, o, :]).then_inc(S["diag_made"], 1)
                    elif kind == "cmax":
                        cross_max(w, i)
                    elif kind == "csum":
                        cross_sum(w, i)
                    elif kind == "up":
                        dve.wait_ge(S["pj_full"], w.at("pj_full", "up", i))
                        dve.wait_ge(S["gelu_made"], w.at("gelu_made", "gate", i))
                        dve.scalar_tensor_tensor(out=hidden(i), in0=pj(w, "up", i)[:, :],
                                                 scalar=cols[:, 6 + i:7 + i],
                                                 in1=(c_probs, c_probsT)[i // 2][:, i % 2, :],
                                                 op0=ALU.add, op1=ALU.mult).then_inc(S["hid_made"], 1)
                    elif kind == "res":
                        add_residual(w, i)

            passes(dve, run)


def rope_tables():
    inv = (1.0 / np.float32(10000.0) ** (np.arange(0, DH, 2, dtype=np.float32) / np.float32(DH))).astype(np.float32)
    ang = np.arange(N, dtype=np.float32)[None, :] * inv[:, None]
    cos, sin = (np.repeat(f(ang).astype(np.float32), 2, axis=0) for f in (np.cos, np.sin))
    sin[0::2] *= -1
    return np.ascontiguousarray(np.concatenate([np.tile(cos, (2, 1)), np.tile(sin, (2, 1))], axis=1))


def kernel(**inputs):
    import numpy as _np
    import concourse.bacc as _bacc
    from concourse.bass_utils import run_bass_kernel_spmd as _run

    w = {k: _np.asarray(v) for k, v in inputs.items()}

    def l0(n):
        return w[f"L0_xcond_{n}"]

    def l1(n):
        return w[f"L1_xcond_{n}"]

    def stack(m):
        return m.reshape(-1, P, m.shape[1]).transpose(1, 0, 2).reshape(P, -1)

    def columns(*vs):
        return _np.concatenate([v.reshape(-1, P).T for v in vs], axis=1)

    arrays = {
        "x": w["x"],
        "ctx": w["ctx_768"].reshape(B * J, CD),
        "cond": w["cond_1024"].T,
        "tables": rope_tables(),
        "w128_0": _np.concatenate([
            l0("sa_wq"), l0("sa_wkv"), l0("ca_wq"), l0("ff_w1"),
            l0("g1_w"), l0("b1_w"), l0("g2_w"), l0("b2_w"), stack(l0("ca_wo")),
            stack(l0("sa_wo")), stack(l0("ff_w2"))], axis=1),
        "w128_1": _np.concatenate([
            l1("q1"), l1("k1"), l1("v1"), l1("ff_w1"),
            l1("n1_w"), l1("n2_w"), l1("n3_w"), stack(l1("o2_w")), l1("q2"),
            stack(l1("o1_w")), stack(l1("ff_w2"))], axis=1),
        "w96_0": l0("ca_wkv"),
        "w96_1": _np.concatenate([l1("k2"), l1("v2")], axis=1),
        "cols_0": columns(l0("ln1_w"), l0("ln1_b"), l0("g1_b"), l0("b1_b"),
                          l0("ln2_w"), l0("ln2_b"), l0("g2_b"), l0("b2_b"), l0("ff_b1")),
        "cols_1": columns(l1("n1_b"), l1("n2_b"), l1("n3_b"), l1("ff_b1")),
        "rows_0": _np.concatenate([l0("sa_bo"), l0("ca_bo"), l0("ff_b2"), l0("ca_lnc_w"), l0("ca_lnc_b")])[None],
        "rows_1": _np.concatenate([l1("o1_b"), l1("o2_b"), l1("ff_b2")])[None],
    }
    arrays = {k: _np.ascontiguousarray(v) for k, v in arrays.items()}
    nc = _bacc.Bacc("TRN2", target_bir_lowering=False, num_devices=1)
    ap = {k: nc.dram_tensor(k, v.shape, F32, kind="ExternalInput").ap() for k, v in arrays.items()}
    mid = nc.dram_tensor("x_mid", (B, N, D), F32, kind="Internal").ap()
    out = nc.dram_tensor("out", (B, N, D), F32, kind="ExternalOutput").ap()
    build(nc, ap["x"], mid, out, ap["ctx"], ap["cond"], ap["tables"], (ap["w128_0"], ap["w128_1"]),
          (ap["w96_0"], ap["w96_1"]), (ap["cols_0"], ap["cols_1"]), (ap["rows_0"], ap["rows_1"]))
    r = _run(nc, [arrays], core_ids=[0])
    return r.results[0]["out"]
```
